# Optimizing a Trainium2 kernel written in Bass

```python
import numpy as np
import jax
import jax.numpy as jnp

def _softmax(x, axis=-1):
    return jax.nn.softmax(x, axis=axis)

def _gelu(x):
    return jax.nn.gelu(x, approximate=True)

def _silu(x):
    return jax.nn.silu(x)

def _sigmoid(x):
    return jax.nn.sigmoid(x)

def _layernorm(x, axis=-1, eps=1e-05):
    m = jnp.mean(x, axis=axis, keepdims=True)
    v = jnp.var(x, axis=axis, keepdims=True)
    return (x - m) / jnp.sqrt(v + eps)

def _scatter_add(tgt, idx, src, axis=0):
    return tgt.at[idx].add(src)

def _segment_sum(src, seg, n):
    return jax.ops.segment_sum(src, seg, n)
kernel_name = 'mk_flamingo_gated_d2_seqx_r8_b38d5e'

def setup_inputs(seed: int=0):
    np.random.seed(seed)
    _w = jnp.asarray

    def _rec_inputs():
        import jax
        import jax.numpy as jnp
        _rk = jax.random.key(seed)
        x = 7.22e-05 + 1 * jax.random.normal(jax.random.fold_in(_rk, 1), (1, 1024, 128), jnp.float32)
        _lenS = 1024 - jax.random.randint(jax.random.fold_in(_rk, 7), (1,), 0, max(1, 1024 // 4) + 1, jnp.int32)
        _lenS2 = 6404 - jax.random.randint(jax.random.fold_in(_rk, 8), (1,), 0, max(1, 6404 // 4) + 1, jnp.int32)
        _ctx_1024P = jax.random.normal(jax.random.fold_in(_rk, 11), (1, 16, 128), jnp.float32)
        _ctx_1024c = jax.random.dirichlet(jax.random.fold_in(_rk, 511), 0.3 * jnp.ones((16,), jnp.float32), (1, 6404))
        _ctx_1024t = jnp.einsum('bsk,bkd->bsd', _ctx_1024c, _ctx_1024P)
        _ctx_1024t = _ctx_1024t * jax.lax.rsqrt(jnp.mean(jnp.square(_ctx_1024t)) + 1e-12) * 0.953939
        ctx_1024 = 4.13588e-05 + 0.999923 * (_ctx_1024t + 0.3 * jax.random.normal(jax.random.fold_in(_rk, 611), (1, 6404, 128), jnp.float32))
        _validS = jnp.arange(1024)[None, :] < _lenS[:, None]
        _validS2 = jnp.arange(6404)[None, :] < _lenS2[:, None]
        _causal = jnp.tril(jnp.ones((1024, 1024), dtype=bool))
        mask_BxS2_ik0 = jnp.where(jnp.broadcast_to(_validS2[:, :], (1, 6404)), 0, 1).astype(jnp.int32)
        _g = jax.random.normal(jax.random.fold_in(_rk, 9001), (2, 2), jnp.float32)
        _g = jnp.sign(_g) * jnp.maximum(jnp.abs(_g), 1.0) + (_g == 0) * 1.0
        g_xattn = _g[0]
        g_ffn = _g[1]
        return (x, ctx_1024, mask_BxS2_ik0, g_xattn, g_ffn)
    x, ctx_1024, mask_BxS2_ik0, g_xattn, g_ffn = _rec_inputs()

    def _L0_xattn_setup():
        import jax, jax.numpy as jnp
        import numpy as np
        DIM = 128
        B, SQ, SK = (4, 256, 256)
        key = jax.random.key(seed)
        ks = jax.random.split(key, 8)
        s = 1.0 / np.sqrt(DIM)
        return {'x1': jax.random.normal(ks[0], (B, SQ, DIM), dtype=jnp.float32), 'x2': jax.random.normal(ks[1], (B, SK, DIM), dtype=jnp.float32), 'Wq': jax.random.uniform(ks[2], (DIM, DIM), jnp.float32, -s, s), 'bq': jax.random.uniform(ks[3], (DIM,), jnp.float32, -s, s), 'Wk': jax.random.uniform(ks[4], (DIM, DIM), jnp.float32, -s, s), 'bk': jax.random.uniform(ks[5], (DIM,), jnp.float32, -s, s), 'Wv': jax.random.uniform(ks[6], (DIM, DIM), jnp.float32, -s, s), 'bv': jax.random.uniform(ks[7], (DIM,), jnp.float32, -s, s)}
    _L0_xattn_all = _L0_xattn_setup()
    _L0_xattn_in = {k: v for k, v in _L0_xattn_all.items() if k in ('Wq', 'bq', 'Wk', 'bk', 'Wv', 'bv')}
    del _L0_xattn_all

    def _L0_ffn_setup():
        import jax, jax.numpy as jnp
        import numpy as np
        from jax import lax
        T, B, I, M, O = (32, 64, 128, 128, 128)

        def _xavier(key, shape):
            fan_out, fan_in = shape
            limit = float(np.sqrt(6.0 / (fan_in + fan_out)))
            return jax.random.uniform(key, shape, jnp.float32, -limit, limit)
        key = jax.random.key(seed)
        ks = jax.random.split(key, 9)
        x = jax.random.normal(ks[0], (T, B, I), jnp.float32)
        return {'x': x, 'wf': _xavier(ks[1], (M, I)), 'uf': _xavier(ks[2], (M, M)), 'bf': jnp.zeros((M,), jnp.float32), 'wi': _xavier(ks[3], (M, I)), 'ui': _xavier(ks[4], (M, M)), 'bi': jnp.zeros((M,), jnp.float32), 'wc': _xavier(ks[5], (M, I)), 'uc': _xavier(ks[6], (M, M)), 'bc': jnp.zeros((M,), jnp.float32), 'wo': _xavier(ks[7], (O, I)), 'uo': _xavier(ks[8], (O, M)), 'bo': jnp.zeros((O,), jnp.float32), 'in_c': jnp.zeros((M,), jnp.float32)}
    _L0_ffn_all = _L0_ffn_setup()
    _L0_ffn_in = {k: v for k, v in _L0_ffn_all.items() if k in ('wf', 'uf', 'bf', 'wi', 'ui', 'bi', 'wc', 'uc', 'bc', 'wo', 'uo', 'bo', 'in_c')}
    del _L0_ffn_all

    def _L1_xattn_setup():
        import jax, jax.numpy as jnp
        import numpy as np
        D = 128

        def _layernorm(x, g, b, eps=1e-05):
            m = jnp.mean(x, axis=-1, keepdims=True)
            v = jnp.var(x, axis=-1, keepdims=True)
            return (x - m) / jnp.sqrt(v + eps) * g + b
        key = jax.random.key(seed)
        ks = jax.random.split(key, 12)
        B, Lt, La = (32, 128, 256)
        s = 1.0 / np.sqrt(D)
        return {'text': jax.random.normal(ks[0], (B, Lt, D), jnp.float32), 'audio': jax.random.normal(ks[1], (B, La, D), jnp.float32), 'audio_masks': jax.random.randint(ks[2], (B, La), 0, 2, jnp.int32), 'ln_t_g': jnp.ones((D,), jnp.float32), 'ln_t_b': jnp.zeros((D,), jnp.float32), 'ln_a_g': jnp.ones((D,), jnp.float32), 'ln_a_b': jnp.zeros((D,), jnp.float32), 'Wq': jax.random.normal(ks[3], (D, D), jnp.float32) * s, 'bq': jnp.zeros((D,), jnp.float32), 'Wk': jax.random.normal(ks[4], (D, D), jnp.float32) * s, 'bk': jnp.zeros((D,), jnp.float32), 'Wv': jax.random.normal(ks[5], (D, D), jnp.float32) * s, 'bv': jnp.zeros((D,), jnp.float32), 'ln_p_g': jnp.ones((D,), jnp.float32), 'ln_p_b': jnp.zeros((D,), jnp.float32)}
    _L1_xattn_all = _L1_xattn_setup()
    _L1_xattn_in = {k: v for k, v in _L1_xattn_all.items() if k in ('ln_t_g', 'ln_t_b', 'ln_a_g', 'ln_a_b', 'Wq', 'bq', 'Wk', 'bk', 'Wv', 'bv', 'ln_p_g', 'ln_p_b')}
    del _L1_xattn_all

    def _L1_ffn_setup():
        import jax, jax.numpy as jnp
        import numpy as np
        HIDDEN = 128
        N_EXPERTS = 32
        MOE_I = 64
        N_GROUP = 4
        TOPK_GROUP = 2
        TOP_K = 6
        N_LOCAL_GROUPS = 16
        ANCHOR_I = 32
        SHARED_I = 64
        ROUTED_SCALE = 0.2
        ANCHOR_ALPHA = 0.1
        BATCH, SEQ = (1, 128)

        def _moe_forward(hidden_states, gate_weight, gate_bias, w_gate, w_up, w_down, shared_w_gate, shared_w_up, shared_w_down, anchor_w_gate, anchor_w_up, anchor_w_down):
            B, S, H = hidden_states.shape
            x = hidden_states.reshape(-1, H)
            T = x.shape[0]
            E = gate_weight.shape[0]
            L = anchor_w_gate.shape[0]
            logits = x @ gate_weight.T
            scores = jax.nn.sigmoid(logits)
            sc = scores + gate_bias
            grp = sc.reshape(T, N_GROUP, E // N_GROUP)
            group_scores = jax.lax.top_k(grp, 2)[0].sum(-1)
            _, gidx = jax.lax.top_k(group_scores, TOPK_GROUP)
            gmask = jax.nn.one_hot(gidx, N_GROUP, dtype=sc.dtype).sum(1)
            emask = jnp.repeat(gmask, E // N_GROUP, axis=1)
            masked = jnp.where(emask > 0, sc, -jnp.inf)
            _, topidx = jax.lax.top_k(masked, TOP_K)
            tw = jnp.take_along_axis(scores, topidx, axis=-1)
            tw = tw / (tw.sum(-1, keepdims=True) + 1e-20) * ROUTED_SCALE
            g = jnp.einsum('th,ehi->tei', x, w_gate)
            u = jnp.einsum('th,ehi->tei', x, w_up)
            eo = jnp.einsum('tei,eih->teh', jax.nn.silu(g) * u, w_down)
            cw = (jax.nn.one_hot(topidx, E, dtype=x.dtype) * tw[..., None]).sum(1)
            routed = jnp.einsum('te,teh->th', cw, eo)
            shared = jax.nn.silu(x @ shared_w_gate) * (x @ shared_w_up) @ shared_w_down
            lg = topidx[:, 0] // (E // L)
            ag = jnp.einsum('th,lhi->tli', x, anchor_w_gate)
            au = jnp.einsum('th,lhi->tli', x, anchor_w_up)
            ao = jnp.einsum('tli,lih->tlh', jax.nn.silu(ag) * au, anchor_w_down)
            acw = jax.nn.one_hot(lg, L, dtype=x.dtype)
            anchor = jnp.einsum('tl,tlh->th', acw, ao)
            out = routed + shared + ANCHOR_ALPHA * anchor
            return out.reshape(B, S, H)
        key = jax.random.key(seed)
        ks = jax.random.split(key, 13)
        s = 0.02
        return {'hidden_states': jax.random.normal(ks[0], (BATCH, SEQ, HIDDEN), jnp.float32), 'gate_weight': s * jax.random.normal(ks[1], (N_EXPERTS, HIDDEN), jnp.float32), 'gate_bias': s * jax.random.normal(ks[2], (N_EXPERTS,), jnp.float32), 'w_gate': s * jax.random.normal(ks[3], (N_EXPERTS, HIDDEN, MOE_I), jnp.float32), 'w_up': s * jax.random.normal(ks[4], (N_EXPERTS, HIDDEN, MOE_I), jnp.float32), 'w_down': s * jax.random.normal(ks[5], (N_EXPERTS, MOE_I, HIDDEN), jnp.float32), 'shared_w_gate': s * jax.random.normal(ks[6], (HIDDEN, SHARED_I), jnp.float32), 'shared_w_up': s * jax.random.normal(ks[7], (HIDDEN, SHARED_I), jnp.float32), 'shared_w_down': s * jax.random.normal(ks[8], (SHARED_I, HIDDEN), jnp.float32), 'anchor_w_gate': s * jax.random.normal(ks[9], (N_LOCAL_GROUPS, HIDDEN, ANCHOR_I), jnp.float32), 'anchor_w_up': s * jax.random.normal(ks[10], (N_LOCAL_GROUPS, HIDDEN, ANCHOR_I), jnp.float32), 'anchor_w_down': s * jax.random.normal(ks[11], (N_LOCAL_GROUPS, ANCHOR_I, HIDDEN), jnp.float32)}
    _L1_ffn_all = _L1_ffn_setup()
    _L1_ffn_in = {k: v for k, v in _L1_ffn_all.items() if k in ('gate_weight', 'gate_bias', 'w_gate', 'w_up', 'w_down', 'shared_w_gate', 'shared_w_up', 'shared_w_down', 'anchor_w_gate', 'anchor_w_up', 'anchor_w_down')}
    del _L1_ffn_all
    return {'x': x, 'ctx_1024': ctx_1024, 'mask_BxS2_ik0': mask_BxS2_ik0, 'g_xattn': g_xattn, 'g_ffn': g_ffn, 'L0_xattn_Wq': _L0_xattn_in['Wq'], 'L0_xattn_bq': _L0_xattn_in['bq'], 'L0_xattn_Wk': _L0_xattn_in['Wk'], 'L0_xattn_bk': _L0_xattn_in['bk'], 'L0_xattn_Wv': _L0_xattn_in['Wv'], 'L0_xattn_bv': _L0_xattn_in['bv'], 'L0_ffn_wf': _L0_ffn_in['wf'], 'L0_ffn_uf': _L0_ffn_in['uf'], 'L0_ffn_bf': _L0_ffn_in['bf'], 'L0_ffn_wi': _L0_ffn_in['wi'], 'L0_ffn_ui': _L0_ffn_in['ui'], 'L0_ffn_bi': _L0_ffn_in['bi'], 'L0_ffn_wc': _L0_ffn_in['wc'], 'L0_ffn_uc': _L0_ffn_in['uc'], 'L0_ffn_bc': _L0_ffn_in['bc'], 'L0_ffn_wo': _L0_ffn_in['wo'], 'L0_ffn_uo': _L0_ffn_in['uo'], 'L0_ffn_bo': _L0_ffn_in['bo'], 'L0_ffn_in_c': _L0_ffn_in['in_c'], 'L1_xattn_ln_t_g': _L1_xattn_in['ln_t_g'], 'L1_xattn_ln_t_b': _L1_xattn_in['ln_t_b'], 'L1_xattn_ln_a_g': _L1_xattn_in['ln_a_g'], 'L1_xattn_ln_a_b': _L1_xattn_in['ln_a_b'], 'L1_xattn_Wq': _L1_xattn_in['Wq'], 'L1_xattn_bq': _L1_xattn_in['bq'], 'L1_xattn_Wk': _L1_xattn_in['Wk'], 'L1_xattn_bk': _L1_xattn_in['bk'], 'L1_xattn_Wv': _L1_xattn_in['Wv'], 'L1_xattn_bv': _L1_xattn_in['bv'], 'L1_xattn_ln_p_g': _L1_xattn_in['ln_p_g'], 'L1_xattn_ln_p_b': _L1_xattn_in['ln_p_b'], 'L1_ffn_gate_weight': _L1_ffn_in['gate_weight'], 'L1_ffn_gate_bias': _L1_ffn_in['gate_bias'], 'L1_ffn_w_gate': _L1_ffn_in['w_gate'], 'L1_ffn_w_up': _L1_ffn_in['w_up'], 'L1_ffn_w_down': _L1_ffn_in['w_down'], 'L1_ffn_shared_w_gate': _L1_ffn_in['shared_w_gate'], 'L1_ffn_shared_w_up': _L1_ffn_in['shared_w_up'], 'L1_ffn_shared_w_down': _L1_ffn_in['shared_w_down'], 'L1_ffn_anchor_w_gate': _L1_ffn_in['anchor_w_gate'], 'L1_ffn_anchor_w_up': _L1_ffn_in['anchor_w_up'], 'L1_ffn_anchor_w_down': _L1_ffn_in['anchor_w_down']}

def reference(x, ctx_1024, mask_BxS2_ik0, g_xattn, g_ffn, L0_xattn_Wq, L0_xattn_bq, L0_xattn_Wk, L0_xattn_bk, L0_xattn_Wv, L0_xattn_bv, L0_ffn_wf, L0_ffn_uf, L0_ffn_bf, L0_ffn_wi, L0_ffn_ui, L0_ffn_bi, L0_ffn_wc, L0_ffn_uc, L0_ffn_bc, L0_ffn_wo, L0_ffn_uo, L0_ffn_bo, L0_ffn_in_c, L1_xattn_ln_t_g, L1_xattn_ln_t_b, L1_xattn_ln_a_g, L1_xattn_ln_a_b, L1_xattn_Wq, L1_xattn_bq, L1_xattn_Wk, L1_xattn_bk, L1_xattn_Wv, L1_xattn_bv, L1_xattn_ln_p_g, L1_xattn_ln_p_b, L1_ffn_gate_weight, L1_ffn_gate_bias, L1_ffn_w_gate, L1_ffn_w_up, L1_ffn_w_down, L1_ffn_shared_w_gate, L1_ffn_shared_w_up, L1_ffn_shared_w_down, L1_ffn_anchor_w_gate, L1_ffn_anchor_w_up, L1_ffn_anchor_w_down):
    import jax
    import jax.numpy as jnp

    def _L0_xattn_ref(x1, x2, Wq, bq, Wk, bk, Wv, bv):
        import jax, jax.numpy as jnp
        import numpy as np
        DIM = 128
        B, SQ, SK = (4, 256, 256)
        q = jnp.einsum('bsd,ed->bse', x1, Wq) + bq
        k = jnp.einsum('bsd,ed->bse', x2, Wk) + bk
        v = jnp.einsum('bsd,ed->bse', x2, Wv) + bv
        scale = 1.0 / jnp.sqrt(jnp.asarray(Wq.shape[0], q.dtype))
        scores = jnp.einsum('bqd,bkd->bqk', q, k) * scale
        attn = jax.nn.softmax(scores, axis=-1)
        return jnp.einsum('bqk,bkd->bqd', attn, v)

    def _L0_ffn_ref(x, wf, uf, bf, wi, ui, bi, wc, uc, bc, wo, uo, bo, in_c):
        import jax, jax.numpy as jnp
        import numpy as np
        from jax import lax
        T, B, I, M, O = (32, 64, 128, 128, 128)

        def _xavier(key, shape):
            fan_out, fan_in = shape
            limit = float(np.sqrt(6.0 / (fan_in + fan_out)))
            return jax.random.uniform(key, shape, jnp.float32, -limit, limit)
        batch = x.shape[1]
        c0 = jnp.broadcast_to(in_c, (batch, in_c.shape[0]))

        def step(c, xt):
            ft = jax.nn.sigmoid(xt @ wf.T + c @ uf.T + bf)
            it = jax.nn.sigmoid(xt @ wi.T + c @ ui.T + bi)
            gt = jnp.tanh(xt @ wc.T + c @ uc.T + bc)
            c = ft * c + it * gt
            return (c, None)
        c_final, _ = lax.scan(step, c0, x)
        h = jnp.tanh(jnp.einsum('tbi,oi->tbo', x, wo) + c_final @ uo.T + bo)
        return h

    def _L1_xattn_ref(text, audio, audio_masks, ln_t_g, ln_t_b, ln_a_g, ln_a_b, Wq, bq, Wk, bk, Wv, bv, ln_p_g, ln_p_b):
        import jax, jax.numpy as jnp
        import numpy as np
        D = 128

        def _layernorm(x, g, b, eps=1e-05):
            m = jnp.mean(x, axis=-1, keepdims=True)
            v = jnp.var(x, axis=-1, keepdims=True)
            return (x - m) / jnp.sqrt(v + eps) * g + b
        t = _layernorm(text, ln_t_g, ln_t_b)
        a = _layernorm(audio, ln_a_g, ln_a_b)
        q = t @ Wq + bq
        k = a @ Wk + bk
        v = a @ Wv + bv
        scale = 1.0 / jnp.sqrt(jnp.asarray(audio.shape[-1], t.dtype))
        scores = jnp.einsum('btd,bsd->bts', q, k) * scale
        scores = jnp.where(audio_masks[:, None, :] == 0, jnp.asarray(-1000000000.0, scores.dtype), scores)
        w = jax.nn.softmax(scores, axis=-1)
        cross = jnp.einsum('bts,bsd->btd', w, v)
        return _layernorm(cross, ln_p_g, ln_p_b)

    def _L1_ffn_ref(hidden_states, gate_weight, gate_bias, w_gate, w_up, w_down, shared_w_gate, shared_w_up, shared_w_down, anchor_w_gate, anchor_w_up, anchor_w_down):
        import jax, jax.numpy as jnp
        import numpy as np
        HIDDEN = 128
        N_EXPERTS = 32
        MOE_I = 64
        N_GROUP = 4
        TOPK_GROUP = 2
        TOP_K = 6
        N_LOCAL_GROUPS = 16
        ANCHOR_I = 32
        SHARED_I = 64
        ROUTED_SCALE = 0.2
        ANCHOR_ALPHA = 0.1
        BATCH, SEQ = (1, 128)

        def _moe_forward(hidden_states, gate_weight, gate_bias, w_gate, w_up, w_down, shared_w_gate, shared_w_up, shared_w_down, anchor_w_gate, anchor_w_up, anchor_w_down):
            B, S, H = hidden_states.shape
            x = hidden_states.reshape(-1, H)
            T = x.shape[0]
            E = gate_weight.shape[0]
            L = anchor_w_gate.shape[0]
            logits = x @ gate_weight.T
            scores = jax.nn.sigmoid(logits)
            sc = scores + gate_bias
            grp = sc.reshape(T, N_GROUP, E // N_GROUP)
            group_scores = jax.lax.top_k(grp, 2)[0].sum(-1)
            _, gidx = jax.lax.top_k(group_scores, TOPK_GROUP)
            gmask = jax.nn.one_hot(gidx, N_GROUP, dtype=sc.dtype).sum(1)
            emask = jnp.repeat(gmask, E // N_GROUP, axis=1)
            masked = jnp.where(emask > 0, sc, -jnp.inf)
            _, topidx = jax.lax.top_k(masked, TOP_K)
            tw = jnp.take_along_axis(scores, topidx, axis=-1)
            tw = tw / (tw.sum(-1, keepdims=True) + 1e-20) * ROUTED_SCALE
            g = jnp.einsum('th,ehi->tei', x, w_gate)
            u = jnp.einsum('th,ehi->tei', x, w_up)
            eo = jnp.einsum('tei,eih->teh', jax.nn.silu(g) * u, w_down)
            cw = (jax.nn.one_hot(topidx, E, dtype=x.dtype) * tw[..., None]).sum(1)
            routed = jnp.einsum('te,teh->th', cw, eo)
            shared = jax.nn.silu(x @ shared_w_gate) * (x @ shared_w_up) @ shared_w_down
            lg = topidx[:, 0] // (E // L)
            ag = jnp.einsum('th,lhi->tli', x, anchor_w_gate)
            au = jnp.einsum('th,lhi->tli', x, anchor_w_up)
            ao = jnp.einsum('tli,lih->tlh', jax.nn.silu(ag) * au, anchor_w_down)
            acw = jax.nn.one_hot(lg, L, dtype=x.dtype)
            anchor = jnp.einsum('tl,tlh->th', acw, ao)
            out = routed + shared + ANCHOR_ALPHA * anchor
            return out.reshape(B, S, H)
        return _moe_forward(hidden_states, gate_weight, gate_bias, w_gate, w_up, w_down, shared_w_gate, shared_w_up, shared_w_down, anchor_w_gate, anchor_w_up, anchor_w_down)
    x = x + jnp.tanh(g_xattn[0]) * _L0_xattn_ref(_layernorm(x, axis=-1), ctx_1024, L0_xattn_Wq, L0_xattn_bq, L0_xattn_Wk, L0_xattn_bk, L0_xattn_Wv, L0_xattn_bv)
    x = x + jnp.tanh(g_ffn[0]) * _L0_ffn_ref(_layernorm(x, axis=-1), L0_ffn_wf, L0_ffn_uf, L0_ffn_bf, L0_ffn_wi, L0_ffn_ui, L0_ffn_bi, L0_ffn_wc, L0_ffn_uc, L0_ffn_bc, L0_ffn_wo, L0_ffn_uo, L0_ffn_bo, L0_ffn_in_c)
    x = x + jnp.tanh(g_xattn[1]) * _L1_xattn_ref(_layernorm(x, axis=-1), ctx_1024, mask_BxS2_ik0, L1_xattn_ln_t_g, L1_xattn_ln_t_b, L1_xattn_ln_a_g, L1_xattn_ln_a_b, L1_xattn_Wq, L1_xattn_bq, L1_xattn_Wk, L1_xattn_bk, L1_xattn_Wv, L1_xattn_bv, L1_xattn_ln_p_g, L1_xattn_ln_p_b)
    x = x + jnp.tanh(g_ffn[1]) * _L1_ffn_ref(_layernorm(x, axis=-1), L1_ffn_gate_weight, L1_ffn_gate_bias, L1_ffn_w_gate, L1_ffn_w_up, L1_ffn_w_down, L1_ffn_shared_w_gate, L1_ffn_shared_w_up, L1_ffn_shared_w_down, L1_ffn_anchor_w_gate, L1_ffn_anchor_w_up, L1_ffn_anchor_w_down)
    return x

_drawn_inputs = setup_inputs


def setup_inputs(seed=0):
    import zlib

    import numpy as np

    out = dict(_drawn_inputs(seed))
    spreads = {'g_ffn': (-1.0, 0.6),
     'L0_ffn_bf': (0.0, 2.0),
     'L0_ffn_bi': (0.0, 0.8),
     'L0_ffn_bc': (0.0, 0.692),
     'L0_ffn_bo': (0.0, 0.1),
     'L0_ffn_in_c': (0.0, 0.376),
     'L1_xattn_ln_t_g': (1.0, 0.2),
     'L1_xattn_ln_t_b': (0.0, 0.348),
     'L1_xattn_ln_a_g': (1.0, 0.2),
     'L1_xattn_ln_a_b': (0.0, 0.1),
     'L1_xattn_bq': (0.0, 0.3),
     'L1_xattn_bk': (0.0, 2.0),
     'L1_xattn_bv': (0.0, 0.1),
     'L1_xattn_ln_p_g': (1.0, 0.2),
     'L1_xattn_ln_p_b': (0.0, 0.1)}
    factors = {'L0_xattn_bq': 21.464,
     'L0_xattn_bk': 64.0,
     'L0_ffn_wf': 8.0,
     'L0_ffn_uf': 8.0,
     'L0_ffn_ui': 8.0,
     'L0_ffn_uc': 4.638,
     'L1_ffn_gate_weight': 8.0,
     'L1_ffn_gate_bias': 8.0,
     'L1_ffn_w_gate': 8.0,
     'L1_ffn_w_up': 8.0,
     'L1_ffn_w_down': 8.0,
     'L1_ffn_shared_w_gate': 8.0,
     'L1_ffn_shared_w_up': 8.0,
     'L1_ffn_shared_w_down': 8.0,
     'L1_ffn_anchor_w_gate': 8.0,
     'L1_ffn_anchor_w_up': 8.0,
     'L1_ffn_anchor_w_down': 8.0}
    for name, (base, spread) in spreads.items():
        noise = np.random.default_rng([zlib.crc32(name.encode()), seed]).standard_normal(out[name].shape)
        drawn = base * np.exp(spread * noise) if base else spread * noise
        out[name] = jnp.asarray(drawn.astype(out[name].dtype))
    for name, factor in factors.items():
        out[name] = (out[name] * factor).astype(out[name].dtype)
    return out
```

```python
import concourse.bass as bass
from concourse import mybir
from concourse.alu_op_type import AluOpType as ALU
from contextlib import ExitStack

F32 = mybir.dt.float32
F16 = mybir.dt.float16
BF16 = mybir.dt.bfloat16
I32 = mybir.dt.int32
ACT = mybir.ActivationFunctionType
AX = mybir.AxisListType

D = 128
NQ = 1024
HALVES = 2
QT = 4
QH = QT * D
NK = 6404
FULL = NK // D
REST = NK - FULL * D
NT = FULL + 1
GRP = 4
NG = 12
TAIL0 = NG * GRP
TAILW = NK - TAIL0 * D
NE, ME = 32, 64
NA, MA = 16, 32
MOE_T = 21
ROUTED_T, ANCHOR_T = 16, 4
TOPK = 6
ROUTED_SCALE = 0.2
ANCHOR_ALPHA = 0.1

SPLIT = 256.0
PROD = SPLIT * SPLIT
ATT_SCALE = float(D) ** -0.5
P_LOG = 12 * 0.6931471805599453 / ATT_SCALE
PEN = 65280.0
CW_SCALE = 1024.0
HID_SCALE = 32.0
LN_EPS = 1e-5
C_F, C_ONE, C_L = 0, D, D + 1
VW = 2 * D + 1


def build(nc, a):
    ctx = ExitStack()
    with ctx:
        def sb(name, shape, dt=F32):
            return ctx.enter_context(nc.sbuf_tensor(name, shape, dt))

        def ps(name, shape, dt=F32):
            return ctx.enter_context(nc.psum_tensor(name, shape, dt))

        made = {}

        def sem(name):
            if name not in made:
                made[name] = ctx.enter_context(nc.semaphore(name))
            return made[name]

        ctx_nat = sb("ctx_nat", [128, NT, D])
        c_val = sb("c_val", [128, NT, VW], F16)
        h_val = sb("h_val", [128, NT, VW], F16)
        c_key = sb("c_key", [128, 2, NT, D], F16)
        h_key = sb("h_key", [128, 2, NT, D], F16)
        h_max = sb("h_max", [128, NT, D], F16)
        p_hi = sb("p_hi", [128, GRP, QH], F16)
        p_lo = sb("p_lo", [128, GRP, QH], F16)
        p_f = sb("p_f", [128, GRP, QH])
        ident = sb("ident", [128, 128])
        ident16 = sb("ident16", [128, 128], F16)
        cent = sb("cent", [128, 128])
        ones = sb("ones", [128, 128])
        augw = sb("augw", [128, 128], BF16)
        WNAMES = ["L0_xattn_Wq", "L0_xattn_Wv", "L0_ffn_wf", "L0_ffn_wi", "L0_ffn_wc", "L0_ffn_wo",
                  "L0_ffn_uo", "L1_xattn_Wk"]
        wT = sb("wT", [128, len(WNAMES), 128])
        W = {n: wT[:, i, :] for i, n in enumerate(WNAMES)}
        wk0 = sb("wk0", [128, 128])
        wq1 = sb("wq1", [128, 128])
        wv1 = sb("wv1", [128, 128])
        gw = sb("gw", [NE, 128])
        gwT = sb("gwT", [128, NE])
        us = sb("us", [128, 3, 128])
        COLS = ["L0_xattn_bq", "L0_xattn_bk", "L0_ffn_bf", "L0_ffn_bi", "L0_ffn_bc", "L0_ffn_in_c",
                "L1_xattn_ln_t_g", "L1_xattn_ln_t_b", "L1_xattn_ln_a_g", "L1_xattn_ln_a_b",
                "L1_xattn_bq", "L1_xattn_bk"]
        cols = sb("cols", [128, len(COLS)])
        C = {n: cols[:, i:i + 1] for i, n in enumerate(COLS)}
        ROWS = ["L0_xattn_bv", "L0_ffn_bo", "L0_ffn_in_c", "L1_xattn_bv", "L1_xattn_ln_p_g",
                "L1_xattn_ln_p_b"]
        rows = sb("rows", [128, len(ROWS), 128])
        R = {n: rows[:, i, :] for i, n in enumerate(ROWS)}
        gates = sb("gates", [128, 4])
        tg = sb("tg", [128, 4])
        gbias = sb("gbias", [128, NE])
        lt4 = sb("lt4", [128, 16])
        seg = sb("seg", [128, 128])
        sel = h_max[:, 0:MOE_T, :]
        xres = sb("xres", [128, HALVES, QT, D])
        pre1 = sb("pre1", [128, 2, QT, D])
        nrm = pre1[:, 1]
        avg = pre1[:, 0]
        scr = sb("scr", [128, QT, D])
        opT = sb("opT", [128, QH])
        gt = sb("gt", [128, 3, QH])
        wraw = gt[:, 0:2, :].rearrange("p a b -> p (a b)").rearrange("p (n d) -> p n d", d=D)
        rt = gt[:, :, :].rearrange("p a b -> p (a b)")[:, 0:8 * QT * NE].rearrange("p (i t e) -> p i t e", i=8, t=QT)
        qT = gt[:, 0, :]
        opT2 = gt[:, 2, :]
        room = sb("room", [128, 6 * QH], F16)
        pre_t = room[:, :].rearrange("p (k s t d) -> p k s t d", k=3, s=2, t=GRP)
        qg = room[:, 0:4 * QH].bitcast(F32).rearrange("p (h q) -> p h q", h=HALVES)
        qm = room[:, 4 * QH:6 * QH].rearrange("p (h q) -> p h q", h=HALVES)
        q_hi = sb("q_hi", [128, HALVES, QH], F16)
        q_lo = sb("q_lo", [128, HALVES, QH], F16)
        aug = sb("aug", [128, QH], BF16)
        mx = sb("mx", [128, QT, NG + 1])
        small = sb("small", [128, 64])
        NLN = 12
        lnst = sb("lnst", [128, QT, 6])
        lnmv = sb("lnmv", [128, NLN + 1, QT, 2])
        lnve = sb("lnve", [128, NLN, QT])
        lnrs = sb("lnrs", [128, NLN, QT])
        mhalf = sb("mhalf", [128, NT])
        cst = sb("cst", [128, NT, 6])
        ck = sb("ck", [128, 8, NT])
        mask_i = sb("mask_i", [128, NT], I32)
        bcols = sb("bcols", [128, 4])
        moe_g = c_key[:, :, 0:21, :]
        moe_u = c_key[:, :, 21:42, :]
        moe_d = c_val[:, :, :].rearrange("p t v -> p (t v)")[:, 0:2 * MOE_T * D].rearrange(
            "p (s t d) -> p s t d", s=2, t=MOE_T)
        stage = [ctx_nat[:, 0:21, :], ctx_nat[:, 21:42, :]]
        r8 = sb("r8", [128, QT, 8])
        g8 = sb("g8", [128, QT, 4, 8])
        gs = sb("gs", [128, 6, QT, 4])
        gp = sb("gp", [128, 3, QT, 16])
        coef = sb("coef", [128, QT, 64])
        cw16 = qm
        cq = sb("cq", [128, HALVES, QT])

        acc = ps("acc", [128, QT, 512])
        sco = ps("sco", [128, 2, 512])
        bk = [ps("bk6", [128, 512]), ps("bk7", [128, 512])]
        b6, b7 = bk

        block = ctx.enter_context(nc.Block())
        H = range(HALVES)

        CHUNKS = [(0, 12), (12, 24), (24, 36), (36, 50)]

        @block.sync
        def _(sp):
            cm = a["ctx_1024"].rearrange("a k d -> (a k) d")
            cmain = cm[0:FULL * D, :].rearrange("(p t) d -> p t d", t=FULL)
            sp.dma_start(xres[:, 0], a["x"].rearrange("a (h p t) d -> (a h) p t d", p=128, t=QT)[0]).then_inc(sem("in_x"), 16)
            sp.dma_start(ident[:, :], a["c_ident"]).then_inc(sem("in_id"), 16)
            sp.wait_ge(sem("clr"), 1)
            sp.dma_start(ctx_nat[0:REST, FULL, :], cm[FULL * D:NK, :]).then_inc(sem("in_rest"), 16)
            for c, (lo, hi) in enumerate(CHUNKS):
                sp.dma_start(ctx_nat[:, lo:hi, :], cmain[:, lo:hi, :]).then_inc(sem(f"in_c{c}"), 16)
            for i, n in enumerate(WNAMES):
                sp.dma_start(wraw[:, i, :], a[n]).then_inc(sem("in_w"), 16)
            sp.dma_start(wk0[:, :], a["L0_xattn_Wk"]).then_inc(sem("in_w"), 16)
            sp.dma_start(gw[:, :], a["L1_ffn_gate_weight"]).then_inc(sem("in_w"), 16)
            sp.dma_start(xres[:, 1], a["x"].rearrange("a (h p t) d -> (a h) p t d", p=128, t=QT)[1]).then_inc(sem("in_x1"), 16)
            for n in COLS:
                sp.dma_start(C[n], a[n].rearrange("(d o) -> d o", o=1)).then_inc(sem("in_v"), 16)
            sp.dma_start(gates[:, 0:2], a["g_xattn"].rearrange("(o d) -> o d", o=1).broadcast_to([128, 2])).then_inc(sem("in_v"), 16)
            sp.dma_start(gates[:, 2:4], a["g_ffn"].rearrange("(o d) -> o d", o=1).broadcast_to([128, 2])).then_inc(sem("in_v"), 16)
            mk = a["mask_BxS2_ik0"].rearrange("a k -> (a k)")
            sp.dma_start(mask_i[:, 0:FULL], mk[0:FULL * D].rearrange("(p t) -> p t", t=FULL)).then_inc(sem("in_m"), 16)
            sp.wait_ge(sem("set"), 1)
            sp.dma_start(mask_i[0:REST, FULL:NT], mk[FULL * D:NK].rearrange("(p t) -> p t", t=1)).then_inc(sem("in_m"), 16)
            sp.dma_start(seg[:, :], a["c_seg"]).then_inc(sem("in_k"), 16)
            sp.dma_start(lt4[:, :], a["c_lt4"]).then_inc(sem("in_k"), 16)
            sp.dma_start(cent[:, :], a["c_cent"]).then_inc(sem("in_u"), 16)
            sp.dma_start(wq1[:, :], a["L1_xattn_Wq"]).then_inc(sem("in_u"), 16)
            sp.dma_start(wv1[:, :], a["L1_xattn_Wv"]).then_inc(sem("in_u"), 16)
            for i, n in enumerate(("uf", "ui", "uc")):
                sp.dma_start(us[:, i, :], a["L0_ffn_" + n]).then_inc(sem("in_u"), 16)
            for n in ROWS:
                sp.dma_start(R[n], a[n].rearrange("(o d) -> o d", o=1).broadcast_to([128, 128])).then_inc(sem("in_u"), 16)
            sp.dma_start(gbias[:, :], a["L1_ffn_gate_bias"].rearrange("(o d) -> o d", o=1).broadcast_to([128, NE])).then_inc(sem("in_u"), 16)
            sp.wait_ge(sem("stage_clr"), 1)
            for i, (r, n, s) in enumerate((("w_gate", "anchor_w_gate", "shared_w_gate"),
                                           ("w_up", "anchor_w_up", "shared_w_up"))):
                sp.dma_start(stage[i][:, 0:16, :].rearrange("p t d -> p (t d)").rearrange("p (e i) -> p e i", e=NE),
                             a["L1_ffn_" + r].rearrange("e h i -> h e i")).then_inc(sem(f"in_w{i}"), 16)
                sp.dma_start(stage[i][:, 16:20, :].rearrange("p t d -> p (t d)").rearrange("p (e i) -> p e i", e=NA),
                             a["L1_ffn_" + n].rearrange("e h i -> h e i")).then_inc(sem(f"in_w{i}"), 16)
                sp.dma_start(stage[i][:, 20, 0:ME], a["L1_ffn_" + s]).then_inc(sem(f"in_w{i}"), 16)
            sp.wait_ge(sem("split_w"), 2)
            sp.dma_start(stage[0][:, 0:16, :], a["L1_ffn_w_down"].rearrange("(t e) i h -> (e i) t h", e=2)).then_inc(sem("in_w2"), 16)
            sp.dma_start(stage[0][:, 16:20, :], a["L1_ffn_anchor_w_down"].rearrange("(t e) i h -> (e i) t h", e=4)).then_inc(sem("in_w2"), 16)
            sp.dma_start(stage[0][0:ME, 20, :], a["L1_ffn_shared_w_down"]).then_inc(sem("in_w2"), 16)
            sp.wait_ge(sem("mx"), 16 * (NG + 1))
            sp.dma_start(sel, a["c_sel"].rearrange("p (t d) -> p t d", t=MOE_T)).then_inc(sem("in_k"), 16)
            for h in H:
                sp.wait_ge(sem("y_out"), h + 1)
                sp.dma_start(a["out"].rearrange("a (h p t) d -> (a h) p t d", p=128, t=QT)[h], xres[:, h]).then_inc(sem("stored"), 16)
            sp.wait_ge(sem("stored"), 32)

        @block.gpsimd
        def _(pool):
            nc.gpsimd.memset(ctx_nat[:, FULL, :], 0.0).then_inc(sem("clr"), 1)
            nc.gpsimd.memset(mhalf[:, :], -0.5).then_inc(sem("half"), 1)
            nc.gpsimd.memset(coef[:, :, :], 0.0).then_inc(sem("coef0"), 1)
            pool.wait_ge(sem("coef0"), 1)
            nc.gpsimd.memset(coef[:, :, 48:49], 1.0).then_inc(sem("coef1"), 1)
            pool.wait_ge(sem("half"), 1)

            def inv_root(n):
                pool.wait_ge(sem("ln_var"), n + 1)
                nc.gpsimd.tensor_tensor(lnrs[:, n, :], lnve[:, n, :], mhalf[:, 0:QT], ALU.pow).then_inc(sem("ln_inv"), 1)

            inv_root(0)
            inv_root(1)
            pool.wait_ge(sem("k_var"), 1)
            nc.gpsimd.tensor_tensor(ck[:, 2, :], ck[:, 1, :], mhalf[:, :], ALU.pow).then_inc(sem("k_inv"), 1)
            pool.wait_ge(sem("k_cols"), 1)

            def bc(i, t0, n):
                return ck[:, i, bass.ds(t0, n)].unsqueeze(2).broadcast_to([128, n, D])

            def prep(t0, n, g, s):
                x = ctx_nat[:, bass.ds(t0, n), :]
                nc.gpsimd.tensor_tensor(x, x, bc(3, t0, n), ALU.mult).then_inc(sem("pp"), 1)
                pool.wait_ge(sem("pp"), g * 2 + 1)
                nc.gpsimd.tensor_tensor(x, x, bc(4, t0, n), ALU.add).then_inc(sem("pp"), 1)
                pool.wait_ge(sem("pp"), g * 2 + 2)
                nc.gpsimd.tensor_tensor(pre1[:, s, 0:n, :], x, bc(5, t0, n), ALU.add).then_inc(sem("prep_pool"), 1)
                pool.wait_ge(sem("prep_pool"), g + 1)
                nc.gpsimd.tensor_tensor(pre_t[:, 2, s, 0:n, :], pre1[:, s, 0:n, :], bc(6, t0, n), ALU.add).then_inc(sem("prep_m"), 1)

            def pslot(g):
                pool.wait_ge(sem("prep_split"), g - 1)
                pool.wait_ge(sem("hm_done"), g - 1)
            prep(0, GRP, 0, 0)
            prep(GRP, GRP, 1, 1)
            with pool.Fori(2, NG - 1, 2) as g:
                for s in range(2):
                    pslot(g + s)
                    prep((g + s) * GRP, GRP, g + s, s)
            pslot(NG)
            prep(TAIL0, NT - TAIL0, NG, 0)
            for n in range(2, 4):
                inv_root(n)
            inv_root(4)
            pool.wait_ge(sem("prep_split"), NG + 1)
            nc.gpsimd.memset(ctx_nat[:, 20, ME:D], 0.0)
            nc.gpsimd.memset(ctx_nat[:, 41, ME:D], 0.0).then_inc(sem("stage_clr"), 1)
            for n in range(5, 8):
                inv_root(n)
            pool.wait_ge(sem("pv_done"), 2 * NT)

            def split(i, dst):
                w = stage[i % 2]
                nc.gpsimd.tensor_scalar(w, w, SPLIT, 1.0, ALU.mult, ALU.mult).then_inc(sem("sw"), 1)
                pool.wait_ge(sem("sw"), 2 * i + 1)
                nc.gpsimd.tensor_copy(dst[:, 0], w).then_inc(sem("sw"), 1)
                pool.wait_ge(sem("sw"), 2 * i + 2)
                nc.gpsimd.tensor_tensor(dst[:, 1], w, dst[:, 0], ALU.subtract).then_inc(sem("split_w"), 1)

            pool.wait_ge(sem("in_w0"), 48)
            split(0, moe_g)
            pool.wait_ge(sem("in_w1"), 48)
            split(1, moe_u)
            pool.wait_ge(sem("split_w"), 2)
            pool.wait_ge(sem("in_w2"), 48)
            nc.gpsimd.memset(ctx_nat[ME:D, 20, :], 0.0).then_inc(sem("dclr"), 1)
            pool.wait_ge(sem("dclr"), 1)
            split(2, moe_d)
            for n in range(8, 12):
                inv_root(n)

        @block.scalar
        def _(act):
            act.wait_ge(sem("in_id"), 16)
            nc.scalar.copy(ident16[:, :], ident[:, :]).then_inc(sem("id16"), 1)
            act.wait_ge(sem("in_rest"), 16)
            nc.scalar.mul(c_val[:, FULL, C_F:C_F + D], ctx_nat[:, FULL, :], SPLIT)
            for c, (lo, hi) in enumerate(CHUNKS):
                act.wait_ge(sem(f"in_c{c}"), 16)
                nc.scalar.mul(c_val[:, lo:hi, C_F:C_F + D], ctx_nat[:, lo:hi, :], SPLIT).then_inc(sem("c_hi"), 1)
            act.wait_ge(sem("wT_ps"), 1)
            nc.scalar.copy(wT[:, 0:4, :].rearrange("p a b -> p (a b)"), acc[:, 0, :])
            nc.scalar.copy(wT[:, 4:8, :].rearrange("p a b -> p (a b)"), acc[:, 1, :])
            nc.scalar.copy(gwT[:, :], acc[:, 2, 0:NE]).then_inc(sem("wT"), 1)
            act.wait_ge(sem("in_v"), 16 * (len(COLS) + 2))
            nc.scalar.activation(tg[:, :], gates[:, :], ACT.Tanh).then_inc(sem("tg"), 1)

            with act.Fori(0, NG - 1, 2) as g:
                act.wait_ge(sem("ct_ps"), g + 1)
                nc.scalar.copy(c_key[:, :, bass.ds(g * GRP, GRP), :].rearrange("p s t d -> p s (t d)"),
                               b6[:, :].bitcast(F16).rearrange("p (s w) -> p s w", s=2)).then_inc(sem("ct_even"), 1)
            act.wait_ge(sem("ct_ps"), NG + 1)
            nc.scalar.copy(c_key[:, :, TAIL0:NT, :].rearrange("p s t d -> p s (t d)"),
                           b6[:, :].bitcast(F16).rearrange("p (s w) -> p s w", s=2)[:, :, 0:(NT - TAIL0) * D]).then_inc(sem("ct_even"), 1)

            def query0(h):
                act.wait_ge(sem("t0"), h + 1)
                nc.scalar.copy(opT[:, :], b6[:, :]).then_inc(sem("t0_sb"), 1)
                act.wait_ge(sem("q0"), h + 1)
                nc.scalar.activation(qT[:, :], b7[:, :], ACT.Identity, bias=C["L0_xattn_bq"]).then_inc(sem("q0_sb"), 1)
                act.wait_ge(sem("k0"), h + 1)
                nc.scalar.mul(q_hi[:, h, :], b6[:, :], SPLIT).then_inc(sem("q_hi"), 1)

            def shift0(h):
                act.wait_ge(sem("m0_ps"), h + 1)
                nc.scalar.copy(aug[:, :], b7[:, :]).then_inc(sem("aug"), 1)

            def evict(idx, nm):
                act.wait_ge(sem("den"), idx + 1)
                for q in range(QT):
                    last = nc.scalar.mul(scr[:, q, :], acc[:, q, C_L:C_L + D], small[:, q:q + 1])
                last.then_inc(sem("av_lo"), 1)

            def mid(h):
                evict(h, 0)
                act.wait_ge(sem("avT"), h + 1)
                nc.scalar.copy(opT[:, :], b7[:, :]).then_inc(sem("avT_sb"), 1)
                act.wait_ge(sem("nT"), h + 1)
                nc.scalar.copy(opT[:, :], b6[:, :]).then_inc(sem("nT_sb"), 1)
                for i in range(3):
                    act.wait_ge(sem("gate_ps"), 3 * h + i + 1)
                    nc.scalar.activation(gt[:, i, :], bk[(i + 1) % 2][:, :], ACT.Tanh, bias=bcols[:, i:i + 1],
                                         scale=0.5 if i < 2 else 1.0).then_inc(sem("gate"), 1)
                act.wait_ge(sem("f_sum"), h + 1)
                nc.scalar.activation(avg[:, :, :], scr[:, :, :], ACT.Tanh).then_inc(sem("f_tanh"), 1)
                act.wait_ge(sem("q1"), h + 1)
                nc.scalar.activation(qT[:, :], b7[:, :], ACT.Identity, bias=C["L1_xattn_bq"]).then_inc(sem("q1_sb"), 1)
                act.wait_ge(sem("qc_sb"), h + 1)
                nc.scalar.activation(qm[:, h, :], qg[:, h, :], ACT.Copy, scale=SPLIT, bias=SPLIT).then_inc(sem("qm"), 1)

            def shift1(h):
                act.wait_ge(sem("g1"), h + 1)
                nc.scalar.mul(q_hi[:, h, :], opT[:, :], SPLIT).then_inc(sem("q_hi"), 1)

            def post(h):
                evict(2 + h, 0)

            def exps(ph, t, s, n=D, first=False):
                c = NT * ph + t
                act.wait_ge(sem("scores"), c + 1)
                if not first:
                    act.wait_ge(sem("pv_done"), c - 2)
                nc.scalar.activation(p_hi[0:n, s, :], sco[0:n, s % 2, :], ACT.Exp, scale=ATT_SCALE / PROD)
                nc.scalar.activation(p_f[0:n, s, :], sco[0:n, s % 2, :], ACT.Exp, scale=ATT_SCALE / PROD).then_inc(sem("exps"), 1)

            def prep_split(g, t0, n, s, first=False):
                act.wait_ge(sem("prep_pool"), g + 1)
                if not first:
                    act.wait_ge(sem("ht_m"), g - 1)
                nc.scalar.copy(h_val[:, bass.ds(t0, n), C_F:C_F + D], ctx_nat[:, bass.ds(t0, n), :])
                nc.scalar.copy(pre_t[:, 0, s, 0:n, :], pre1[:, s, 0:n, :]).then_inc(sem("h_hi"), 1)

            def prep_out(g, t0, n):
                act.wait_ge(sem("ht_ps"), g + 1)
                nc.scalar.copy(h_key[:, :, bass.ds(t0, n), :].rearrange("p s t d -> p s (t d)"),
                               b7[:, :].bitcast(F16).rearrange("p (s w) -> p s w", s=2)[:, :, 0:n * D]).then_inc(sem("ht_out"), 1)

            def main(ph):
                pr = ph == 0

                def trip(g, k, first):
                    if pr:
                        prep_split(g, g * GRP, GRP, k, first=first)
                    for s in range(GRP):
                        exps(ph, g * GRP + s, s, first=first and ph == 0 and k == 0 and s < 3)
                    if pr:
                        prep_out(g, g * GRP, GRP)
                trip(0, 0, True)
                trip(1, 1, True)
                with act.Fori(2, NG - 1, 2) as g:
                    trip(g, 0, False)
                    trip(g + 1, 1, False)
                if pr:
                    prep_split(NG, TAIL0, NT - TAIL0, 0)
                exps(ph, TAIL0, 0)
                exps(ph, TAIL0 + 1, 1)
                exps(ph, TAIL0 + 2, 2, REST)
                if pr:
                    prep_out(NG, TAIL0, NT - TAIL0)

            query0(0)
            query0(1)
            shift0(0)
            main(0)
            mid(0)
            shift0(1)
            main(1)
            mid(1)
            shift1(0)
            main(2)
            def post_act(h):
                evict(2 + h, 0)
                act.wait_ge(sem("n3T"), h + 1)
                nc.scalar.copy(opT[:, :], b6[:, :]).then_inc(sem("n3T_sb"), 1)
                act.wait_ge(sem("n3T_sb"), h + 1)
                nc.scalar.mul(q_hi[:, h, :], opT[:, :], SPLIT).then_inc(sem("x3_hi"), 1)
                act.wait_ge(sem("lg"), h + 1)
                nc.scalar.activation(rt[:, 0, :, :].rearrange("p a b -> p (a b)"), b7[:, 0:QT * NE], ACT.Tanh, scale=0.5).then_inc(sem("lg_t"), 1)
                act.wait_ge(sem("cwT"), h + 1)
                nc.scalar.mul(cw16[0:64, h, :], b6[0:64, :], CW_SCALE).then_inc(sem("cw_hi"), 1)

            def moe_act(h):
                def silu(t, s, first=False):
                    c = MOE_T * h + t
                    act.wait_ge(sem("gu"), c + 1)
                    if not first:
                        act.wait_ge(sem("t2"), c - 1)
                    elif h:
                        act.wait_ge(sem("t2"), MOE_T * h)
                    nc.scalar.activation(p_f[:, s, :], acc[:, s, :], ACT.Silu, scale=1.0 / PROD).then_inc(sem("silu"), 1)

                def high(t, s, first=False):
                    c = MOE_T * h + t
                    act.wait_ge(sem("t2"), c + 1)
                    if not first:
                        act.wait_ge(sem("down"), c - 1)
                    elif h:
                        act.wait_ge(sem("down"), MOE_T * h)
                    nc.scalar.copy(p_hi[:, s, :], p_f[:, 2 + s, :]).then_inc(sem("hid_hi"), 1)
                silu(0, 0, True)
                silu(1, 1, True)
                high(0, 0, True)
                silu(2, 0)
                high(1, 1, True)
                with act.Fori(2, MOE_T - 2, 2) as t:
                    silu(t + 1, 1)
                    high(t, 0)
                    silu(t + 2, 0)
                    high(t + 1, 1)
                high(MOE_T - 1, 0)
                act.wait_ge(sem("down"), MOE_T * h + MOE_T)
                nc.scalar.mul(opT[:, :], b7[:, :], 1.0 / (HID_SCALE * SPLIT)).then_inc(sem("yT"), 1)

            post_act(0)
            shift1(1)
            main(3)
            post_act(1)
            moe_act(0)
            moe_act(1)

        @block.vector
        def _(dve):
            chain = [0]
            V = nc.vector

            def link(ins):
                chain[0] += 1
                ins.then_inc(sem("v_chain"), 1)
                dve.wait_ge(sem("v_chain"), chain[0])

            def norm(n, src, dst, done):
                for q in range(QT):
                    last = V.bn_stats(lnst[:, q, :], src[:, q, :])
                link(last)
                for q in range(QT):
                    last = V.bn_aggr(lnmv[:, n, q, :], lnst[:, q, :])
                link(last)
                V.tensor_scalar(lnve[:, n, :], lnmv[:, n, :, 1], LN_EPS, None, ALU.add).then_inc(sem("ln_var"), 1)
                dve.wait_ge(sem("ln_inv"), n + 1)
                for q in range(QT):
                    last = V.tensor_scalar(dst[:, q, :], src[:, q, :], lnmv[:, n, q, 0:1], lnrs[:, n, q:q + 1],
                                           ALU.subtract, ALU.mult)
                if done:
                    last.then_inc(sem(done), 1)
                else:
                    link(last)

            def over(v, n=QT):
                return v.unsqueeze(1).broadcast_to([128, n, v.shape[1]])

            link(V.memset(ones[:, :], 1.0))
            V.memset(augw[:, :], PROD / 128.0)
            V.memset(c_val[:, :, C_ONE:C_ONE + 1], SPLIT)
            V.memset(mask_i[:, FULL:NT], 0).then_inc(sem("set"), 1)
            dve.wait_ge(sem("in_x"), 16)
            norm(0, xres[:, 0], nrm, "n0")
            for c, (lo, hi) in enumerate([(FULL, NT)] + CHUNKS):
                dve.wait_ge(sem("c_hi"), max(c, 1))
                V.scalar_tensor_tensor(c_val[:, lo:hi, C_L:C_L + D], ctx_nat[:, lo:hi, :], SPLIT,
                                       c_val[:, lo:hi, C_F:C_F + D], ALU.mult, ALU.subtract).then_inc(sem("c_lo"), 1)
            with dve.Fori(1, NG, 2) as g:
                dve.wait_ge(sem("ct_ps"), g + 1)
                V.tensor_copy(c_key[:, :, bass.ds(g * GRP, GRP), :].rearrange("p s t d -> p s (t d)"),
                              b7[:, :].bitcast(F16).rearrange("p (s w) -> p s w", s=2)).then_inc(sem("ct_odd"), 1)

            def query0(h):
                dve.wait_ge(sem("c0"), h + 1)
                V.tensor_copy(cq[:, h, :], b7[:, 0:QT]).then_inc(sem("cq"), 1)
                dve.wait_ge(sem("q_hi"), h + 1)
                V.scalar_tensor_tensor(q_lo[:, h, :], b6[:, :], SPLIT, q_hi[:, h, :], ALU.mult, ALU.subtract).then_inc(sem("q_lo"), 1)

            query0(0)
            dve.wait_ge(sem("in_x1"), 16)
            dve.wait_ge(sem("t0"), 1)
            norm(1, xres[:, 1], nrm, "n0")
            query0(1)

            for t in range(NT):
                last = V.bn_stats(cst[:, t, :], ctx_nat[:, t, :])
            link(last)
            link(V.tensor_tensor(ck[:, 0, :], cst[:, :, 1], cst[:, :, 4], ALU.add))
            link(V.tensor_tensor(ck[:, 1, :], cst[:, :, 2], cst[:, :, 5], ALU.add))
            link(V.tensor_tensor(ck[:, 7, :], cst[:, :, 1], cst[:, :, 4], ALU.subtract))
            link(V.tensor_scalar(ck[:, 0, :], ck[:, 0, :], 0.5, None, ALU.mult))
            link(V.tensor_tensor(ck[:, 7, :], ck[:, 7, :], ck[:, 7, :], ALU.mult))
            link(V.tensor_scalar(ck[:, 1, :], ck[:, 1, :], 1.0 / D, LN_EPS, ALU.mult, ALU.add))
            V.scalar_tensor_tensor(ck[:, 1, :], ck[:, 7, :], 0.25, ck[:, 1, :], ALU.mult, ALU.add).then_inc(sem("k_var"), 1)
            dve.wait_ge(sem("in_m"), 32)
            link(V.tensor_scalar(ck[:, 5, :], mask_i[:, :], 0.0, None, ALU.not_equal))
            V.reduce_max(small[:, 8:9], ck[:, 5, :], axis=AX.X).then_inc(sem("any"), 1)
            dve.wait_ge(sem("any_ps"), 1)
            link(V.tensor_scalar(small[:, 9:10], b7[:, 4:5], 1.0, None, ALU.min))
            link(V.tensor_scalar(small[:, 10:11], small[:, 9:10], -1.0, 1.0, ALU.mult, ALU.add))
            link(V.tensor_scalar(ck[:, 5, :], ck[:, 5, :], small[:, 10:11], None, ALU.max))
            V.tensor_scalar(ck[:, 6, :], ck[:, 5, :], 1.0, PEN, ALU.subtract, ALU.mult)
            link(V.tensor_scalar(ck[:, 5, :], ck[:, 5, :], SPLIT, None, ALU.mult))
            V.tensor_copy(h_val[:, :, C_ONE], ck[:, 5, :])
            dve.wait_ge(sem("k_inv"), 1)
            link(V.tensor_tensor(ck[:, 3, :], ck[:, 2, :], ck[:, 5, :], ALU.mult))
            V.scalar_tensor_tensor(ck[:, 4, :], ck[:, 0, :], -1.0, ck[:, 3, :], ALU.mult, ALU.mult).then_inc(sem("k_cols"), 1)
            dve.wait_ge(sem("in_u"), 16 * 13)
            dve.wait_ge(sem("tg"), 1)
            link(V.tensor_tensor(scr[:, 0:3, :], us[:, :, :], over(R["L0_ffn_in_c"], 3), ALU.mult))
            link(V.reduce_sum(bcols[:, 0:3], scr[:, 0:3, :], axis=AX.X))
            link(V.tensor_tensor(bcols[:, 0:3], bcols[:, 0:3], cols[:, 2:5], ALU.add))
            link(V.tensor_scalar(bcols[:, 0:2], bcols[:, 0:2], 0.5, None, ALU.mult))
            V.tensor_scalar(bcols[:, 3:4], C["L0_ffn_in_c"], 0.5, None, ALU.mult)
            for h in H:
                V.scalar_tensor_tensor(xres[:, h], over(R["L0_xattn_bv"]), tg[:, 0:1], xres[:, h], ALU.mult, ALU.add).then_inc(sem("consts"), 1)

            def low_p(ph, t, s, n=D):
                c = NT * ph + t
                dve.wait_ge(sem("exps"), c + 1)
                V.tensor_tensor(p_lo[0:n, s, :], p_f[0:n, s, :], p_hi[0:n, s, :], ALU.subtract).then_inc(sem("p_low"), 1)

            def max_g(k, g, j, bank, n=512):
                dve.wait_ge(sem("mx_ps"), 4 * (NG + 1) * k + 4 * g + j + 1)
                V.reduce_max(mx[:, j, bass.ds(g, 1)], bank[:, 0:n], axis=AX.X).then_inc(sem("mx"), 1)

            def prep_low(g, t0, n, s):
                dve.wait_ge(sem("h_hi"), g + 1)
                V.tensor_tensor(h_val[:, bass.ds(t0, n), C_L:C_L + D], ctx_nat[:, bass.ds(t0, n), :],
                                h_val[:, bass.ds(t0, n), C_F:C_F + D], ALU.subtract)
                V.tensor_tensor(pre_t[:, 1, s, 0:n, :], pre1[:, s, 0:n, :], pre_t[:, 0, s, 0:n, :],
                                ALU.subtract).then_inc(sem("prep_split"), 1)

            def hm_out(g, t0, n):
                dve.wait_ge(sem("ht_m"), g + 1)
                V.tensor_copy(h_max[:, bass.ds(t0, n), :].rearrange("p t d -> p (t d)"),
                              b7[:, :].bitcast(F16)[:, 0:n * D]).then_inc(sem("hm_done"), 1)

            def main(ph):
                k = ph + 1 if ph < 3 else None
                pr = ph == 0

                def trip(g, m, first):
                    if pr:
                        prep_low(g, g * GRP, GRP, m)
                    for s in range(GRP):
                        low_p(ph, g * GRP + s, s)
                        if k is not None:
                            max_g(k, g, s, b6)
                        if pr and s == 0 and not (first and m == 0):
                            hm_out(g - 1, (g - 1) * GRP, GRP)
                trip(0, 0, True)
                trip(1, 1, True)
                with dve.Fori(2, NG - 1, 2) as g:
                    trip(g, 0, False)
                    trip(g + 1, 1, False)
                if pr:
                    prep_low(NG, TAIL0, NT - TAIL0, 0)
                low_p(ph, TAIL0, 0)
                if pr:
                    hm_out(NG - 1, (NG - 1) * GRP, GRP)
                low_p(ph, TAIL0 + 1, 1)
                low_p(ph, TAIL0 + 2, 2, REST)
                if k is not None:
                    for j in range(QT):
                        max_g(k, NG, j, b6, TAILW)
                if pr:
                    hm_out(NG, TAIL0, NT - TAIL0)

            def diag(h, done):
                for q in range(QT):
                    last = V.tensor_scalar(scr[:, q, :], ident[:, :], small[:, 4 + q:5 + q], None, ALU.mult)
                last.then_inc(sem(done), 1)

            def shift0(h):
                dve.wait_ge(sem("mx"), 4 * (NG + 1) * (1 + h))
                link(V.reduce_max(small[:, 0:4], mx[:, :, :], axis=AX.X))
                link(V.scalar_tensor_tensor(small[:, 0:4], small[:, 0:4], 1.0 / PROD, cq[:, h, :], ALU.mult, ALU.add))
                link(V.tensor_tensor(small[:, 4:8], cq[:, h, :], small[:, 0:4], ALU.subtract))
                link(V.tensor_scalar(small[:, 4:8], small[:, 4:8], P_LOG, None, ALU.add))
                diag(h, "dg0")

            def shift1(h):
                dve.wait_ge(sem("mx"), 4 * (NG + 1) * (3 + h))
                link(V.reduce_max(small[:, 0:4], mx[:, :, :], axis=AX.X))
                link(V.tensor_scalar(small[:, 0:4], small[:, 0:4], 1.0 / PROD, -float(D), ALU.mult, ALU.add))
                link(V.scalar_tensor_tensor(small[:, 0:4], small[:, 0:4], small[:, 9:10], cq[:, h, :], ALU.mult, ALU.add))
                link(V.tensor_tensor(small[:, 4:8], cq[:, h, :], small[:, 0:4], ALU.subtract))
                link(V.tensor_scalar(small[:, 4:8], small[:, 4:8], P_LOG, 1.0 / D, ALU.add, ALU.mult))
                diag(h, "dg1")
                dve.wait_ge(sem("m1_ps"), h + 1)
                V.tensor_tensor(opT[:, :], b7[:, :], qg[:, h, :], ALU.add).then_inc(sem("g1"), 1)
                dve.wait_ge(sem("q_hi"), 3 + h)
                V.scalar_tensor_tensor(q_lo[:, h, :], opT[:, :], SPLIT, q_hi[:, h, :], ALU.mult, ALU.subtract).then_inc(sem("q_lo"), 1)

            def evict(idx):
                dve.wait_ge(sem("pv_done"), NT * (idx + 1))
                V.reciprocal(small[:, 0:4], acc[:, :, C_ONE]).then_inc(sem("den"), 1)
                dve.wait_ge(sem("av_lo"), idx + 1)
                dve.wait_ge(sem("den"), idx + 1)
                for q in range(QT):
                    last = V.scalar_tensor_tensor(avg[:, q, :], acc[:, q, C_F:C_F + D], small[:, q:q + 1],
                                                  scr[:, q, :], ALU.mult, ALU.add)
                last.then_inc(sem("av_done"), 1)

            def mid(h):
                evict(h)
                dve.wait_ge(sem("o_ps"), h + 1)
                link(V.scalar_tensor_tensor(xres[:, h], b6[:, :].rearrange("p (t d) -> p t d", t=QT), tg[:, 0:1],
                                            xres[:, h], ALU.mult, ALU.add))
                norm(2 + 3 * h, xres[:, h], nrm, "n1")
                dve.wait_ge(sem("gate"), 3 * h + 3)
                link(V.tensor_scalar(gt[:, 0, :], gt[:, 0, :], 1.0, bcols[:, 3:4], ALU.add, ALU.mult))
                link(V.scalar_tensor_tensor(gt[:, 1, :], gt[:, 1, :], 1.0, gt[:, 2, :], ALU.add, ALU.mult))
                V.scalar_tensor_tensor(opT2[:, :], gt[:, 1, :], 0.5, gt[:, 0, :], ALU.mult, ALU.add).then_inc(sem("cell"), 1)
                dve.wait_ge(sem("ffn_ps"), h + 1)
                V.tensor_tensor(scr[:, :, :], b6[:, :].rearrange("p (t d) -> p t d", t=QT), over(R["L0_ffn_bo"]),
                                ALU.add).then_inc(sem("f_sum"), 1)
                dve.wait_ge(sem("f_tanh"), h + 1)
                link(V.scalar_tensor_tensor(xres[:, h], avg[:, :, :], tg[:, 2:3], xres[:, h], ALU.mult, ALU.add))
                norm(3 + 3 * h, xres[:, h], nrm, None)
                norm(4 + 3 * h, nrm, avg, "n2")
                dve.wait_ge(sem("tT"), h + 1)
                V.tensor_scalar(opT[:, :], b6[:, :], C["L1_xattn_ln_t_g"], C["L1_xattn_ln_t_b"], ALU.mult, ALU.add).then_inc(sem("tT_sb"), 1)
                dve.wait_ge(sem("g0"), h + 1)
                V.tensor_copy(opT[:, :], b6[:, :])
                V.tensor_scalar(opT2[:, :], b6[:, :], C["L1_xattn_ln_a_g"], None, ALU.mult).then_inc(sem("g0_sb"), 1)
                dve.wait_ge(sem("qc"), h + 1)
                V.tensor_copy(cq[:, h, :], b7[:, 0:QT])
                V.tensor_scalar(qg[:, h, :], b6[:, :], small[:, 9:10], None, ALU.mult).then_inc(sem("qc_sb"), 1)

            def post(h):
                evict(2 + h)
                dve.wait_ge(sem("av1T"), h + 1)
                V.tensor_scalar(opT[:, :], b7[:, :], C["L1_xattn_ln_a_g"], C["L1_xattn_ln_a_b"], ALU.mult, ALU.add).then_inc(sem("av1T_sb"), 1)
                dve.wait_ge(sem("o1_ps"), h + 1)
                link(V.tensor_tensor(scr[:, :, :], b6[:, :].rearrange("p (t d) -> p t d", t=QT), over(R["L1_xattn_bv"]), ALU.add))
                norm(8 + 2 * h, scr, nrm, None)
                link(V.tensor_tensor(nrm[:, :, :], nrm[:, :, :], over(R["L1_xattn_ln_p_g"]), ALU.mult))
                link(V.tensor_tensor(nrm[:, :, :], nrm[:, :, :], over(R["L1_xattn_ln_p_b"]), ALU.add))
                link(V.scalar_tensor_tensor(xres[:, h], nrm[:, :, :], tg[:, 1:2], xres[:, h], ALU.mult, ALU.add))
                norm(9 + 2 * h, xres[:, h], nrm, "n3")
                dve.wait_ge(sem("x3_hi"), h + 1)
                V.scalar_tensor_tensor(q_lo[:, h, :], opT[:, :], SPLIT, q_hi[:, h, :], ALU.mult, ALU.subtract).then_inc(sem("x3_lo"), 1)
                route(h)
                dve.wait_ge(sem("cw_hi"), h + 1)
                V.scalar_tensor_tensor(cw16[64:128, h, :], b6[0:64, :], CW_SCALE, cw16[0:64, h, :], ALU.mult, ALU.subtract).then_inc(sem("cw_lo"), 1)

            def wide(v, n):
                return v.unsqueeze(3).broadcast_to([128, QT, v.shape[2], n])

            def route(h):
                dve.wait_ge(sem("lg_t"), h + 1)
                sc, sb_, m, gtv, eq, pre, pick, top = (rt[:, i, :, :] for i in range(8))
                link(V.tensor_scalar(sc, sc, 0.5, 0.5, ALU.mult, ALU.add))
                link(V.tensor_tensor(sb_, sc, over(gbias[:, :]), ALU.add))
                for q in range(QT):
                    for g in range(4):
                        last = V.max(g8[:, q, g, :], rt[:, 1, q, 8 * g:8 * g + 8])
                link(last)
                link(V.tensor_tensor(gs[:, 0], g8[:, :, :, 0], g8[:, :, :, 1], ALU.add))
                mine = gs[:, 0].unsqueeze(3).broadcast_to([128, QT, 4, 4])
                other = gs[:, 0].unsqueeze(2).broadcast_to([128, QT, 4, 4])

                def v4(i):
                    return gp[:, i].rearrange("p t (i j) -> p t i j", i=4)
                V.tensor_tensor(v4(0), other, mine, ALU.is_gt)
                link(V.tensor_tensor(v4(1), other, mine, ALU.is_equal))
                link(V.tensor_tensor(gp[:, 1], gp[:, 1], over(lt4[:, :]), ALU.mult))
                link(V.tensor_tensor(gp[:, 0], gp[:, 0], gp[:, 1], ALU.add))
                link(V.reduce_sum(gs[:, 1], v4(0), axis=AX.X))
                link(V.tensor_scalar(gs[:, 2], gs[:, 1], 1.5, None, ALU.is_lt))
                link(V.tensor_scalar(gs[:, 3], gs[:, 2], 1.0, 1e30, ALU.subtract, ALU.mult))
                link(V.tensor_tensor(m.rearrange("p t (g e) -> p t g e", g=4), sb_.rearrange("p t (g e) -> p t g e", g=4),
                                     wide(gs[:, 3], 8), ALU.add))
                for q in range(QT):
                    last = V.max(r8[:, q, :], rt[:, 2, q, :])
                link(last)

                def nth(i):
                    return r8[:, :, i:i + 1].broadcast_to([128, QT, NE])

                def place(eqv, out):
                    link(V.tensor_tensor_scan(out.rearrange("p t e -> p (t e)"), seg[:, :],
                                              eqv.rearrange("p t e -> p (t e)"), 0.0, ALU.mult, ALU.add))
                V.tensor_tensor(gtv, m, nth(TOPK - 1), ALU.is_gt)
                V.tensor_tensor(top, m, nth(0), ALU.is_equal)
                link(V.tensor_tensor(eq, m, nth(TOPK - 1), ALU.is_equal))
                link(V.reduce_sum(gs[:, 4, :, 0], gtv, axis=AX.X))
                place(eq, pre)
                link(V.tensor_tensor(pre, pre, gs[:, 4, :, 0:1].broadcast_to([128, QT, NE]), ALU.add))
                link(V.scalar_tensor_tensor(pre, pre, TOPK + 0.5, eq, ALU.is_lt, ALU.mult))
                link(V.tensor_tensor(pick, gtv, pre, ALU.add))
                link(V.tensor_tensor(pick, pick, sc, ALU.mult))
                link(V.reduce_sum(gs[:, 5, :, 0], pick, axis=AX.X))
                link(V.tensor_scalar(gs[:, 5, :, 0], gs[:, 5, :, 0], 1e-20, None, ALU.add))
                link(V.reciprocal(gs[:, 5, :, 1], gs[:, 5, :, 0]))
                link(V.tensor_scalar(gs[:, 5, :, 1], gs[:, 5, :, 1], ROUTED_SCALE, None, ALU.mult))
                if h == 0:
                    dve.wait_ge(sem("coef1"), 1)
                V.tensor_tensor(coef[:, :, 0:NE], pick, gs[:, 5, :, 1:2].broadcast_to([128, QT, NE]), ALU.mult)
                place(top, pre)
                link(V.scalar_tensor_tensor(pre, pre, 1.5, top, ALU.is_lt, ALU.mult))
                pairs = pre.rearrange("p t (a b) -> p t a b", b=2)
                link(V.tensor_tensor(coef[:, :, NE:NE + NA], pairs[:, :, :, 0], pairs[:, :, :, 1], ALU.add))
                V.tensor_scalar(coef[:, :, NE:NE + NA], coef[:, :, NE:NE + NA], ANCHOR_ALPHA, None, ALU.mult).then_inc(sem("coef"), 1)

            def moe(h):
                def t1(t, s):
                    dve.wait_ge(sem("silu"), MOE_T * h + t + 1)
                    V.scalar_tensor_tensor(p_f[:, s, :], acc[:, 2 + s, :], HID_SCALE / (PROD * CW_SCALE), p_f[:, s, :],
                                           ALU.mult, ALU.mult).then_inc(sem("t1"), 1)

                def low(t, s):
                    dve.wait_ge(sem("hid_hi"), MOE_T * h + t + 1)
                    V.tensor_tensor(p_lo[:, s, :], p_f[:, 2 + s, :], p_hi[:, s, :], ALU.subtract).then_inc(sem("hid_lo"), 1)

                def t2(t, s):
                    dve.wait_ge(sem("t1"), MOE_T * h + t + 1)
                    V.tensor_tensor(p_f[:, 2 + s, :], sco[:, s, :], p_f[:, s, :], ALU.mult).then_inc(sem("t2"), 1)
                t1(0, 0)
                t2(0, 0)
                t1(1, 1)
                low(0, 0)
                t2(1, 1)
                with dve.Fori(2, MOE_T - 2, 2) as t:
                    t1(t, 0)
                    low(t - 1, 1)
                    t2(t, 0)
                    t1(t + 1, 1)
                    low(t, 0)
                    t2(t + 1, 1)
                t1(MOE_T - 1, 0)
                low(MOE_T - 2, 1)
                t2(MOE_T - 1, 0)
                low(MOE_T - 1, 0)
                dve.wait_ge(sem("y_ps"), h + 1)
                V.scalar_tensor_tensor(xres[:, h], b6[:, :].rearrange("p (t d) -> p t d", t=QT), tg[:, 3:4],
                                       xres[:, h], ALU.mult, ALU.add).then_inc(sem("y_out"), 1)

            with dve.Fori(0, NG) as g:
                for j in range(QT):
                    max_g(0, g, j, bk[j % 2])
            for j in range(QT):
                max_g(0, NG, j, bk[j % 2], TAILW)
            shift0(0)
            main(0)
            mid(0)
            shift0(1)
            main(1)
            mid(1)
            shift1(0)
            main(2)
            post(0)
            shift1(1)
            main(3)
            post(1)
            moe(0)
            moe(1)

        @block.tensor
        def _(pe):
            T = nc.tensor

            def transp4(dst, src, done, n=128):
                for q in range(QT):
                    last = T.transpose(dst[0:n, q * D:(q + 1) * D], src[:, q, :], ident[:, :])
                last.then_inc(sem(done), 1)

            pe.wait_ge(sem("in_w"), 16 * (len(WNAMES) + 2))
            pe.wait_ge(sem("in_id"), 16)
            for i in range(len(WNAMES)):
                T.transpose(acc[:, i // 4, (i % 4) * D:(i % 4 + 1) * D], wraw[:, i, :], ident[:, :])
            T.transpose(acc[:, 2, 0:NE], gw[:, :], ident[0:NE, 0:NE]).then_inc(sem("wT_ps"), 1)

            def turn(bank, t0, n):
                for half, c0 in ((0, C_F), (1, C_L)):
                    for j in range(n):
                        last = T.transpose(bank[:, :].bitcast(F16)[:, half * 512 + j * D:half * 512 + (j + 1) * D],
                                           c_val[:, t0 + j, c0:c0 + D], ident16[:, :])
                last.then_inc(sem("ct_ps"), 1)
            pe.wait_ge(sem("id16"), 1)
            for g in range(3):
                if g == 0:
                    pe.wait_ge(sem("c_lo"), 2)
                if g == 2:
                    pe.wait_ge(sem("ct_even"), 1)
                turn(bk[g % 2], g * GRP, GRP)
            pe.wait_ge(sem("c_lo"), 5)
            with pe.Fori(1, NG // 2 - 1) as u:
                pe.wait_ge(sem("ct_odd"), u)
                turn(b7, (2 * u + 1) * GRP, GRP)
                pe.wait_ge(sem("ct_even"), u + 1)
                turn(b6, (2 * u + 2) * GRP, GRP)
            pe.wait_ge(sem("ct_odd"), 5)
            turn(b7, (NG - 1) * GRP, GRP)
            pe.wait_ge(sem("ct_even"), 6)
            turn(b6, TAIL0, NT - TAIL0)

            def query0(h):
                pe.wait_ge(sem("n0"), h + 1)
                if h == 0:
                    pe.wait_ge(sem("ct_even"), 7)
                    pe.wait_ge(sem("ct_odd"), 6)
                    pe.wait_ge(sem("wT"), 1)
                else:
                    pe.wait_ge(sem("q_lo"), 1)
                transp4(b6, nrm, "t0")
                pe.wait_ge(sem("t0_sb"), h + 1)
                if h:
                    pe.wait_ge(sem("cq"), h)
                T.matmul(b7[:, :], W["L0_xattn_Wq"], opT[:, :], start=True, stop=True).then_inc(sem("q0"), 1)
                pe.wait_ge(sem("q0_sb"), h + 1)
                for q in range(QT):
                    last = T.matmul(b7[:, q:q + 1], qT[:, q * D:(q + 1) * D], C["L0_xattn_bk"], start=True, stop=True)
                last.then_inc(sem("c0"), 1)
                T.matmul(b6[:, :], wk0[:, :], qT[:, :], start=True, stop=True).then_inc(sem("k0"), 1)

            pe.wait_ge(sem("in_v"), 16 * (len(COLS) + 2))
            query0(0)
            query0(1)
            pe.wait_ge(sem("any"), 1)
            pe.wait_ge(sem("cq"), 2)
            T.matmul(b7[:, 4:5], ones[:, :], small[:, 8:9], start=True, stop=True).then_inc(sem("any_ps"), 1)

            def max_mm(k, g, j, bank, n=512, two=False, first=False):
                c = 4 * (NG + 1) * k + 4 * g + j
                if not first:
                    pe.wait_ge(sem("mx"), c - 1 if two else c)
                keys, qs = (c_key[:, 0], q_hi) if k < 2 else (h_max, qm)
                T.matmul(bank[:, 0:n], qs[:, k % 2, j * D:(j + 1) * D],
                         keys[:, bass.ds(g * GRP, GRP), :].rearrange("p t d -> p (t d)") if n == 512 else
                         keys[:, TAIL0:NT, :].rearrange("p t d -> p (t d)")[:, 0:n],
                         start=True, stop=True).then_inc(sem("mx_ps"), 1)

            def scores(ph, t, s, n=D, first=False):
                c = NT * ph + t
                L, h = ph // 2, ph % 2
                if not first:
                    pe.wait_ge(sem("exps"), c - 1)
                elif ph:
                    pe.wait_ge(sem("exps"), NT * ph)
                kk = h_key if L else c_key
                out = sco[0:n, s, :]
                if L == 0:
                    T.matmul(out, augw[:, 0:n], aug[:, :], start=True, stop=False)
                T.matmul(out, kk[:, 0, t, 0:n], q_hi[:, h, :], start=bool(L), stop=False)
                T.matmul(out, kk[:, 0, t, 0:n], q_lo[:, h, :], start=False, stop=False)
                T.matmul(out, kk[:, 1, t, 0:n], q_hi[:, h, :], start=False, stop=True).then_inc(sem("scores"), 1)

            def pv(ph, t, s, n=D, start=False, stop=False):
                pe.wait_ge(sem("p_low"), NT * ph + t + 1)
                if start and ph:
                    pe.wait_ge(sem("av_done"), ph)
                val = h_val if ph // 2 else c_val
                for q in range(QT):
                    T.matmul(acc[:, q, 0:VW], p_hi[0:n, s, q * D:(q + 1) * D], val[0:n, t, :], start=start, stop=False)
                    last = T.matmul(acc[:, q, 0:D + 1], p_lo[0:n, s, q * D:(q + 1) * D], val[0:n, t, 0:D + 1],
                                    start=False, stop=stop)
                last.then_inc(sem("pv_done"), 1)

            def turn_h(g, s, n, m):
                if m == 0:
                    pe.wait_ge(sem("prep_split"), g + 1)
                else:
                    pe.wait_ge(sem("ht_out"), g + 1)
                    pe.wait_ge(sem("prep_m"), g + 1)
                for half in ((0, 1) if m == 0 else (2,)):
                    for j in range(n):
                        o = (half % 2) * 512 + j * D
                        last = T.transpose(b7[:, :].bitcast(F16)[:, o:o + D], pre_t[:, half, s, j, :], ident16[:, :])
                last.then_inc(sem("ht_ps" if m == 0 else "ht_m"), 1)

            def main(ph):
                k = ph + 1 if ph < 3 else None
                pr = ph == 0

                def trip(g, m, first):
                    for s in range(GRP):
                        scores(ph, g * GRP + s + 2, s % 2)
                        pv(ph, g * GRP + s, s, start=first and m == 0 and s == 0)
                        if k is not None:
                            max_mm(k, g, s, b6)
                        if pr and s == 1:
                            if not (first and m == 0):
                                pe.wait_ge(sem("hm_done"), g)
                            turn_h(g, m, GRP, 0)
                        if pr and s == 3:
                            turn_h(g, m, GRP, 1)
                if ph < 2:
                    pe.wait_ge(sem("aug"), ph % 2 + 1)
                else:
                    pe.wait_ge(sem("q_lo"), 3 + ph % 2)
                if k is not None and k >= 2:
                    pe.wait_ge(sem("qm"), k - 1)
                    pe.wait_ge(sem("hm_done"), NG + 1)
                scores(ph, 0, 0, first=True)
                scores(ph, 1, 1, first=True)
                trip(0, 0, True)
                trip(1, 1, True)
                with pe.Fori(2, NG - 1, 2) as g:
                    trip(g, 0, False)
                    trip(g + 1, 1, False)
                scores(ph, FULL, 0, REST)
                pv(ph, TAIL0, 0)
                if pr:
                    pe.wait_ge(sem("hm_done"), NG)
                    turn_h(NG, 0, NT - TAIL0, 0)
                pv(ph, TAIL0 + 1, 1)
                pv(ph, TAIL0 + 2, 2, REST, stop=True)
                if k is not None:
                    for j in range(QT):
                        max_mm(k, NG, j, b6, TAILW)
                if pr:
                    turn_h(NG, 0, NT - TAIL0, 1)

            def shift(h, L):
                pe.wait_ge(sem(f"dg{L}"), h + 1)
                if h == 1 and L == 0:
                    pe.wait_ge(sem("qc_sb"), 1)
                if h == 0 and L == 1:
                    pe.wait_ge(sem("qc_sb"), 2)
                T.matmul(b7[:, :], ones[:, :], scr[:, :, :].rearrange("p t d -> p (t d)"), start=True,
                         stop=True).then_inc(sem(f"m{L}_ps"), 1)

            def mid(h):
                pe.wait_ge(sem("av_done"), h + 1)
                pe.wait_ge(sem("aug"), h + 1)
                if h == 0:
                    pe.wait_ge(sem("hm_done"), NG + 1)
                transp4(b7, avg, "avT")
                pe.wait_ge(sem("avT_sb"), h + 1)
                pe.wait_ge(sem("mx"), 4 * (NG + 1) * (h + 2))
                for q in range(QT):
                    last = T.matmul(b6[:, q * D:(q + 1) * D], opT[:, q * D:(q + 1) * D], W["L0_xattn_Wv"], start=True, stop=True)
                last.then_inc(sem("o_ps"), 1)
                pe.wait_ge(sem("n1"), h + 1)
                transp4(b6, nrm, "nT")
                pe.wait_ge(sem("nT_sb"), h + 1)
                for i, n in enumerate(("wf", "wi", "wc")):
                    if i == 2:
                        pe.wait_ge(sem("gate"), 3 * h + 1)
                    T.matmul(bk[(i + 1) % 2][:, :], W["L0_ffn_" + n], opT[:, :], start=True, stop=True).then_inc(sem("gate_ps"), 1)
                pe.wait_ge(sem("cell"), h + 1)
                for q in range(QT):
                    o = b6[:, q * D:(q + 1) * D]
                    T.matmul(o, opT[:, q * D:(q + 1) * D], W["L0_ffn_wo"], start=True, stop=False)
                    last = T.matmul(o, opT2[:, q * D:(q + 1) * D], W["L0_ffn_uo"], start=False, stop=True)
                last.then_inc(sem("ffn_ps"), 1)
                pe.wait_ge(sem("n2"), h + 1)
                transp4(b6, avg, "tT")
                pe.wait_ge(sem("tT_sb"), h + 1)
                T.matmul(b7[:, :], wq1[:, :], opT[:, :], start=True, stop=True).then_inc(sem("q1"), 1)
                pe.wait_ge(sem("q1_sb"), h + 1)
                T.matmul(b6[:, :], W["L1_xattn_Wk"], qT[:, :], start=True, stop=True).then_inc(sem("g0"), 1)
                pe.wait_ge(sem("g0_sb"), h + 1)
                for q in range(QT):
                    T.matmul(b7[:, q:q + 1], opT[:, q * D:(q + 1) * D], C["L1_xattn_ln_a_b"], start=True, stop=False)
                    T.matmul(b7[:, q:q + 1], qT[:, q * D:(q + 1) * D], C["L1_xattn_bk"], start=False, stop=True)
                T.matmul(b6[:, :], cent[:, :], opT2[:, :], start=True, stop=True).then_inc(sem("qc"), 1)

            def post(h):
                pe.wait_ge(sem("av_done"), 3 + h)
                transp4(b7, avg, "av1T")
                pe.wait_ge(sem("av1T_sb"), h + 1)
                if h == 0:
                    pe.wait_ge(sem("mx"), 4 * (NG + 1) * 4)
                for q in range(QT):
                    last = T.matmul(b6[:, q * D:(q + 1) * D], opT[:, q * D:(q + 1) * D], wv1[:, :], start=True, stop=True)
                last.then_inc(sem("o1_ps"), 1)
                pe.wait_ge(sem("n3"), h + 1)
                transp4(b6, nrm, "n3T")
                pe.wait_ge(sem("n3T_sb"), h + 1)
                for q in range(QT):
                    last = T.matmul(b7[:, q * NE:(q + 1) * NE], opT[:, q * D:(q + 1) * D], gwT[:, :], start=True, stop=True)
                last.then_inc(sem("lg"), 1)
                pe.wait_ge(sem("coef"), h + 1)
                transp4(b6, coef, "cwT", 64)

            def moe(h):
                def gu(t, s, first=False):
                    c = MOE_T * h + t
                    if not first:
                        pe.wait_ge(sem("t2"), c - 1)
                    elif h:
                        pe.wait_ge(sem("t2"), MOE_T * h)
                    for w, out in ((moe_g, acc[:, s, :]), (moe_u, acc[:, 2 + s, :])):
                        T.matmul(out, w[:, 0, t, :], q_hi[:, h, :], start=True, stop=False)
                        T.matmul(out, w[:, 0, t, :], q_lo[:, h, :], start=False, stop=False)
                        T.matmul(out, w[:, 1, t, :], q_hi[:, h, :], start=False, stop=True)
                    T.matmul(sco[:, s, :], sel[:, t, :], cw16[:, h, :], start=True, stop=True).then_inc(sem("gu"), 1)

                def down(t, s, start=False, stop=False):
                    pe.wait_ge(sem("hid_lo"), MOE_T * h + t + 1)
                    T.matmul(b7[:, :], moe_d[:, 0, t, :], p_hi[:, s, :], start=start, stop=False)
                    T.matmul(b7[:, :], moe_d[:, 0, t, :], p_lo[:, s, :], start=False, stop=False)
                    T.matmul(b7[:, :], moe_d[:, 1, t, :], p_hi[:, s, :], start=False, stop=stop).then_inc(sem("down"), 1)
                gu(0, 0, True)
                gu(1, 1, True)
                gu(2, 0)
                if h:
                    pe.wait_ge(sem("yT"), h)
                down(0, 0, start=True)
                gu(3, 1)
                down(1, 1)
                with pe.Fori(2, MOE_T - 4, 2) as t:
                    gu(t + 2, 0)
                    down(t, 0)
                    gu(t + 3, 1)
                    down(t + 1, 1)
                gu(MOE_T - 1, 0)
                down(MOE_T - 3, 0)
                down(MOE_T - 2, 1)
                down(MOE_T - 1, 0, stop=True)
                pe.wait_ge(sem("yT"), h + 1)
                if h:
                    pe.wait_ge(sem("y_out"), h)
                transp4(b6, opT[:, :].rearrange("p (t d) -> p t d", t=QT), "y_ps")

            pe.wait_ge(sem("q_lo"), 2)
            for j in range(QT):
                if j == 1:
                    pe.wait_ge(sem("k_cols"), 1)
                max_mm(0, 0, j, bk[j % 2], two=True, first=j < 2)
            with pe.Fori(1, NG) as g:
                for j in range(QT):
                    max_mm(0, g, j, bk[j % 2], two=True)
            for j in range(QT):
                max_mm(0, NG, j, bk[j % 2], TAILW, two=True)
            pe.wait_ge(sem("mx"), 4 * (NG + 1))
            shift(0, 0)
            main(0)
            mid(0)
            shift(1, 0)
            main(1)
            mid(1)
            shift(0, 1)
            main(2)
            post(0)
            shift(1, 1)
            main(3)
            post(1)
            pe.wait_ge(sem("cw_lo"), 2)
            pe.wait_ge(sem("split_w"), 3)
            pe.wait_ge(sem("in_k"), 48)
            moe(0)
            moe(1)


_INS = ['x', 'ctx_1024', 'mask_BxS2_ik0', 'g_xattn', 'g_ffn', 'L0_xattn_Wq', 'L0_xattn_bq', 'L0_xattn_Wk', 'L0_xattn_bk', 'L0_xattn_Wv', 'L0_xattn_bv', 'L0_ffn_wf', 'L0_ffn_uf', 'L0_ffn_bf', 'L0_ffn_wi', 'L0_ffn_ui', 'L0_ffn_bi', 'L0_ffn_wc', 'L0_ffn_uc', 'L0_ffn_bc', 'L0_ffn_wo', 'L0_ffn_uo', 'L0_ffn_bo', 'L0_ffn_in_c', 'L1_xattn_ln_t_g', 'L1_xattn_ln_t_b', 'L1_xattn_ln_a_g', 'L1_xattn_ln_a_b', 'L1_xattn_Wq', 'L1_xattn_bq', 'L1_xattn_Wk', 'L1_xattn_bk', 'L1_xattn_Wv', 'L1_xattn_bv', 'L1_xattn_ln_p_g', 'L1_xattn_ln_p_b', 'L1_ffn_gate_weight', 'L1_ffn_gate_bias', 'L1_ffn_w_gate', 'L1_ffn_w_up', 'L1_ffn_w_down', 'L1_ffn_shared_w_gate', 'L1_ffn_shared_w_up', 'L1_ffn_shared_w_down', 'L1_ffn_anchor_w_gate', 'L1_ffn_anchor_w_up', 'L1_ffn_anchor_w_down']


def _constants():
    import numpy as np
    seg = np.ones((128, QT, NE), np.float32)
    seg[:, :, 0] = 0.0
    i, j = np.divmod(np.arange(16), 4)
    lt4 = np.broadcast_to((j < i).astype(np.float32), (128, 16))
    sel = np.zeros((128, MOE_T, D), np.float16)
    lane = np.arange(D)
    for t in range(MOE_T):
        if t < ROUTED_T:
            r = 2 * t + lane // ME
        elif t < ROUTED_T + ANCHOR_T:
            r = NE + 4 * (t - ROUTED_T) + lane // MA
        else:
            r = np.full(D, NE + NA)
        sel[r, t, lane] = 1.0
        sel[64 + r, t, lane] = 1.0
    return {
        "c_ident": np.eye(D, dtype=np.float32),
        "c_cent": (np.eye(D) - 1.0 / D).astype(np.float32),
        "c_seg": seg.reshape(128, QT * NE),
        "c_lt4": np.ascontiguousarray(lt4),
        "c_sel": sel.reshape(128, MOE_T * D),
    }


def kernel(**inputs):
    import numpy as _np
    import concourse.bacc as _bacc
    from concourse import mybir as _mybir
    from concourse.bass_utils import run_bass_kernel_spmd as _run

    nc = _bacc.Bacc("TRN2", target_bir_lowering=False, num_devices=1)
    arrays, args = {}, {}
    data = {name: inputs[name] for name in _INS}
    data.update(_constants())
    for name, value in data.items():
        v = _np.ascontiguousarray(value)
        arrays[f"in_{name}_dram"] = v
        args[name] = nc.dram_tensor(f"in_{name}_dram", v.shape, _mybir.dt.from_np(v.dtype), kind="ExternalInput").ap()
    args["out"] = nc.dram_tensor("out_0_dram", (1, NQ, D), _mybir.dt.float32, kind="ExternalOutput").ap()
    build(nc, args)
    r = _run(nc, [arrays], core_ids=[0])
    return r.results[0]["out_0_dram"]
```

```python
import concourse.bass as bass
from concourse import mybir
from concourse.alu_op_type import AluOpType as ALU
from contextlib import ExitStack

F32 = mybir.dt.float32
F16 = mybir.dt.float16
BF16 = mybir.dt.bfloat16
I32 = mybir.dt.int32
ACT = mybir.ActivationFunctionType
AX = mybir.AxisListType

D = 128
NQ = 1024
HALVES = 2
QT = 4
QH = QT * D
NK = 6404
FULL = NK // D
REST = NK - FULL * D
NT = FULL + 1
GRP = 4
NG = 12
TAIL0 = NG * GRP
TAILW = NK - TAIL0 * D
NE, ME = 32, 64
NA, MA = 16, 32
MOE_T = 21
ROUTED_T, ANCHOR_T = 16, 4
TOPK = 6
ROUTED_SCALE = 0.2
ANCHOR_ALPHA = 0.1

SPLIT = 256.0
PROD = SPLIT * SPLIT
ATT_SCALE = float(D) ** -0.5
P_LOG = 12 * 0.6931471805599453 / ATT_SCALE
PEN = 65280.0
CW_SCALE = 1024.0
HID_SCALE = 32.0
LN_EPS = 1e-5
C_F, C_ONE, C_L = 0, D, D + 1
VW = 2 * D + 1


def build(nc, a):
    ctx = ExitStack()
    with ctx:
        def sb(name, shape, dt=F32):
            return ctx.enter_context(nc.sbuf_tensor(name, shape, dt))

        def ps(name, shape, dt=F32):
            return ctx.enter_context(nc.psum_tensor(name, shape, dt))

        made = {}

        def sem(name):
            if name not in made:
                made[name] = ctx.enter_context(nc.semaphore(name))
            return made[name]

        ctx_nat = sb("ctx_nat", [128, NT, D])
        c_val = sb("c_val", [128, NT, VW], F16)
        h_val = sb("h_val", [128, NT, VW], F16)
        c_key = sb("c_key", [128, 2, NT, D], F16)
        h_key = sb("h_key", [128, 2, NT, D], F16)
        h_max = sb("h_max", [128, NT, D], F16)
        p_hi = sb("p_hi", [128, GRP, QH], F16)
        p_lo = sb("p_lo", [128, GRP, QH], F16)
        p_f = sb("p_f", [128, GRP, QH])
        ident = sb("ident", [128, 128])
        ident16 = sb("ident16", [128, 128], F16)
        cent = sb("cent", [128, 128])
        ones = sb("ones", [128, 128])
        ones16 = sb("ones16", [128, 1], F16)
        augw = sb("augw", [128, 128], BF16)
        WNAMES = ["L0_xattn_Wq", "L0_xattn_Wv", "L0_ffn_wf", "L0_ffn_wi", "L0_ffn_wc", "L0_ffn_wo",
                  "L0_ffn_uo", "L1_xattn_Wk"]
        wT = sb("wT", [128, len(WNAMES), 128])
        W = {n: wT[:, i, :] for i, n in enumerate(WNAMES)}
        wk0 = sb("wk0", [128, 128])
        wq1 = sb("wq1", [128, 128])
        wv1 = sb("wv1", [128, 128])
        gw = sb("gw", [NE, 128])
        gwT = sb("gwT", [128, NE])
        us = sb("us", [128, 3, 128])
        COLS = ["L0_xattn_bq", "L0_xattn_bk", "L0_ffn_bf", "L0_ffn_bi", "L0_ffn_bc", "L0_ffn_in_c",
                "L1_xattn_ln_t_g", "L1_xattn_ln_t_b", "L1_xattn_ln_a_g", "L1_xattn_ln_a_b",
                "L1_xattn_bq", "L1_xattn_bk"]
        cols = sb("cols", [128, len(COLS)])
        C = {n: cols[:, i:i + 1] for i, n in enumerate(COLS)}
        ROWS = ["L0_xattn_bv", "L0_ffn_bo", "L0_ffn_in_c", "L1_xattn_bv", "L1_xattn_ln_p_g",
                "L1_xattn_ln_p_b"]
        rows = sb("rows", [128, len(ROWS), 128])
        R = {n: rows[:, i, :] for i, n in enumerate(ROWS)}
        gates = sb("gates", [128, 4])
        tg = sb("tg", [128, 4])
        gbias = sb("gbias", [128, NE])
        lt4 = sb("lt4", [128, 16])
        seg = sb("seg", [128, 128])
        sel = h_max[:, 0:MOE_T, :]
        xres = sb("xres", [128, HALVES, QT, D])
        pre1 = sb("pre1", [128, 2, QT, D])
        nrm = pre1[:, 1]
        avg = pre1[:, 0]
        scr = sb("scr", [128, QT, D])
        opT = sb("opT", [128, QH])
        gt = sb("gt", [128, 3, QH])
        wraw = p_f[:, 0:2, :].rearrange("p a b -> p (a b)").rearrange("p (n d) -> p n d", d=D)
        rt = gt[:, :, :].rearrange("p a b -> p (a b)")[:, 0:8 * QT * NE].rearrange("p (i t e) -> p i t e", i=8, t=QT)
        ev = gt[:, :, :].rearrange("p a b -> p (a b)")[:, 0:QT * VW].rearrange("p (t v) -> p t v", t=QT)
        junk = h_val[:, :, 0:D]
        qT = gt[:, 0, :]
        opT2 = gt[:, 2, :]
        room = sb("room", [128, 6 * QH], F16)
        pre_t = room[:, :].rearrange("p (k s t d) -> p k s t d", k=3, s=2, t=GRP)
        qg = room[:, 0:4 * QH].bitcast(F32).rearrange("p (h q) -> p h q", h=HALVES)
        qm = room[:, 4 * QH:6 * QH].rearrange("p (h q) -> p h q", h=HALVES)
        q_hi = sb("q_hi", [128, HALVES, QH], F16)
        q_lo = sb("q_lo", [128, HALVES, QH], F16)
        aug = sb("aug", [128, QH], BF16)
        mx = sb("mx", [128, QT, NG + 1])
        small = sb("small", [128, 64])
        NLN = 12
        lnst = sb("lnst", [128, QT, 6])
        lnmv = sb("lnmv", [128, NLN + 1, QT, 2])
        lnve = sb("lnve", [128, NLN, QT])
        lnrs = sb("lnrs", [128, NLN, QT])
        mhalf = sb("mhalf", [128, NT])
        ck = sb("ck", [128, 8, NT])
        mask_i = sb("mask_i", [128, NT], I32)
        bcols = sb("bcols", [128, 4])
        moe_g = c_key[:, :, 0:21, :]
        moe_u = c_key[:, :, 21:42, :]
        moe_d = c_val[:, :, :].rearrange("p t v -> p (t v)")[:, 0:2 * MOE_T * D].rearrange(
            "p (s t d) -> p s t d", s=2, t=MOE_T)
        stage = [ctx_nat[:, 0:21, :], ctx_nat[:, 21:42, :]]
        r8 = sb("r8", [128, QT, 8])
        g8 = sb("g8", [128, QT, 4, 8])
        gs = sb("gs", [128, 6, QT, 4])
        gp = sb("gp", [128, 3, QT, 16])
        coef = sb("coef", [128, QT, 64])
        cw16 = qm
        cq = sb("cq", [128, HALVES, QT])

        acc = ps("acc", [128, QT, 512])
        sco = ps("sco", [128, 2, 512])
        bk = [ps("bk6", [128, 512]), ps("bk7", [128, 512])]
        b6, b7 = bk

        block = ctx.enter_context(nc.Block())
        H = range(HALVES)
        STATIC = (4, 6, 6, 5)
        MXP = GRP * (NG + 1)
        MX1 = 3 * MXP

        def mx_count(ph, g, s, b, static):
            if ph == 0:
                return 6 * g + s + s // 2 + b if static and g < 2 else 12 + 4 * (g - 2) + s
            if static:
                return MXP * ph + 2 * (4 * g + s - 22) + b
            return MXP * ph + 4 + 8 * (g - 6) + 2 * s + b

        CHUNKS = [(0, 12), (12, 24), (24, 36), (36, 50)]
        GROUPS = [(0, 3), (3, 6), (6, 9), (9, 13)]

        @block.sync
        def _(sp):
            cm = a["ctx_1024"].rearrange("a k d -> (a k) d")
            cmain = cm[0:FULL * D, :].rearrange("(p t) d -> p t d", t=FULL)
            for c, (lo, hi) in enumerate(CHUNKS):
                sp.dma_start(ctx_nat[:, lo:hi, :], cmain[:, lo:hi, :]).then_inc(sem(f"in_c{c}"), 16)
            sp.wait_ge(sem("clr"), 1)
            sp.dma_start(ctx_nat[0:REST, FULL, :], cm[FULL * D:NK, :]).then_inc(sem("in_rest"), 16)
            mk = a["mask_BxS2_ik0"].rearrange("a k -> (a k)")
            sp.dma_start(mask_i[:, 0:FULL], mk[0:FULL * D].rearrange("(p t) -> p t", t=FULL)).then_inc(sem("in_m"), 16)
            sp.dma_start(mask_i[0:REST, FULL:NT], mk[FULL * D:NK].rearrange("(p t) -> p t", t=1)).then_inc(sem("in_m"), 16)
            for n in COLS[2:]:
                sp.dma_start(C[n], a[n].rearrange("(d o) -> d o", o=1)).then_inc(sem("in_v"), 16)
            sp.dma_start(gates[:, 0:2], a["g_xattn"].rearrange("(o d) -> o d", o=1).broadcast_to([128, 2])).then_inc(sem("in_v"), 16)
            sp.dma_start(gates[:, 2:4], a["g_ffn"].rearrange("(o d) -> o d", o=1).broadcast_to([128, 2])).then_inc(sem("in_v"), 16)
            sp.dma_start(seg[:, :], a["c_seg"]).then_inc(sem("in_k"), 16)
            sp.dma_start(lt4[:, :], a["c_lt4"]).then_inc(sem("in_k"), 16)
            sp.dma_start(cent[:, :], a["c_cent"]).then_inc(sem("in_u"), 16)
            sp.dma_start(wq1[:, :], a["L1_xattn_Wq"]).then_inc(sem("in_u"), 16)
            sp.dma_start(wv1[:, :], a["L1_xattn_Wv"]).then_inc(sem("in_u"), 16)
            for i, n in enumerate(("uf", "ui", "uc")):
                sp.dma_start(us[:, i, :], a["L0_ffn_" + n]).then_inc(sem("in_u"), 16)
            for n in ROWS:
                sp.dma_start(R[n], a[n].rearrange("(o d) -> o d", o=1).broadcast_to([128, 128])).then_inc(sem("in_u"), 16)
            sp.dma_start(gbias[:, :], a["L1_ffn_gate_bias"].rearrange("(o d) -> o d", o=1).broadcast_to([128, NE])).then_inc(sem("in_u"), 16)
            sp.wait_ge(sem("stage_clr"), 1)
            for i, (r, n, s) in enumerate((("w_gate", "anchor_w_gate", "shared_w_gate"),
                                           ("w_up", "anchor_w_up", "shared_w_up"))):
                sp.dma_start(stage[i][:, 0:16, :].rearrange("p t d -> p (t d)").rearrange("p (e i) -> p e i", e=NE),
                             a["L1_ffn_" + r].rearrange("e h i -> h e i")).then_inc(sem(f"in_w{i}"), 16)
                sp.dma_start(stage[i][:, 16:20, :].rearrange("p t d -> p (t d)").rearrange("p (e i) -> p e i", e=NA),
                             a["L1_ffn_" + n].rearrange("e h i -> h e i")).then_inc(sem(f"in_w{i}"), 16)
                sp.dma_start(stage[i][:, 20, 0:ME], a["L1_ffn_" + s]).then_inc(sem(f"in_w{i}"), 16)
            sp.wait_ge(sem("split_w"), 2)
            sp.dma_start(stage[0][:, 0:16, :], a["L1_ffn_w_down"].rearrange("(t e) i h -> (e i) t h", e=2)).then_inc(sem("in_w2"), 16)
            sp.dma_start(stage[0][:, 16:20, :], a["L1_ffn_anchor_w_down"].rearrange("(t e) i h -> (e i) t h", e=4)).then_inc(sem("in_w2"), 16)
            sp.dma_start(stage[0][0:ME, 20, :], a["L1_ffn_shared_w_down"]).then_inc(sem("in_w2"), 16)
            sp.wait_ge(sem("mx"), MX1)
            sp.dma_start(sel, a["c_sel"].rearrange("p (t d) -> p t d", t=MOE_T)).then_inc(sem("in_k"), 16)
            for h in H:
                sp.wait_ge(sem("y_out"), h + 1)
                sp.dma_start(a["out"].rearrange("a (h p t) d -> (a h) p t d", p=128, t=QT)[h], xres[:, h]).then_inc(sem("stored"), 16)
            sp.wait_ge(sem("stored"), 32)

        @block.gpsimd
        def _(pool):
            nc.gpsimd.memset(ctx_nat[:, FULL, :], 0.0)
            nc.gpsimd.memset(mask_i[:, FULL:NT], 0).then_inc(sem("clr"), 1)
            nc.gpsimd.memset(augw[:, :], PROD / 64.0)
            nc.gpsimd.memset(ones16[:, :], 1.0)
            nc.gpsimd.memset(ones[:, :], 1.0)
            nc.gpsimd.memset(c_val[:, :, C_ONE:C_ONE + 1], SPLIT).then_inc(sem("set"), 1)
            nc.gpsimd.memset(mhalf[:, :], -0.5).then_inc(sem("half"), 1)
            nc.gpsimd.memset(coef[:, :, :], 0.0).then_inc(sem("coef0"), 1)
            pool.wait_ge(sem("coef0"), 1)
            nc.gpsimd.memset(coef[:, :, 48:49], 1.0).then_inc(sem("coef1"), 1)
            pool.wait_ge(sem("half"), 1)

            def inv_root(n):
                pool.wait_ge(sem("ln_var"), n + 1)
                nc.gpsimd.tensor_tensor(lnrs[:, n, :], lnve[:, n, :], mhalf[:, 0:QT], ALU.pow).then_inc(sem("ln_inv"), 1)

            inv_root(0)
            inv_root(1)
            pool.wait_ge(sem("k_var"), 1)
            nc.gpsimd.tensor_tensor(ck[:, 2, :], ck[:, 1, :], mhalf[:, :], ALU.pow).then_inc(sem("k_inv"), 1)
            pool.wait_ge(sem("k_cols"), 1)

            def bc(i, t0, n):
                return ck[:, i, bass.ds(t0, n)].unsqueeze(2).broadcast_to([128, n, D])

            def prep(t0, n, g, s):
                x = ctx_nat[:, bass.ds(t0, n), :]
                nc.gpsimd.tensor_tensor(x, x, bc(3, t0, n), ALU.mult).then_inc(sem("pp"), 1)
                pool.wait_ge(sem("pp"), g * 2 + 1)
                nc.gpsimd.tensor_tensor(x, x, bc(4, t0, n), ALU.add).then_inc(sem("pp"), 1)
                pool.wait_ge(sem("pp"), g * 2 + 2)
                nc.gpsimd.tensor_tensor(pre1[:, s, 0:n, :], x, bc(5, t0, n), ALU.add).then_inc(sem("prep_pool"), 1)
                pool.wait_ge(sem("prep_pool"), g + 1)
                nc.gpsimd.tensor_tensor(pre_t[:, 2, s, 0:n, :], pre1[:, s, 0:n, :], bc(6, t0, n), ALU.add).then_inc(sem("prep_m"), 1)

            def pslot(g):
                pool.wait_ge(sem("prep_split"), g - 1)
                pool.wait_ge(sem("hm_done"), g - 1)
            prep(0, GRP, 0, 0)
            prep(GRP, GRP, 1, 1)
            with pool.Fori(2, NG - 1, 2) as g:
                for s in range(2):
                    pslot(g + s)
                    prep((g + s) * GRP, GRP, g + s, s)
            pslot(NG)
            prep(TAIL0, NT - TAIL0, NG, 0)
            pool.wait_ge(sem("prep_split"), NG + 1)
            nc.gpsimd.memset(ctx_nat[:, 20, ME:D], 0.0)
            nc.gpsimd.memset(ctx_nat[:, 41, ME:D], 0.0).then_inc(sem("stage_clr"), 1)
            for n in range(2, 8):
                inv_root(n)

            def split(i, dst):
                w = stage[i % 2]
                nc.gpsimd.tensor_scalar(w, w, SPLIT, 1.0, ALU.mult, ALU.mult).then_inc(sem("sw"), 1)
                pool.wait_ge(sem("sw"), 2 * i + 1)
                nc.gpsimd.tensor_copy(dst[:, 0], w).then_inc(sem("sw"), 1)
                pool.wait_ge(sem("sw"), 2 * i + 2)
                nc.gpsimd.tensor_tensor(dst[:, 1], w, dst[:, 0], ALU.subtract).then_inc(sem("split_w"), 1)

            pool.wait_ge(sem("pv_done"), 2 * NT)
            pool.wait_ge(sem("in_w0"), 48)
            split(0, moe_g)
            pool.wait_ge(sem("in_w1"), 48)
            split(1, moe_u)
            inv_root(8)
            inv_root(9)
            pool.wait_ge(sem("in_w2"), 48)
            pool.wait_ge(sem("ln_inv"), 10)
            nc.gpsimd.memset(ctx_nat[ME:D, 20, :], 0.0).then_inc(sem("dclr"), 1)
            pool.wait_ge(sem("dclr"), 1)
            split(2, moe_d)

            def low(h, t, s):
                pool.wait_ge(sem("hid_hi"), MOE_T * h + t + 1)
                nc.gpsimd.tensor_tensor(p_lo[:, s, :], p_f[:, 2 + s, :], p_hi[:, s, :], ALU.subtract).then_inc(sem("hid_lo"), 1)
            for t in range(MOE_T):
                if t == 5:
                    inv_root(10)
                if t == 8:
                    inv_root(11)
                low(0, t, t % 2)
            with pool.Fori(0, MOE_T - 2, 2) as t:
                low(1, t, 0)
                low(1, t + 1, 1)
            low(1, MOE_T - 1, 0)

        @block.scalar
        def _(act):
            xv = a["x"].rearrange("a (h p t) d -> (a h) p t d", p=128, t=QT)
            act.dma_start(xres[:, 0], xv[0]).then_inc(sem("in_x"), 16)
            act.dma_start(ident[:, :], a["c_ident"]).then_inc(sem("in_id"), 16)
            act.dma_start(wraw[:, 0, :], a[WNAMES[0]]).then_inc(sem("in_q"), 16)
            act.dma_start(wk0[:, :], a["L0_xattn_Wk"]).then_inc(sem("in_q"), 16)
            for n in COLS[:2]:
                act.dma_start(C[n], a[n].rearrange("(d o) -> d o", o=1)).then_inc(sem("in_b"), 16)
            act.wait_ge(sem("in_id"), 16)
            nc.scalar.copy(ident16[:, :], ident[:, :]).then_inc(sem("id16"), 1)
            act.wait_ge(sem("wq_ps"), 1)
            nc.scalar.copy(W[WNAMES[0]], b7[:, 0:D]).then_inc(sem("wq_sb"), 1)
            for i, n in list(enumerate(WNAMES))[1:]:
                act.dma_start(wraw[:, i, :], a[n]).then_inc(sem("in_w"), 16)
            act.dma_start(gw[:, :], a["L1_ffn_gate_weight"]).then_inc(sem("in_w"), 16)
            act.dma_start(xres[:, 1], xv[1]).then_inc(sem("in_x1"), 16)

            def high(c):
                lo, hi = CHUNKS[c]
                act.wait_ge(sem(f"in_c{c}"), 16)
                if c == 3:
                    act.wait_ge(sem("in_rest"), 16)
                    nc.scalar.mul(c_val[:, FULL, C_F:C_F + D], ctx_nat[:, FULL, :], SPLIT)
                nc.scalar.mul(c_val[:, lo:hi, C_F:C_F + D], ctx_nat[:, lo:hi, :], SPLIT).then_inc(sem("c_hi"), 1)

            def turned(c):
                for g in range(*GROUPS[c]):
                    n = min(GRP, NT - g * GRP)
                    act.wait_ge(sem("ct_ps"), g + 1)
                    nc.scalar.copy(c_key[:, :, g * GRP:g * GRP + n, :].rearrange("p s t d -> p s (t d)"),
                                   sco[:, g % 2, :].bitcast(F16).rearrange("p (s w) -> p s w", s=2)[:, :, 0:n * D]).then_inc(sem("ct_out"), 1)

            def spread(c):
                lo, hi = CHUNKS[c]
                act.wait_ge(sem("mean"), c + 1)
                for t in range(lo, NT if c == 3 else hi):
                    last = nc.scalar.activation(junk[:, t, :], ctx_nat[:, t, :], ACT.Square, bias=ck[:, 0, t:t + 1],
                                                accum_out=ck[:, 1, t:t + 1])
                last.then_inc(sem("spread"), 1)

            def query0(h, part):
                if part == 0:
                    act.wait_ge(sem("t0"), h + 1)
                    nc.scalar.copy(opT[:, :], b6[:, :]).then_inc(sem("t0_sb"), 1)
                    act.wait_ge(sem("q0"), h + 1)
                    nc.scalar.activation(qT[:, :], b7[:, :], ACT.Identity, bias=C["L0_xattn_bq"]).then_inc(sem("q0_sb"), 1)
                else:
                    act.wait_ge(sem("k0"), h + 1)
                    nc.scalar.mul(q_hi[:, h, :], b6[:, :], SPLIT).then_inc(sem("q_hi"), 1)

            high(0)
            act.wait_ge(sem("in_b"), 32)
            query0(0, 0)
            high(1)
            query0(0, 1)
            turned(0)
            act.wait_ge(sem("wT_ps"), 1)
            nc.scalar.copy(wT[:, 1:8, :].rearrange("p a b -> p (a b)")[:, 0:512], acc[:, 0, :])
            nc.scalar.copy(wT[:, 1:8, :].rearrange("p a b -> p (a b)")[:, 512:896], acc[:, 1, 0:384])
            nc.scalar.copy(gwT[:, :], acc[:, 2, 0:NE]).then_inc(sem("wT"), 1)
            high(2)
            turned(1)
            spread(0)
            high(3)
            turned(2)
            spread(1)
            turned(3)
            spread(2)
            spread(3)
            act.wait_ge(sem("in_v"), 16 * len(COLS))
            nc.scalar.activation(tg[:, :], gates[:, :], ACT.Tanh).then_inc(sem("tg"), 1)
            query0(1, 0)
            query0(1, 1)

            def shift(ph):
                if ph < 2:
                    act.wait_ge(sem("m_ps"), ph + 1)
                    nc.scalar.copy(aug[:, :], b6[:, :]).then_inc(sem("aug_hi"), 1)
                else:
                    act.wait_ge(sem("g1"), ph - 1)
                    nc.scalar.mul(q_hi[:, ph % 2, :], opT[:, :], SPLIT).then_inc(sem("q_hi"), 1)

            def evict(ph):
                act.wait_ge(sem("pv_done"), NT * (ph + 1))
                for q in range(2):
                    last = nc.scalar.copy(ev[:, q, :], acc[:, q, 0:VW])
                last.then_inc(sem("ev_a"), 1)

            def mid(h, i):
                if i == 2:
                    act.wait_ge(sem("avT"), h + 1)
                    nc.scalar.copy(opT[:, :], b7[:, :]).then_inc(sem("avT_sb"), 1)
                elif i == 6:
                    act.wait_ge(sem("nT"), h + 1)
                    nc.scalar.copy(opT[:, :], b6[:, :]).then_inc(sem("nT_sb"), 1)
                elif i == 7:
                    gate(h, 0)
                    gate(h, 1)
                elif i == 8:
                    gate(h, 2)
                elif i == 11:
                    act.wait_ge(sem("f_sum"), h + 1)
                    nc.scalar.activation(avg[:, :, :], scr[:, :, :], ACT.Tanh).then_inc(sem("f_tanh"), 1)
                elif i == 17:
                    act.wait_ge(sem("q1"), h + 1)
                    nc.scalar.activation(qT[:, :], b7[:, :], ACT.Identity, bias=C["L1_xattn_bq"]).then_inc(sem("q1_sb"), 1)
                elif i == 21:
                    act.wait_ge(sem("qc_sb"), h + 1)
                    nc.scalar.activation(qm[:, h, :], qg[:, h, :], ACT.Copy, scale=SPLIT, bias=SPLIT).then_inc(sem("qm"), 1)

            def gate(h, i):
                act.wait_ge(sem("gate_ps"), 3 * h + i + 1)
                nc.scalar.activation(gt[:, i, :], bk[(i + 1) % 2][:, :], ACT.Tanh, bias=bcols[:, i:i + 1],
                                     scale=0.5 if i < 2 else 1.0).then_inc(sem("gate"), 1)

            def post(h, i):
                if i == 10:
                    act.wait_ge(sem("n3T"), h + 1)
                    nc.scalar.copy(opT[:, :], b6[:, :]).then_inc(sem("n3T_sb"), 1)
                    nc.scalar.mul(q_hi[:, h, :], b6[:, :], SPLIT).then_inc(sem("x3_hi"), 1)
                elif i == 12:
                    act.wait_ge(sem("lg"), h + 1)
                    nc.scalar.activation(rt[:, 0, :, :].rearrange("p a b -> p (a b)"), b6[:, 0:QT * NE], ACT.Tanh, scale=0.5).then_inc(sem("lg_t"), 1)
                elif i == 18:
                    act.wait_ge(sem("cwT"), h + 1)
                    nc.scalar.mul(cw16[0:64, h, :], b6[0:64, :], CW_SCALE).then_inc(sem("cw_hi"), 1)

            def exps(ph, t, s, n=D, first=False):
                c = NT * ph + t
                act.wait_ge(sem("scores"), c + 1)
                if not first:
                    act.wait_ge(sem("pv_done"), c - 2)
                nc.scalar.activation(p_hi[0:n, s, :], sco[0:n, s % 2, :], ACT.Exp, scale=ATT_SCALE / PROD)
                nc.scalar.activation(p_f[0:n, s, :], sco[0:n, s % 2, :], ACT.Exp, scale=ATT_SCALE / PROD).then_inc(sem("exps"), 1)

            def prep_split(g, t0, n, s, first=False):
                act.wait_ge(sem("prep_pool"), g + 1)
                if not first:
                    act.wait_ge(sem("ht_m"), g - 1)
                nc.scalar.copy(h_val[:, bass.ds(t0, n), C_F:C_F + D], ctx_nat[:, bass.ds(t0, n), :])
                nc.scalar.copy(pre_t[:, 0, s, 0:n, :], pre1[:, s, 0:n, :]).then_inc(sem("h_hi"), 1)

            def prep_out(g, t0, n):
                act.wait_ge(sem("ht_ps"), g + 1)
                nc.scalar.copy(h_key[:, :, bass.ds(t0, n), :].rearrange("p s t d -> p s (t d)"),
                               b7[:, :].bitcast(F16).rearrange("p (s w) -> p s w", s=2)[:, :, 0:n * D]).then_inc(sem("ht_out"), 1)

            def main(ph):
                pr = ph == 0

                def trip(g, slot, static):
                    for s in range(GRP):
                        exps(ph, g * GRP + s, s, first=static and ph == 0 and g == 0 and s < 3)
                        if static and ph in (1, 2):
                            mid(ph - 1, g * GRP + s)
                            if ph == 1 and g * GRP + s == 12:
                                prep_out(NG, TAIL0, NT - TAIL0)
                        if static and ph == 3:
                            post(0, g * GRP + s)
                        if pr and s == 0 and not (static and g == 0):
                            prep_split(g - 1, (g - 1) * GRP, GRP, slot, first=static and g <= 2)
                        if pr and s == 3 and not (static and g == 0):
                            prep_out(g - 1, (g - 1) * GRP, GRP)
                for g in range(STATIC[ph]):
                    trip(g, (g + 1) % 2, True)
                if pr:
                    with act.Fori(STATIC[ph], NG - 1, 2) as g:
                        trip(g, 1, False)
                        trip(g + 1, 0, False)
                else:
                    with act.Fori(STATIC[ph], NG) as g:
                        trip(g, None, False)
                exps(ph, TAIL0, 0)
                if pr:
                    prep_split(NG - 1, TAIL0 - GRP, GRP, 1)
                exps(ph, TAIL0 + 1, 1)
                exps(ph, TAIL0 + 2, 2, REST)
                if pr:
                    prep_out(NG - 1, TAIL0 - GRP, GRP)
                if ph < 3:
                    shift(ph + 1)
                evict(ph)
                if pr:
                    prep_split(NG, TAIL0, NT - TAIL0, 0)

            def moe(h):
                def silu(t, s, first=False):
                    c = MOE_T * h + t
                    act.wait_ge(sem("gu"), c + 1)
                    if not first:
                        act.wait_ge(sem("t2"), c - 1)
                    elif h:
                        act.wait_ge(sem("t2"), MOE_T * h)
                    nc.scalar.activation(p_f[:, s, :], acc[:, s, :], ACT.Silu, scale=1.0 / PROD).then_inc(sem("silu"), 1)

                def high(t, s, first=False):
                    c = MOE_T * h + t
                    act.wait_ge(sem("t2"), c + 1)
                    if not first:
                        act.wait_ge(sem("down"), c - 1)
                    elif h:
                        act.wait_ge(sem("down"), MOE_T * h)
                    nc.scalar.copy(p_hi[:, s, :], p_f[:, 2 + s, :]).then_inc(sem("hid_hi"), 1)
                silu(0, 0, True)
                if h == 0:
                    for t in range(1, MOE_T):
                        silu(t, t % 2, t < 2)
                        high(t - 1, (t - 1) % 2, t <= 2)
                        post(1, t - 1)
                else:
                    silu(1, 1, True)
                    high(0, 0, True)
                    silu(2, 0)
                    high(1, 1, True)
                    with act.Fori(2, MOE_T - 2, 2) as t:
                        silu(t + 1, 1)
                        high(t, 0)
                        silu(t + 2, 0)
                        high(t + 1, 1)
                high(MOE_T - 1, 0)
                act.wait_ge(sem("down"), MOE_T * h + MOE_T)
                nc.scalar.mul(opT[:, :], b7[:, :], 1.0 / (HID_SCALE * SPLIT)).then_inc(sem("yT"), 1)

            shift(0)
            for ph in range(4):
                main(ph)
            moe(0)
            moe(1)

        @block.vector
        def _(dve):
            chain = [0]
            V = nc.vector

            def link(ins):
                chain[0] += 1
                ins.then_inc(sem("v_chain"), 1)
                dve.wait_ge(sem("v_chain"), chain[0])

            def norm(n, src, dst, done):
                for q in range(QT):
                    last = V.bn_stats(lnst[:, q, :], src[:, q, :])
                link(last)
                for q in range(QT):
                    last = V.bn_aggr(lnmv[:, n, q, :], lnst[:, q, :])
                link(last)
                V.tensor_scalar(lnve[:, n, :], lnmv[:, n, :, 1], LN_EPS, None, ALU.add).then_inc(sem("ln_var"), 1)
                dve.wait_ge(sem("ln_inv"), n + 1)
                for q in range(QT):
                    last = V.tensor_scalar(dst[:, q, :], src[:, q, :], lnmv[:, n, q, 0:1], lnrs[:, n, q:q + 1],
                                           ALU.subtract, ALU.mult)
                if done:
                    last.then_inc(sem(done), 1)
                else:
                    link(last)

            def over(v, n=QT):
                return v.unsqueeze(1).broadcast_to([128, n, v.shape[1]])

            def low(c):
                lo, hi = CHUNKS[c]
                dve.wait_ge(sem("c_hi"), c + 1)
                V.scalar_tensor_tensor(c_val[:, lo:hi, C_L:C_L + D], ctx_nat[:, lo:hi, :], SPLIT,
                                       c_val[:, lo:hi, C_F:C_F + D], ALU.mult, ALU.subtract).then_inc(sem("c_lo"), 1)
                if c == 3:
                    V.scalar_tensor_tensor(c_val[:, FULL, C_L:C_L + D], ctx_nat[:, FULL, :], SPLIT,
                                           c_val[:, FULL, C_F:C_F + D], ALU.mult, ALU.subtract).then_inc(sem("c_lo"), 1)

            def mean(c):
                lo, hi = CHUNKS[c]
                hi = NT if c == 3 else hi
                dve.wait_ge(sem("sum_ps"), c + 1)
                V.tensor_scalar(ck[:, 0, lo:hi], b6[:, lo:hi], -1.0 / (D * SPLIT), None, ALU.mult).then_inc(sem("mean"), 1)

            def query0(h):
                dve.wait_ge(sem("c0"), h + 1)
                V.tensor_copy(cq[:, h, :], b7[:, 0:QT]).then_inc(sem("cq"), 1)
                dve.wait_ge(sem("q_hi"), h + 1)
                V.scalar_tensor_tensor(q_lo[:, h, :], b6[:, :], SPLIT, q_hi[:, h, :], ALU.mult, ALU.subtract).then_inc(sem("q_lo"), 1)

            def first_max(c):
                for g in range(*GROUPS[c]):
                    n = 512 if g < NG else TAILW
                    for j in range(2):
                        dve.wait_ge(sem("mf_ps"), 2 * g + j + 1)
                        V.reduce_max(mx[:, 2 * j:2 * j + 2, g], acc[:, 2 * j:2 * j + 2, 0:n], axis=AX.X).then_inc(sem("mf"), 1)

            dve.wait_ge(sem("in_x"), 16)
            norm(0, xres[:, 0], nrm, "n0")
            low(0)
            low(1)
            query0(0)
            mean(0)
            first_max(0)
            mean(1)
            low(2)
            low(3)
            first_max(1)
            mean(2)
            mean(3)
            dve.wait_ge(sem("in_x1"), 16)
            norm(1, xres[:, 1], nrm, "n0")
            dve.wait_ge(sem("in_m"), 32)
            link(V.tensor_scalar(ck[:, 5, :], mask_i[:, :], 0.0, None, ALU.not_equal))
            V.reduce_max(small[:, 8:9], ck[:, 5, :], axis=AX.X).then_inc(sem("any"), 1)
            first_max(2)
            query0(1)
            dve.wait_ge(sem("any_ps"), 1)
            link(V.tensor_scalar(small[:, 9:10], b7[:, 4:5], 1.0, None, ALU.min))
            link(V.tensor_scalar(small[:, 10:11], small[:, 9:10], -1.0, 1.0, ALU.mult, ALU.add))
            link(V.tensor_scalar(ck[:, 5, :], ck[:, 5, :], small[:, 10:11], None, ALU.max))
            V.tensor_scalar(ck[:, 6, :], ck[:, 5, :], 1.0, PEN, ALU.subtract, ALU.mult)
            link(V.tensor_scalar(ck[:, 5, :], ck[:, 5, :], SPLIT, None, ALU.mult))
            V.tensor_copy(h_val[:, :, C_ONE], ck[:, 5, :])
            dve.wait_ge(sem("spread"), 4)
            V.tensor_scalar(ck[:, 1, :], ck[:, 1, :], 1.0 / D, LN_EPS, ALU.mult, ALU.add).then_inc(sem("k_var"), 1)
            first_max(3)
            dve.wait_ge(sem("k_inv"), 1)
            link(V.tensor_tensor(ck[:, 3, :], ck[:, 2, :], ck[:, 5, :], ALU.mult))
            V.tensor_tensor(ck[:, 4, :], ck[:, 0, :], ck[:, 3, :], ALU.mult).then_inc(sem("k_cols"), 1)

            def consts():
                dve.wait_ge(sem("in_u"), 16 * 13)
                dve.wait_ge(sem("tg"), 1)
                link(V.tensor_tensor(scr[:, 0:3, :], us[:, :, :], over(R["L0_ffn_in_c"], 3), ALU.mult))
                link(V.reduce_sum(bcols[:, 0:3], scr[:, 0:3, :], axis=AX.X))
                link(V.tensor_tensor(bcols[:, 0:3], bcols[:, 0:3], cols[:, 2:5], ALU.add))
                V.tensor_scalar(bcols[:, 3:4], C["L0_ffn_in_c"], 0.5, None, ALU.mult)
                link(V.tensor_scalar(bcols[:, 0:2], bcols[:, 0:2], 0.5, None, ALU.mult))
                for h in H:
                    V.scalar_tensor_tensor(xres[:, h], over(R["L0_xattn_bv"]), tg[:, 0:1], xres[:, h], ALU.mult, ALU.add).then_inc(sem("consts"), 1)

            def low_p(ph, t, s, n=D):
                c = NT * ph + t
                dve.wait_ge(sem("exps"), c + 1)
                V.tensor_tensor(p_lo[0:n, s, :], p_f[0:n, s, :], p_hi[0:n, s, :], ALU.subtract).then_inc(sem("p_low"), 1)

            def max_g(c, g, j, bank, n=512):
                dve.wait_ge(sem("mx_ps"), c + 1)
                V.reduce_max(mx[:, j, bass.ds(g, 1)], bank[:, 0:n], axis=AX.X).then_inc(sem("mx"), 1)

            def prep_low(g, t0, n, s):
                dve.wait_ge(sem("h_hi"), g + 1)
                V.tensor_tensor(h_val[:, bass.ds(t0, n), C_L:C_L + D], ctx_nat[:, bass.ds(t0, n), :],
                                h_val[:, bass.ds(t0, n), C_F:C_F + D], ALU.subtract)
                V.tensor_tensor(pre_t[:, 1, s, 0:n, :], pre1[:, s, 0:n, :], pre_t[:, 0, s, 0:n, :],
                                ALU.subtract).then_inc(sem("prep_split"), 1)

            def hm_out(g, t0, n):
                dve.wait_ge(sem("ht_m"), g + 1)
                V.tensor_copy(h_max[:, bass.ds(t0, n), :].rearrange("p t d -> p (t d)"),
                              b7[:, :].bitcast(F16)[:, 0:n * D]).then_inc(sem("hm_done"), 1)

            def main(ph):
                pr = ph == 0

                def trip(g, slot, static):
                    for s in range(GRP):
                        i = g * GRP + s
                        low_p(ph, i, s)
                        if pr:
                            max_g(mx_count(ph, g, s, 0, static), g, s, b6)
                            if static and g < 2 and s % 2:
                                max_g(mx_count(ph, g, s, 1, static), NG, 2 * g + s // 2, b6, TAILW)
                            if s == 1 and not (static and g <= 1):
                                hm_out(g - 2, (g - 2) * GRP, GRP)
                            if s == 1 and not (static and g == 0):
                                prep_low(g - 1, (g - 1) * GRP, GRP, slot)
                        elif ph < 3:
                            if static and i < 22:
                                mid(ph - 1, i)
                                if ph == 1 and i == 14:
                                    hm_out(NG, TAIL0, NT - TAIL0)
                            elif static:
                                for b in range(2):
                                    max_g(mx_count(ph, g, s, b, static), NG, 2 * (i - 22) + b, bk[b], TAILW)
                            else:
                                for b in range(2):
                                    max_g(mx_count(ph, g, s, b, static), 2 * (g - 6) + s // 2, 2 * (s % 2) + b, bk[b])
                        elif static:
                            post(0, i)
                for g in range(STATIC[ph]):
                    trip(g, (g + 1) % 2, True)
                if pr:
                    with dve.Fori(STATIC[ph], NG - 1, 2) as g:
                        trip(g, 1, False)
                        trip(g + 1, 0, False)
                else:
                    with dve.Fori(STATIC[ph], NG) as g:
                        trip(g, None, False)
                low_p(ph, TAIL0, 0)
                if pr:
                    hm_out(NG - 2, (NG - 2) * GRP, GRP)
                    prep_low(NG - 1, TAIL0 - GRP, GRP, 1)
                if ph < 3:
                    shift(ph + 1, 0)
                low_p(ph, TAIL0 + 1, 1)
                low_p(ph, TAIL0 + 2, 2, REST)
                if ph < 3:
                    shift(ph + 1, 1)
                evict(ph)
                if pr:
                    hm_out(NG - 1, TAIL0 - GRP, GRP)
                    prep_low(NG, TAIL0, NT - TAIL0, 0)

            def shift(ph, part):
                h, L = ph % 2, ph // 2
                if part == 0:
                    if ph:
                        dve.wait_ge(sem("mx"), 4 * (NG + 1) * ph)
                    else:
                        dve.wait_ge(sem("mf"), 2 * (NG + 1))
                    link(V.reduce_max(small[:, 0:4], mx[:, :, :], axis=AX.X))
                    if L:
                        link(V.tensor_scalar(small[:, 0:4], small[:, 0:4], 1.0 / PROD, -float(D), ALU.mult, ALU.add))
                        link(V.scalar_tensor_tensor(small[:, 0:4], small[:, 0:4], small[:, 9:10], cq[:, h, :], ALU.mult, ALU.add))
                    else:
                        link(V.scalar_tensor_tensor(small[:, 0:4], small[:, 0:4], 1.0 / PROD, cq[:, h, :], ALU.mult, ALU.add))
                    link(V.tensor_tensor(small[:, 4:8], cq[:, h, :], small[:, 0:4], ALU.subtract))
                    link(V.tensor_scalar(small[:, 4:8], small[:, 4:8], P_LOG, 1.0 / D if L else 1.0, ALU.add, ALU.mult))
                    for q in range(QT):
                        last = V.tensor_scalar(scr[:, q, :], ident[:, :], small[:, 4 + q:5 + q], None, ALU.mult)
                    last.then_inc(sem("dg"), 1)
                elif L:
                    dve.wait_ge(sem("m_ps"), ph + 1)
                    V.tensor_tensor(opT[:, :], b6[:, :], qg[:, h, :], ALU.add).then_inc(sem("g1"), 1)
                    dve.wait_ge(sem("q_hi"), ph + 1)
                    V.scalar_tensor_tensor(q_lo[:, h, :], opT[:, :], SPLIT, q_hi[:, h, :], ALU.mult, ALU.subtract).then_inc(sem("q_lo"), 1)
                else:
                    dve.wait_ge(sem("aug_hi"), ph + 1)
                    V.tensor_tensor(aug[64:128, :], b6[64:128, :], aug[64:128, :], ALU.subtract).then_inc(sem("aug"), 1)

            def evict(ph):
                dve.wait_ge(sem("pv_done"), NT * (ph + 1))
                for q in range(2, QT):
                    last = V.tensor_copy(ev[:, q, :], acc[:, q, 0:VW])
                last.then_inc(sem("ev_v"), 1)

            def average(ph):
                dve.wait_ge(sem("ev_a"), ph + 1)
                dve.wait_ge(sem("ev_v"), ph + 1)
                if ph == 0:
                    dve.wait_ge(sem("prep_m"), NG + 1)
                    dve.wait_ge(sem("prep_split"), NG + 1)
                V.reciprocal(small[:, 0:4], ev[:, :, C_ONE])
                link(V.tensor_tensor(avg[:, :, :], ev[:, :, C_F:C_F + D], ev[:, :, C_L:C_L + D], ALU.add))
                V.tensor_tensor(avg[:, :, :], avg[:, :, :], small[:, 0:4].unsqueeze(2).broadcast_to([128, QT, D]),
                                ALU.mult).then_inc(sem("av_done"), 1)

            def norm_a(n, src):
                for q in range(QT):
                    last = V.bn_stats(lnst[:, q, :], src[:, q, :])
                link(last)
                for q in range(QT):
                    last = V.bn_aggr(lnmv[:, n, q, :], lnst[:, q, :])
                link(last)
                V.tensor_scalar(lnve[:, n, :], lnmv[:, n, :, 1], LN_EPS, None, ALU.add).then_inc(sem("ln_var"), 1)

            def norm_b(n, src, dst, done=None):
                dve.wait_ge(sem("ln_inv"), n + 1)
                for q in range(QT):
                    last = V.tensor_scalar(dst[:, q, :], src[:, q, :], lnmv[:, n, q, 0:1], lnrs[:, n, q:q + 1],
                                           ALU.subtract, ALU.mult)
                if done:
                    last.then_inc(sem(done), 1)
                else:
                    link(last)

            def rows_of(bank):
                return bank[:, :].rearrange("p (t d) -> p t d", t=QT)

            def mid(h, i):
                if i == 0:
                    average(h)
                    if h == 0:
                        consts()
                elif i == 3:
                    dve.wait_ge(sem("o_ps"), h + 1)
                    link(V.scalar_tensor_tensor(xres[:, h], rows_of(b6), tg[:, 0:1], xres[:, h], ALU.mult, ALU.add))
                    norm_a(2 + 3 * h, xres[:, h])
                elif i == 4:
                    norm_b(2 + 3 * h, xres[:, h], nrm, "n1")
                elif i == 8:
                    dve.wait_ge(sem("gate"), 3 * h + 3)
                    link(V.tensor_scalar(gt[:, 0, :], gt[:, 0, :], 1.0, bcols[:, 3:4], ALU.add, ALU.mult))
                    link(V.scalar_tensor_tensor(gt[:, 1, :], gt[:, 1, :], 1.0, gt[:, 2, :], ALU.add, ALU.mult))
                    V.scalar_tensor_tensor(opT2[:, :], gt[:, 1, :], 0.5, gt[:, 0, :], ALU.mult, ALU.add).then_inc(sem("cell"), 1)
                elif i == 10:
                    dve.wait_ge(sem("ffn_ps"), h + 1)
                    V.tensor_tensor(scr[:, :, :], rows_of(b6), over(R["L0_ffn_bo"]), ALU.add).then_inc(sem("f_sum"), 1)
                elif i == 11:
                    dve.wait_ge(sem("f_tanh"), h + 1)
                    link(V.scalar_tensor_tensor(xres[:, h], avg[:, :, :], tg[:, 2:3], xres[:, h], ALU.mult, ALU.add))
                    norm_a(3 + 3 * h, xres[:, h])
                elif i == 12:
                    norm_b(3 + 3 * h, xres[:, h], nrm)
                    norm_a(4 + 3 * h, nrm)
                elif i == 13:
                    norm_b(4 + 3 * h, nrm, avg, "n2")
                elif i == 15:
                    dve.wait_ge(sem("tT"), h + 1)
                    V.tensor_scalar(opT[:, :], b6[:, :], C["L1_xattn_ln_t_g"], C["L1_xattn_ln_t_b"], ALU.mult, ALU.add).then_inc(sem("tT_sb"), 1)
                elif i == 18:
                    dve.wait_ge(sem("g0"), h + 1)
                    V.tensor_copy(opT[:, :], b6[:, :])
                    V.tensor_scalar(opT2[:, :], b6[:, :], C["L1_xattn_ln_a_g"], None, ALU.mult).then_inc(sem("g0_sb"), 1)
                elif i == 20:
                    dve.wait_ge(sem("qc"), h + 1)
                    V.tensor_copy(cq[:, h, :], b7[:, 0:QT])
                    V.tensor_scalar(qg[:, h, :], b6[:, :], small[:, 9:10], None, ALU.mult).then_inc(sem("qc_sb"), 1)

            def post(h, i):
                if i == 0:
                    average(2 + h)
                elif i == 2:
                    dve.wait_ge(sem("av1T"), h + 1)
                    V.tensor_scalar(opT[:, :], b6[:, :], C["L1_xattn_ln_a_g"], C["L1_xattn_ln_a_b"], ALU.mult, ALU.add).then_inc(sem("av1T_sb"), 1)
                elif i == 4:
                    dve.wait_ge(sem("o1_ps"), h + 1)
                    link(V.tensor_tensor(scr[:, :, :], rows_of(b6), over(R["L1_xattn_bv"]), ALU.add))
                    norm_a(8 + 2 * h, scr)
                elif i == 5:
                    norm_b(8 + 2 * h, scr, nrm)
                    link(V.tensor_tensor(nrm[:, :, :], nrm[:, :, :], over(R["L1_xattn_ln_p_g"]), ALU.mult))
                elif i == 6:
                    link(V.tensor_tensor(nrm[:, :, :], nrm[:, :, :], over(R["L1_xattn_ln_p_b"]), ALU.add))
                    link(V.scalar_tensor_tensor(xres[:, h], nrm[:, :, :], tg[:, 1:2], xres[:, h], ALU.mult, ALU.add))
                elif i == 7:
                    norm_a(9 + 2 * h, xres[:, h])
                elif i == 8:
                    norm_b(9 + 2 * h, xres[:, h], nrm, "n3")
                elif i == 11:
                    dve.wait_ge(sem("x3_hi"), h + 1)
                    V.scalar_tensor_tensor(q_lo[:, h, :], opT[:, :], SPLIT, q_hi[:, h, :], ALU.mult, ALU.subtract).then_inc(sem("x3_lo"), 1)
                elif 13 <= i <= 16:
                    route(h, i - 13)
                elif i == 18:
                    dve.wait_ge(sem("cw_hi"), h + 1)
                    V.scalar_tensor_tensor(cw16[64:128, h, :], b6[0:64, :], CW_SCALE, cw16[0:64, h, :], ALU.mult, ALU.subtract).then_inc(sem("cw_lo"), 1)

            def wide(v, n):
                return v.unsqueeze(3).broadcast_to([128, QT, v.shape[2], n])

            def route(h, part):
                sc, sb_, m, gtv, eq, pre, pick, top = (rt[:, i, :, :] for i in range(8))

                def nth(i):
                    return r8[:, :, i:i + 1].broadcast_to([128, QT, NE])

                def place(eqv, out):
                    link(V.tensor_tensor_scan(out.rearrange("p t e -> p (t e)"), seg[:, :],
                                              eqv.rearrange("p t e -> p (t e)"), 0.0, ALU.mult, ALU.add))
                if part == 0:
                    dve.wait_ge(sem("lg_t"), h + 1)
                    link(V.tensor_scalar(sc, sc, 0.5, 0.5, ALU.mult, ALU.add))
                    link(V.tensor_tensor(sb_, sc, over(gbias[:, :]), ALU.add))
                    for q in range(QT):
                        for g in range(4):
                            last = V.max(g8[:, q, g, :], rt[:, 1, q, 8 * g:8 * g + 8])
                    link(last)
                    link(V.tensor_tensor(gs[:, 0], g8[:, :, :, 0], g8[:, :, :, 1], ALU.add))
                elif part == 1:
                    mine = gs[:, 0].unsqueeze(3).broadcast_to([128, QT, 4, 4])
                    other = gs[:, 0].unsqueeze(2).broadcast_to([128, QT, 4, 4])

                    def v4(i):
                        return gp[:, i].rearrange("p t (i j) -> p t i j", i=4)
                    V.tensor_tensor(v4(0), other, mine, ALU.is_gt)
                    link(V.tensor_tensor(v4(1), other, mine, ALU.is_equal))
                    link(V.tensor_tensor(gp[:, 1], gp[:, 1], over(lt4[:, :]), ALU.mult))
                    link(V.tensor_tensor(gp[:, 0], gp[:, 0], gp[:, 1], ALU.add))
                    link(V.reduce_sum(gs[:, 1], v4(0), axis=AX.X))
                    link(V.tensor_scalar(gs[:, 2], gs[:, 1], 1.5, None, ALU.is_lt))
                    link(V.tensor_scalar(gs[:, 3], gs[:, 2], 1.0, 1e30, ALU.subtract, ALU.mult))
                    link(V.tensor_tensor(m.rearrange("p t (g e) -> p t g e", g=4), sb_.rearrange("p t (g e) -> p t g e", g=4),
                                         wide(gs[:, 3], 8), ALU.add))
                    for q in range(QT):
                        last = V.max(r8[:, q, :], rt[:, 2, q, :])
                    link(last)

                elif part == 2:
                    V.tensor_tensor(gtv, m, nth(TOPK - 1), ALU.is_gt)
                    V.tensor_tensor(top, m, nth(0), ALU.is_equal)
                    link(V.tensor_tensor(eq, m, nth(TOPK - 1), ALU.is_equal))
                    link(V.reduce_sum(gs[:, 4, :, 0], gtv, axis=AX.X))
                    place(eq, pre)
                    link(V.tensor_tensor(pre, pre, gs[:, 4, :, 0:1].broadcast_to([128, QT, NE]), ALU.add))
                    link(V.scalar_tensor_tensor(pre, pre, TOPK + 0.5, eq, ALU.is_lt, ALU.mult))
                    link(V.tensor_tensor(pick, gtv, pre, ALU.add))
                else:
                    link(V.tensor_tensor(pick, pick, sc, ALU.mult))
                    link(V.reduce_sum(gs[:, 5, :, 0], pick, axis=AX.X))
                    link(V.tensor_scalar(gs[:, 5, :, 0], gs[:, 5, :, 0], 1e-20, None, ALU.add))
                    link(V.reciprocal(gs[:, 5, :, 1], gs[:, 5, :, 0]))
                    link(V.tensor_scalar(gs[:, 5, :, 1], gs[:, 5, :, 1], ROUTED_SCALE, None, ALU.mult))
                    if h == 0:
                        dve.wait_ge(sem("coef1"), 1)
                    V.tensor_tensor(coef[:, :, 0:NE], pick, gs[:, 5, :, 1:2].broadcast_to([128, QT, NE]), ALU.mult)
                    place(top, pre)
                    link(V.scalar_tensor_tensor(pre, pre, 1.5, top, ALU.is_lt, ALU.mult))
                    pairs = pre.rearrange("p t (a b) -> p t a b", b=2)
                    link(V.tensor_tensor(coef[:, :, NE:NE + NA], pairs[:, :, :, 0], pairs[:, :, :, 1], ALU.add))
                    V.tensor_scalar(coef[:, :, NE:NE + NA], coef[:, :, NE:NE + NA], ANCHOR_ALPHA, None, ALU.mult).then_inc(sem("coef"), 1)

            def moe(h):
                def t1(t, s):
                    dve.wait_ge(sem("silu"), MOE_T * h + t + 1)
                    V.scalar_tensor_tensor(p_f[:, s, :], acc[:, 2 + s, :], HID_SCALE / (PROD * CW_SCALE), p_f[:, s, :],
                                           ALU.mult, ALU.mult).then_inc(sem("t1"), 1)

                def t2(t, s, first=False):
                    dve.wait_ge(sem("t1"), MOE_T * h + t + 1)
                    if not first:
                        dve.wait_ge(sem("hid_lo"), MOE_T * h + t - 1)
                    elif h:
                        dve.wait_ge(sem("hid_lo"), MOE_T * h)
                    V.tensor_tensor(p_f[:, 2 + s, :], sco[:, s, :], p_f[:, s, :], ALU.mult).then_inc(sem("t2"), 1)
                if h == 0:
                    for t in range(MOE_T):
                        t1(t, t % 2)
                        t2(t, t % 2, t < 2)
                        post(1, t)
                else:
                    for t in range(2):
                        t1(t, t)
                        t2(t, t, True)
                    with dve.Fori(2, MOE_T - 2, 2) as t:
                        t1(t, 0)
                        t2(t, 0)
                        t1(t + 1, 1)
                        t2(t + 1, 1)
                    t1(MOE_T - 1, 0)
                    t2(MOE_T - 1, 0)
                dve.wait_ge(sem("y_ps"), h + 1)
                V.scalar_tensor_tensor(xres[:, h], rows_of(b6), tg[:, 3:4], xres[:, h], ALU.mult, ALU.add).then_inc(sem("y_out"), 1)

            shift(0, 0)
            shift(0, 1)
            for ph in range(4):
                main(ph)
            moe(0)
            moe(1)

        @block.tensor
        def _(pe):
            T = nc.tensor

            def transp4(dst, src, done, n=128):
                for q in range(QT):
                    last = T.transpose(dst[0:n, q * D:(q + 1) * D], src[:, q, :], ident[:, :])
                last.then_inc(sem(done), 1)

            def turn(g):
                n = min(GRP, NT - g * GRP)
                if g >= 2:
                    pe.wait_ge(sem("ct_out"), g - 1)
                for half, c0 in ((0, C_F), (1, C_L)):
                    for j in range(n):
                        last = T.transpose(sco[:, g % 2, :].bitcast(F16)[:, half * 512 + j * D:half * 512 + (j + 1) * D],
                                           c_val[:, g * GRP + j, c0:c0 + D], ident16[:, :])
                last.then_inc(sem("ct_ps"), 1)

            def turns(c):
                pe.wait_ge(sem("c_lo"), c + 1 if c < 3 else 5)
                for g in range(*GROUPS[c]):
                    turn(g)

            def sums(c):
                lo, hi = CHUNKS[c]
                pe.wait_ge(sem("ct_out"), GROUPS[c][1])
                if c:
                    pe.wait_ge(sem("mean"), c)
                for t in range(lo, NT if c == 3 else hi):
                    T.matmul(b6[:, t:t + 1], c_key[:, 0, t, :], ones16[:, :], start=True, stop=False)
                    last = T.matmul(b6[:, t:t + 1], c_key[:, 1, t, :], ones16[:, :], start=False, stop=True)
                last.then_inc(sem("sum_ps"), 1)

            def query0(h, part):
                if part == 0:
                    pe.wait_ge(sem("n0"), h + 1)
                    if h:
                        pe.wait_ge(sem("mean"), 4)
                        pe.wait_ge(sem("cq"), 1)
                    transp4(b6, nrm, "t0")
                    pe.wait_ge(sem("t0_sb"), h + 1)
                    T.matmul(b7[:, :], W["L0_xattn_Wq"], opT[:, :], start=True, stop=True).then_inc(sem("q0"), 1)
                else:
                    pe.wait_ge(sem("q0_sb"), h + 1)
                    for q in range(QT):
                        last = T.matmul(b7[:, q:q + 1], qT[:, q * D:(q + 1) * D], C["L0_xattn_bk"], start=True, stop=True)
                    last.then_inc(sem("c0"), 1)
                    T.matmul(b6[:, :], wk0[:, :], qT[:, :], start=True, stop=True).then_inc(sem("k0"), 1)

            def first_max(c):
                for g in range(*GROUPS[c]):
                    n = 512 if g < NG else TAILW
                    for j in range(2):
                        if g:
                            pe.wait_ge(sem("mf"), 2 * g + j - 1)
                        for q in (2 * j, 2 * j + 1):
                            last = T.matmul(acc[:, q, 0:n], q_hi[:, 0, q * D:(q + 1) * D],
                                            c_key[:, 0, g * GRP:min(NT, g * GRP + GRP), :].rearrange("p t d -> p (t d)")[:, 0:n],
                                            start=True, stop=True)
                        last.then_inc(sem("mf_ps"), 1)

            pe.wait_ge(sem("in_id"), 16)
            pe.wait_ge(sem("in_q"), 32)
            T.transpose(b7[:, 0:D], wraw[:, 0, :], ident[:, :]).then_inc(sem("wq_ps"), 1)
            pe.wait_ge(sem("wq_sb"), 1)
            pe.wait_ge(sem("in_b"), 32)
            query0(0, 0)
            pe.wait_ge(sem("id16"), 1)
            query0(0, 1)
            turns(0)
            pe.wait_ge(sem("in_w"), 16 * len(WNAMES))
            for i in range(1, len(WNAMES)):
                T.transpose(acc[:, (i - 1) // 4, ((i - 1) % 4) * D:((i - 1) % 4 + 1) * D], wraw[:, i, :], ident[:, :])
            T.transpose(acc[:, 2, 0:NE], gw[:, :], ident[0:NE, 0:NE]).then_inc(sem("wT_ps"), 1)
            pe.wait_ge(sem("q_lo"), 1)
            pe.wait_ge(sem("set"), 1)
            sums(0)
            turns(1)
            pe.wait_ge(sem("wT"), 1)
            first_max(0)
            sums(1)
            turns(2)
            first_max(1)
            sums(2)
            turns(3)
            sums(3)
            query0(1, 0)
            first_max(2)
            query0(1, 1)
            pe.wait_ge(sem("any"), 1)
            pe.wait_ge(sem("cq"), 2)
            T.matmul(b7[:, 4:5], ones[:, :], small[:, 8:9], start=True, stop=True).then_inc(sem("any_ps"), 1)
            first_max(3)

            def max_mm(ph, c, g, j, bank, two, static, n=512):
                if ph or not static or c:
                    pe.wait_ge(sem("mx"), c - 1 if two else c)
                keys, qs = (c_key[:, 0], q_hi) if ph == 0 else (h_max, qm)
                T.matmul(bank[:, 0:n], qs[:, (ph + 1) % 2, j * D:(j + 1) * D],
                         keys[:, bass.ds(g * GRP, GRP), :].rearrange("p t d -> p (t d)") if n == 512 else
                         keys[:, TAIL0:NT, :].rearrange("p t d -> p (t d)")[:, 0:n],
                         start=True, stop=True).then_inc(sem("mx_ps"), 1)

            def scores(ph, t, s, n=D, first=False):
                c = NT * ph + t
                L, h = ph // 2, ph % 2
                if not first:
                    pe.wait_ge(sem("exps"), c - 1)
                elif ph:
                    pe.wait_ge(sem("exps"), NT * ph)
                kk = h_key if L else c_key
                out = sco[0:n, s, :]
                if L == 0:
                    T.matmul(out, augw[:, 0:n], aug[:, :], start=True, stop=False)
                T.matmul(out, kk[:, 0, t, 0:n], q_hi[:, h, :], start=bool(L), stop=False)
                T.matmul(out, kk[:, 0, t, 0:n], q_lo[:, h, :], start=False, stop=False)
                T.matmul(out, kk[:, 1, t, 0:n], q_hi[:, h, :], start=False, stop=True).then_inc(sem("scores"), 1)

            def pv(ph, t, s, n=D, start=False, stop=False):
                pe.wait_ge(sem("p_low"), NT * ph + t + 1)
                if start and ph:
                    pe.wait_ge(sem("ev_a"), ph)
                    pe.wait_ge(sem("ev_v"), ph)
                val = h_val if ph // 2 else c_val
                for q in range(QT):
                    T.matmul(acc[:, q, 0:VW], p_hi[0:n, s, q * D:(q + 1) * D], val[0:n, t, :], start=start, stop=False)
                    last = T.matmul(acc[:, q, 0:D + 1], p_lo[0:n, s, q * D:(q + 1) * D], val[0:n, t, 0:D + 1],
                                    start=False, stop=stop)
                last.then_inc(sem("pv_done"), 1)

            def turn_h(g, s, n, m):
                if m == 0:
                    pe.wait_ge(sem("prep_split"), g + 1)
                else:
                    pe.wait_ge(sem("ht_out"), g + 1)
                    pe.wait_ge(sem("prep_m"), g + 1)
                for half in ((0, 1) if m == 0 else (2,)):
                    for j in range(n):
                        o = (half % 2) * 512 + j * D
                        last = T.transpose(b7[:, :].bitcast(F16)[:, o:o + D], pre_t[:, half, s, j, :], ident16[:, :])
                last.then_inc(sem("ht_ps" if m == 0 else "ht_m"), 1)

            def shift(ph):
                pe.wait_ge(sem("dg"), ph + 1)
                if ph == 0:
                    pe.wait_ge(sem("q_lo"), 2)
                T.matmul(b6[:, :], ones[:, :], scr[:, :, :].rearrange("p t d -> p (t d)"), start=True,
                         stop=True).then_inc(sem("m_ps"), 1)

            def main(ph):
                pr = ph == 0

                def trip(g, slot, static):
                    for s in range(GRP):
                        i = g * GRP + s
                        scores(ph, i + 2, s % 2)
                        if pr:
                            max_mm(ph, mx_count(ph, g, s, 0, static), g, s, b6, False, static)
                        elif ph < 3 and (not static or i >= 22):
                            for b in range(2):
                                if static:
                                    max_mm(ph, mx_count(ph, g, s, b, static), NG, 2 * (i - 22) + b, bk[b], True, True, TAILW)
                                else:
                                    max_mm(ph, mx_count(ph, g, s, b, static), 2 * (g - 6) + s // 2, 2 * (s % 2) + b, bk[b], True, False)
                        pv(ph, i, s, start=static and i == 0)
                        if pr:
                            if static and g < 2 and s % 2:
                                max_mm(ph, mx_count(ph, g, s, 1, static), NG, 2 * g + s // 2, b6, False, True, TAILW)
                            if s == 0 and not (static and g <= 1):
                                turn_h(g - 2, 1 - slot, GRP, 1)
                            if s == 2 and not (static and g == 0):
                                if not (static and g == 1):
                                    pe.wait_ge(sem("hm_done"), g - 1)
                                turn_h(g - 1, slot, GRP, 0)
                        elif static and ph < 3:
                            mid(ph - 1, i)
                            if ph == 1 and i == 10:
                                pe.wait_ge(sem("hm_done"), NG)
                                turn_h(NG, 0, NT - TAIL0, 0)
                            if ph == 1 and i == 12:
                                turn_h(NG, 0, NT - TAIL0, 1)
                            if i == 21:
                                pe.wait_ge(sem("qm"), ph)
                                pe.wait_ge(sem("hm_done"), NG + 1)
                        elif static:
                            post(0, i)

                if ph < 2:
                    pe.wait_ge(sem("aug"), ph + 1)
                else:
                    pe.wait_ge(sem("q_lo"), ph + 1)
                scores(ph, 0, 0, first=True)
                scores(ph, 1, 1, first=True)
                for g in range(STATIC[ph]):
                    trip(g, (g + 1) % 2, True)
                if pr:
                    with pe.Fori(STATIC[ph], NG - 1, 2) as g:
                        trip(g, 1, False)
                        trip(g + 1, 0, False)
                else:
                    with pe.Fori(STATIC[ph], NG) as g:
                        trip(g, None, False)
                scores(ph, FULL, 0, REST)
                pv(ph, TAIL0, 0)
                if pr:
                    turn_h(NG - 2, 0, GRP, 1)
                    pe.wait_ge(sem("hm_done"), NG - 1)
                    turn_h(NG - 1, 1, GRP, 0)
                pv(ph, TAIL0 + 1, 1)
                pv(ph, TAIL0 + 2, 2, REST, stop=True)
                if ph < 3:
                    shift(ph + 1)
                if pr:
                    turn_h(NG - 1, 1, GRP, 1)

            def mid(h, i):
                if i == 1:
                    pe.wait_ge(sem("av_done"), h + 1)
                    if h == 0:
                        pe.wait_ge(sem("hm_done"), NG)
                    transp4(b7, avg, "avT")
                elif i == 2:
                    pe.wait_ge(sem("avT_sb"), h + 1)
                    for q in range(QT):
                        last = T.matmul(b6[:, q * D:(q + 1) * D], opT[:, q * D:(q + 1) * D], W["L0_xattn_Wv"], start=True, stop=True)
                    last.then_inc(sem("o_ps"), 1)
                elif i == 5:
                    pe.wait_ge(sem("n1"), h + 1)
                    transp4(b6, nrm, "nT")
                elif i == 6:
                    pe.wait_ge(sem("nT_sb"), h + 1)
                    for i, n in enumerate(("wf", "wi")):
                        T.matmul(bk[(i + 1) % 2][:, :], W["L0_ffn_" + n], opT[:, :], start=True, stop=True).then_inc(sem("gate_ps"), 1)
                elif i == 7:
                    pe.wait_ge(sem("gate"), 3 * h + 1)
                    T.matmul(b7[:, :], W["L0_ffn_wc"], opT[:, :], start=True, stop=True).then_inc(sem("gate_ps"), 1)
                elif i == 9:
                    pe.wait_ge(sem("cell"), h + 1)
                    for q in range(QT):
                        o = b6[:, q * D:(q + 1) * D]
                        T.matmul(o, opT[:, q * D:(q + 1) * D], W["L0_ffn_wo"], start=True, stop=False)
                        last = T.matmul(o, opT2[:, q * D:(q + 1) * D], W["L0_ffn_uo"], start=False, stop=True)
                    last.then_inc(sem("ffn_ps"), 1)
                elif i == 14:
                    pe.wait_ge(sem("n2"), h + 1)
                    transp4(b6, avg, "tT")
                elif i == 16:
                    pe.wait_ge(sem("tT_sb"), h + 1)
                    T.matmul(b7[:, :], wq1[:, :], opT[:, :], start=True, stop=True).then_inc(sem("q1"), 1)
                elif i == 17:
                    pe.wait_ge(sem("q1_sb"), h + 1)
                    T.matmul(b6[:, :], W["L1_xattn_Wk"], qT[:, :], start=True, stop=True).then_inc(sem("g0"), 1)
                elif i == 19:
                    pe.wait_ge(sem("g0_sb"), h + 1)
                    for q in range(QT):
                        T.matmul(b7[:, q:q + 1], opT[:, q * D:(q + 1) * D], C["L1_xattn_ln_a_b"], start=True, stop=False)
                        T.matmul(b7[:, q:q + 1], qT[:, q * D:(q + 1) * D], C["L1_xattn_bk"], start=False, stop=True)
                    T.matmul(b6[:, :], cent[:, :], opT2[:, :], start=True, stop=True).then_inc(sem("qc"), 1)

            def post(h, i):
                if i == 1:
                    pe.wait_ge(sem("av_done"), 3 + h)
                    if h:
                        pe.wait_ge(sem("cw_lo"), 1)
                    transp4(b6, avg, "av1T")
                elif i == 3:
                    pe.wait_ge(sem("av1T_sb"), h + 1)
                    for q in range(QT):
                        last = T.matmul(b6[:, q * D:(q + 1) * D], opT[:, q * D:(q + 1) * D], wv1[:, :], start=True, stop=True)
                    last.then_inc(sem("o1_ps"), 1)
                elif i == 9:
                    pe.wait_ge(sem("n3"), h + 1)
                    transp4(b6, nrm, "n3T")
                elif i == 11:
                    pe.wait_ge(sem("x3_hi"), h + 1)
                    for q in range(QT):
                        last = T.matmul(b6[:, q * NE:(q + 1) * NE], opT[:, q * D:(q + 1) * D], gwT[:, :], start=True, stop=True)
                    last.then_inc(sem("lg"), 1)
                elif i == 17:
                    pe.wait_ge(sem("coef"), h + 1)
                    transp4(b6, coef, "cwT", 64)

            def moe(h):
                def gu(t, s, first=False):
                    c = MOE_T * h + t
                    if not first:
                        pe.wait_ge(sem("t2"), c - 1)
                    elif h:
                        pe.wait_ge(sem("t2"), MOE_T * h)
                    for w, out in ((moe_g, acc[:, s, :]), (moe_u, acc[:, 2 + s, :])):
                        T.matmul(out, w[:, 0, t, :], q_hi[:, h, :], start=True, stop=False)
                        T.matmul(out, w[:, 0, t, :], q_lo[:, h, :], start=False, stop=False)
                        T.matmul(out, w[:, 1, t, :], q_hi[:, h, :], start=False, stop=True)
                    T.matmul(sco[:, s, :], sel[:, t, :], cw16[:, h, :], start=True, stop=True).then_inc(sem("gu"), 1)

                def down(t, s, start=False, stop=False):
                    pe.wait_ge(sem("hid_lo"), MOE_T * h + t + 1)
                    T.matmul(b7[:, :], moe_d[:, 0, t, :], p_hi[:, s, :], start=start, stop=False)
                    T.matmul(b7[:, :], moe_d[:, 0, t, :], p_lo[:, s, :], start=False, stop=False)
                    T.matmul(b7[:, :], moe_d[:, 1, t, :], p_hi[:, s, :], start=False, stop=stop).then_inc(sem("down"), 1)
                if h == 0:
                    pe.wait_ge(sem("ev_a"), 4)
                    pe.wait_ge(sem("ev_v"), 4)
                    pe.wait_ge(sem("exps"), 4 * NT)
                    pe.wait_ge(sem("split_w"), 3)
                    pe.wait_ge(sem("in_k"), 48)
                pe.wait_ge(sem("cw_lo"), h + 1)
                gu(0, 0, True)
                gu(1, 1, True)
                gu(2, 0)
                if h:
                    pe.wait_ge(sem("yT"), h)
                down(0, 0, start=True)
                if h == 0:
                    post(1, 0)
                    for t in range(1, MOE_T - 3):
                        gu(t + 2, t % 2)
                        down(t, t % 2)
                        post(1, t)
                else:
                    gu(3, 1)
                    down(1, 1)
                    with pe.Fori(2, MOE_T - 4, 2) as t:
                        gu(t + 2, 0)
                        down(t, 0)
                        gu(t + 3, 1)
                        down(t + 1, 1)
                gu(MOE_T - 1, 0)
                down(MOE_T - 3, 0)
                if h == 0:
                    post(1, MOE_T - 3)
                down(MOE_T - 2, 1)
                down(MOE_T - 1, 0, stop=True)
                pe.wait_ge(sem("yT"), h + 1)
                if h:
                    pe.wait_ge(sem("y_out"), h)
                transp4(b6, opT[:, :].rearrange("p (t d) -> p t d", t=QT), "y_ps")

            shift(0)
            for ph in range(4):
                main(ph)
            moe(0)
            moe(1)


_INS = ['x', 'ctx_1024', 'mask_BxS2_ik0', 'g_xattn', 'g_ffn', 'L0_xattn_Wq', 'L0_xattn_bq', 'L0_xattn_Wk', 'L0_xattn_bk', 'L0_xattn_Wv', 'L0_xattn_bv', 'L0_ffn_wf', 'L0_ffn_uf', 'L0_ffn_bf', 'L0_ffn_wi', 'L0_ffn_ui', 'L0_ffn_bi', 'L0_ffn_wc', 'L0_ffn_uc', 'L0_ffn_bc', 'L0_ffn_wo', 'L0_ffn_uo', 'L0_ffn_bo', 'L0_ffn_in_c', 'L1_xattn_ln_t_g', 'L1_xattn_ln_t_b', 'L1_xattn_ln_a_g', 'L1_xattn_ln_a_b', 'L1_xattn_Wq', 'L1_xattn_bq', 'L1_xattn_Wk', 'L1_xattn_bk', 'L1_xattn_Wv', 'L1_xattn_bv', 'L1_xattn_ln_p_g', 'L1_xattn_ln_p_b', 'L1_ffn_gate_weight', 'L1_ffn_gate_bias', 'L1_ffn_w_gate', 'L1_ffn_w_up', 'L1_ffn_w_down', 'L1_ffn_shared_w_gate', 'L1_ffn_shared_w_up', 'L1_ffn_shared_w_down', 'L1_ffn_anchor_w_gate', 'L1_ffn_anchor_w_up', 'L1_ffn_anchor_w_down']


def _constants():
    import numpy as np
    seg = np.ones((128, QT, NE), np.float32)
    seg[:, :, 0] = 0.0
    i, j = np.divmod(np.arange(16), 4)
    lt4 = np.broadcast_to((j < i).astype(np.float32), (128, 16))
    sel = np.zeros((128, MOE_T, D), np.float16)
    lane = np.arange(D)
    for t in range(MOE_T):
        if t < ROUTED_T:
            r = 2 * t + lane // ME
        elif t < ROUTED_T + ANCHOR_T:
            r = NE + 4 * (t - ROUTED_T) + lane // MA
        else:
            r = np.full(D, NE + NA)
        sel[r, t, lane] = 1.0
        sel[64 + r, t, lane] = 1.0
    return {
        "c_ident": np.eye(D, dtype=np.float32),
        "c_cent": (np.eye(D) - 1.0 / D).astype(np.float32),
        "c_seg": seg.reshape(128, QT * NE),
        "c_lt4": np.ascontiguousarray(lt4),
        "c_sel": sel.reshape(128, MOE_T * D),
    }


def kernel(**inputs):
    import numpy as _np
    import concourse.bacc as _bacc
    from concourse import mybir as _mybir
    from concourse.bass_utils import run_bass_kernel_spmd as _run

    nc = _bacc.Bacc("TRN2", target_bir_lowering=False, num_devices=1)
    arrays, args = {}, {}
    data = {name: inputs[name] for name in _INS}
    data.update(_constants())
    for name, value in data.items():
        v = _np.ascontiguousarray(value)
        arrays[f"in_{name}_dram"] = v
        args[name] = nc.dram_tensor(f"in_{name}_dram", v.shape, _mybir.dt.from_np(v.dtype), kind="ExternalInput").ap()
    args["out"] = nc.dram_tensor("out_0_dram", (1, NQ, D), _mybir.dt.float32, kind="ExternalOutput").ap()
    build(nc, args)
    r = _run(nc, [arrays], core_ids=[0])
    return r.results[0]["out_0_dram"]
```

```python
import concourse.bass as bass
from concourse import mybir
from concourse.alu_op_type import AluOpType as ALU
from contextlib import ExitStack

F32 = mybir.dt.float32
F16 = mybir.dt.float16
BF16 = mybir.dt.bfloat16
I32 = mybir.dt.int32
ACT = mybir.ActivationFunctionType
AX = mybir.AxisListType

D = 128
NQ = 1024
HALVES = 2
QT = 4
QH = QT * D
NK = 6404
FULL = NK // D
REST = NK - FULL * D
NT = FULL + 1
GRP = 4
NG = 12
TAIL0 = NG * GRP
TAILW = NK - TAIL0 * D
NE, ME = 32, 64
NA, MA = 16, 32
MOE_T = 21
ROUTED_T, ANCHOR_T = 16, 4
TOPK = 6
ROUTED_SCALE = 0.2
ANCHOR_ALPHA = 0.1

SPLIT = 256.0
PROD = SPLIT * SPLIT
ATT_SCALE = float(D) ** -0.5
P_LOG = 12 * 0.6931471805599453 / ATT_SCALE
PEN = 65280.0
CW_SCALE = 1024.0
HID_SCALE = 32.0
LN_EPS = 1e-5
VW = 2 * D
C_F, C_L = 0, D


def build(nc, a):
    ctx = ExitStack()
    with ctx:
        def sb(name, shape, dt=F32):
            return ctx.enter_context(nc.sbuf_tensor(name, shape, dt))

        def ps(name, shape, dt=F32):
            return ctx.enter_context(nc.psum_tensor(name, shape, dt))

        made = {}

        def sem(name):
            if name not in made:
                made[name] = ctx.enter_context(nc.semaphore(name))
            return made[name]

        ctx_nat = sb("ctx_nat", [128, NT, D])
        c_val = sb("c_val", [128, NT, VW], F16)
        h_val = sb("h_val", [128, NT, VW], F16)
        c_key = sb("c_key", [128, 2, NT, D], F16)
        h_key = sb("h_key", [128, 2, NT, D], F16)
        h_max = sb("h_max", [128, NT, D], F16)
        p_hi = sb("p_hi", [128, GRP, QH], F16)
        p_lo = sb("p_lo", [128, GRP, QH], F16)
        p_f = sb("p_f", [128, GRP, QH])
        ident = sb("ident", [128, 128])
        ident16 = sb("ident16", [128, 128], F16)
        cent = sb("cent", [128, 128])
        ones = sb("ones", [128, 128])
        ones16 = sb("ones16", [128, 1], F16)
        split_col = sb("split_col", [128, 1])
        augw = sb("augw", [128, 128], BF16)
        WNAMES = ["L0_xattn_Wq", "L0_xattn_Wv", "L0_ffn_wf", "L0_ffn_wi", "L0_ffn_wc", "L0_ffn_wo",
                  "L0_ffn_uo", "L1_xattn_Wk"]
        wT = sb("wT", [128, len(WNAMES), 128])
        W = {n: wT[:, i, :] for i, n in enumerate(WNAMES)}
        wk0 = sb("wk0", [128, 128])
        wq1 = sb("wq1", [128, 128])
        wv1 = sb("wv1", [128, 128])
        gw = p_f[0:NE, 2, 0:D]
        gwT = sb("gwT", [128, NE])
        COLS = ["L0_xattn_bq", "L0_xattn_bk", "L0_ffn_bf", "L0_ffn_bi", "L0_ffn_bc", "L0_ffn_in_c",
                "L1_xattn_ln_t_g", "L1_xattn_ln_t_b", "L1_xattn_ln_a_g", "L1_xattn_ln_a_b",
                "L1_xattn_bq", "L1_xattn_bk"]
        cols = sb("cols", [128, len(COLS)])
        C = {n: cols[:, i:i + 1] for i, n in enumerate(COLS)}
        ROWS = ["L0_xattn_bv", "L0_ffn_bo", "L1_xattn_bv", "L1_xattn_ln_p_g",
                "L1_xattn_ln_p_b"]
        rows = sb("rows", [128, len(ROWS), 128])
        R = {n: rows[:, i, :] for i, n in enumerate(ROWS)}
        gates = sb("gates", [128, 4])
        tg = sb("tg", [128, 4])
        gbias = sb("gbias", [128, NE])
        lt4 = sb("lt4", [128, 16])
        seg = sb("seg", [128, 128])
        sel = h_max[:, 0:MOE_T, :]
        xres = sb("xres", [128, HALVES, QT, D])
        nrm = sb("nrm", [128, QT, D])
        avg = sb("avg", [128, QT, D])
        us = avg[:, 0:3, :]
        den = sb("den", [128, 2, QH])
        scr = sb("scr", [128, QT, D])
        opT = sb("opT", [128, QH])
        gt = sb("gt", [128, 3, QH])
        wraw = p_f[:, 0:2, :].rearrange("p a b -> p (a b)").rearrange("p (n d) -> p n d", d=D)
        rt = gt[:, :, :].rearrange("p a b -> p (a b)")[:, 0:8 * QT * NE].rearrange("p (i t e) -> p i t e", i=8, t=QT)
        junk = h_val[:, :, 0:D]
        qT = gt[:, 0, :]
        opT2 = gt[:, 2, :]
        room = sb("room", [128, 6 * QH], F16)
        pre_t = room[:, :].rearrange("p (k s t d) -> p k s t d", k=3, s=2, t=GRP)
        qg = room[:, 0:4 * QH].bitcast(F32).rearrange("p (h q) -> p h q", h=HALVES)
        qm = room[:, 4 * QH:6 * QH].rearrange("p (h q) -> p h q", h=HALVES)
        q_hi = sb("q_hi", [128, HALVES, QH], F16)
        q_lo = sb("q_lo", [128, HALVES, QH], F16)
        aug = sb("aug", [128, HALVES, QH], BF16)
        mx = sb("mx", [128, QT, NG + 1])
        small = sb("small", [128, 64])
        NLN = 10
        lnst = sb("lnst", [128, QT, 6])
        lnmv = sb("lnmv", [128, NLN, QT, 2])
        lnve = sb("lnve", [128, NLN, QT])
        lnrs = sb("lnrs", [128, NLN, QT])
        mhalf = sb("mhalf", [128, NT])
        ck = sb("ck", [128, 8, NT])
        away4 = sb("away4", [128, GRP])
        mask_i = sb("mask_i", [128, NT], I32)
        bcols = sb("bcols", [128, 4])
        moe_g = c_key[:, :, 0:21, :]
        moe_u = c_key[:, :, 21:42, :]
        moe_d = c_val[:, :, :].rearrange("p t v -> p (t v)")[:, 0:2 * MOE_T * D].rearrange(
            "p (s t d) -> p s t d", s=2, t=MOE_T)
        MOE_W = [moe_g, moe_u, moe_d]
        stage = [ctx_nat[:, 0:21, :], ctx_nat[:, 21:42, :],
                 c_val[:, :, :].rearrange("p t v -> p (t v)")[:, 2 * MOE_T * D:4 * MOE_T * D].bitcast(F32).rearrange(
                     "p (t d) -> p t d", t=MOE_T)]
        r8 = sb("r8", [128, QT, 8])
        g8 = sb("g8", [128, QT, 4, 8])
        gs = sb("gs", [128, 6, QT, 4])
        gp = sb("gp", [128, 3, QT, 16])
        coef = sb("coef", [128, QT, 64])
        cw16 = qm
        cq = sb("cq", [128, HALVES, QT])

        sco = ps("sco", [128, GRP, 512])
        acc = ps("acc", [128, 2, 512])
        bk = [ps("bk6", [128, 512]), ps("bk7", [128, 512])]
        b6, b7 = bk

        block = ctx.enter_context(nc.Block())
        H = range(HALVES)
        LOOP = ((4, 10), (6, 11), (6, 11), (6, 12))
        LAG = 2
        AHEAD = 2
        MXP = GRP * (NG + 1)
        MX1 = 3 * MXP
        CW = 3

        MOE_PE = {1: 3, 9: 12, 11: 13, 18: 22}
        MOE_ACT = {11: 12, 13: 14, 20: 21}
        MOE_DVE = {2: (2,), 3: (3,), 4: (4,), 6: (5, 6), 7: (7,), 8: (8,), 10: (10,), 12: (13,), 13: (15,), 14: (16,), 15: (17,),
                   16: (18,), 17: (19,), 18: (20,)}

        def written(ph, side):
            lo, hi = LOOP[ph]
            return range(0, lo) if side == 0 else range(hi, NG)

        def mx_plan(ph, i):
            def extra(e):
                return ((NG, e), (NG - 2, e - 4), (NG - 1, e - 8))[e // 4]
            if ph == 0 and i < 16:
                return i + min(max(i - 1, 0), 12), [(i // 4, i % 4)] + ([extra(i - 1)] if 1 <= i <= 12 else [])
            if ph in (1, 2) and i in (22, 23, 44, 45):
                k = (22, 23, 44, 45).index(i)
                return MXP * ph + (0, 3, 46, 49)[k], [extra(3 * k + m) for m in range(3)]
            return 0, []

        def mx_loop(ph, g, s):
            if ph == 0:
                return 28 + 4 * (g - 4) + s, [(g, s)]
            if ph == 3:
                return 0, []
            return MXP * ph + 6 + 8 * (g - 6) + 2 * s, [(2 * (g - 6) + s // 2, 2 * (s % 2) + b) for b in range(2)]

        CHUNKS = [(0, 12), (12, 24), (24, 36), (36, 50)]
        GROUPS = [(0, 3), (3, 6), (6, 9), (9, 13)]

        @block.sync
        def _(sp):
            cm = a["ctx_1024"].rearrange("a k d -> (a k) d")
            cmain = cm[0:FULL * D, :].rearrange("(p t) d -> p t d", t=FULL)
            sp.dma_start(ident[:, :], a["c_ident"]).then_inc(sem("in_id"), 16)
            for c, (lo, hi) in enumerate(CHUNKS):
                sp.dma_start(ctx_nat[:, lo:hi, :], cmain[:, lo:hi, :]).then_inc(sem(f"in_c{c}"), 16)
            sp.wait_ge(sem("clr"), 1)
            sp.dma_start(ctx_nat[0:REST, FULL, :], cm[FULL * D:NK, :]).then_inc(sem("in_rest"), 16)
            mk = a["mask_BxS2_ik0"].rearrange("a k -> (a k)")
            sp.dma_start(mask_i[:, 0:FULL], mk[0:FULL * D].rearrange("(p t) -> p t", t=FULL)).then_inc(sem("in_m"), 16)
            sp.dma_start(mask_i[0:REST, FULL:NT], mk[FULL * D:NK].rearrange("(p t) -> p t", t=1)).then_inc(sem("in_m"), 16)
            sp.dma_start(xres[:, 1], a["x"].rearrange("a (h p t) d -> (a h) p t d", p=128, t=QT)[1]).then_inc(sem("in_x1"), 16)
            for i, n in list(enumerate(WNAMES))[1:]:
                sp.dma_start(wraw[:, i, :], a[n]).then_inc(sem("in_w"), 16)
            sp.dma_start(gw[:, :], a["L1_ffn_gate_weight"]).then_inc(sem("in_w"), 16)
            for n in COLS[2:]:
                sp.dma_start(C[n], a[n].rearrange("(d o) -> d o", o=1)).then_inc(sem("in_v"), 16)
            sp.dma_start(gates[:, 0:2], a["g_xattn"].rearrange("(o d) -> o d", o=1).broadcast_to([128, 2])).then_inc(sem("in_v"), 16)
            sp.dma_start(gates[:, 2:4], a["g_ffn"].rearrange("(o d) -> o d", o=1).broadcast_to([128, 2])).then_inc(sem("in_v"), 16)
            sp.dma_start(seg[:, :], a["c_seg"]).then_inc(sem("in_k"), 16)
            sp.dma_start(lt4[:, :], a["c_lt4"]).then_inc(sem("in_k"), 16)
            sp.dma_start(cent[:, :], a["c_cent"]).then_inc(sem("in_u"), 16)
            sp.dma_start(wq1[:, :], a["L1_xattn_Wq"]).then_inc(sem("in_u"), 16)
            sp.dma_start(wv1[:, :], a["L1_xattn_Wv"]).then_inc(sem("in_u"), 16)
            for i, n in enumerate(("uf", "ui", "uc")):
                sp.dma_start(us[:, i, :], a["L0_ffn_" + n]).then_inc(sem("in_u"), 16)
            sp.dma_start(avg[:, 3, :], a["L0_ffn_in_c"].rearrange("(o d) -> o d", o=1).broadcast_to([128, 128])).then_inc(sem("in_u"), 16)
            for n in ROWS:
                sp.dma_start(R[n], a[n].rearrange("(o d) -> o d", o=1).broadcast_to([128, 128])).then_inc(sem("in_u"), 16)
            sp.dma_start(gbias[:, :], a["L1_ffn_gate_bias"].rearrange("(o d) -> o d", o=1).broadcast_to([128, NE])).then_inc(sem("in_u"), 16)
            sp.wait_ge(sem("stage_clr"), 1)
            for i, (r, n, s) in enumerate((("w_gate", "anchor_w_gate", "shared_w_gate"),
                                           ("w_up", "anchor_w_up", "shared_w_up"))):
                sp.dma_start(stage[i][:, 0:16, :].rearrange("p t d -> p (t d)").rearrange("p (e i) -> p e i", e=NE),
                             a["L1_ffn_" + r].rearrange("e h i -> h e i")).then_inc(sem(f"in_w{i}"), 16)
                sp.dma_start(stage[i][:, 16:20, :].rearrange("p t d -> p (t d)").rearrange("p (e i) -> p e i", e=NA),
                             a["L1_ffn_" + n].rearrange("e h i -> h e i")).then_inc(sem(f"in_w{i}"), 16)
                sp.dma_start(stage[i][:, 20, 0:ME], a["L1_ffn_" + s]).then_inc(sem(f"in_w{i}"), 16)
            sp.wait_ge(sem("down_clr"), 1)
            sp.dma_start(stage[2][:, 0:16, :], a["L1_ffn_w_down"].rearrange("(t e) i h -> (e i) t h", e=2)).then_inc(sem("in_w2"), 16)
            sp.dma_start(stage[2][:, 16:20, :], a["L1_ffn_anchor_w_down"].rearrange("(t e) i h -> (e i) t h", e=4)).then_inc(sem("in_w2"), 16)
            sp.dma_start(stage[2][0:ME, 20, :], a["L1_ffn_shared_w_down"]).then_inc(sem("in_w2"), 16)
            sp.wait_ge(sem("mx"), MX1)
            sp.dma_start(sel, a["c_sel"].rearrange("p (t d) -> p t d", t=MOE_T)).then_inc(sem("in_k"), 16)
            for h in H:
                sp.wait_ge(sem("y_out"), h + 1)
                sp.dma_start(a["out"].rearrange("a (h p t) d -> (a h) p t d", p=128, t=QT)[h], xres[:, h]).then_inc(sem("stored"), 16)
            sp.wait_ge(sem("stored"), 32)

        @block.gpsimd
        def _(pool):
            nc.gpsimd.memset(ctx_nat[:, FULL, :], 0.0)
            nc.gpsimd.memset(mask_i[:, FULL:NT], 0).then_inc(sem("clr"), 1)
            nc.gpsimd.memset(augw[:, :], PROD / 64.0)
            nc.gpsimd.memset(ones16[:, :], 1.0)
            nc.gpsimd.memset(split_col[:, :], SPLIT)
            nc.gpsimd.memset(ones[:, :], 1.0).then_inc(sem("set"), 1)
            nc.gpsimd.memset(mhalf[:, :], -0.5).then_inc(sem("half"), 1)
            nc.gpsimd.memset(coef[:, :, :], 0.0).then_inc(sem("coef0"), 1)
            pool.wait_ge(sem("coef0"), 1)
            nc.gpsimd.memset(coef[:, :, 48:49], 1.0).then_inc(sem("coef1"), 1)
            pool.wait_ge(sem("half"), 1)

            def inv_root(n):
                pool.wait_ge(sem("ln_var"), n + 1)
                nc.gpsimd.tensor_tensor(lnrs[:, n, :], lnve[:, n, :], mhalf[:, 0:QT], ALU.pow).then_inc(sem("ln_inv"), 1)

            def bc(i, t0, n):
                return ck[:, i, bass.ds(t0, n)].unsqueeze(2).broadcast_to([128, n, D])

            def centre(c):
                lo, hi = CHUNKS[c]
                hi = NT if c == 3 else hi
                pool.wait_ge(sem("mean"), c + 1)
                x = ctx_nat[:, lo:hi, :]
                nc.gpsimd.tensor_tensor(x, x, bc(0, lo, hi - lo), ALU.add).then_inc(sem("centred"), 1)

            inv_root(0)
            inv_root(1)
            for c in range(4):
                centre(c)

            def column(c):
                lo, hi = CHUNKS[c]
                hi = NT if c == 3 else hi
                pool.wait_ge(sem("spread"), c + 1)
                nc.gpsimd.tensor_scalar(ck[:, 1, lo:hi], ck[:, 1, lo:hi], 1.0 / D, LN_EPS, ALU.mult, ALU.add).then_inc(sem("k_var"), 1)
                pool.wait_ge(sem("k_var"), c + 1)
                nc.gpsimd.tensor_tensor(ck[:, 2, lo:hi], ck[:, 1, lo:hi], mhalf[:, lo:hi], ALU.pow).then_inc(sem("k_inv"), 1)
                pool.wait_ge(sem("k_inv"), c + 1)
                if c == 0:
                    pool.wait_ge(sem("w"), 1)
                nc.gpsimd.tensor_tensor(ck[:, 3, lo:hi], ck[:, 2, lo:hi], ck[:, 5, lo:hi], ALU.mult).then_inc(sem("k_cols"), 1)
                pool.wait_ge(sem("k_cols"), c + 1)

            for c in range(4):
                column(c)

            def prep(g, t0, n, s, part, first=False):
                x = ctx_nat[:, bass.ds(t0, n), :]
                if part == 0:
                    nc.gpsimd.tensor_tensor(x, x, bc(3, t0, n), ALU.mult).then_inc(sem("prep_pool"), 1)
                else:
                    pool.wait_ge(sem("prep_pool"), g + 1)
                    if not first:
                        pool.wait_ge(sem("ht_m"), g - 1)
                    nc.gpsimd.tensor_tensor(pre_t[:, 2, s, 0:n, :], x, bc(6, t0, n), ALU.add).then_inc(sem("prep_m"), 1)

            def add(ph, t, s, n=D, first=False):
                c = NT * ph + t
                pool.wait_ge(sem("exps"), c + 1)
                b = ph % 2
                if first:
                    if ph >= 2:
                        pool.wait_ge(sem("den_ps"), ph - 1)
                    nc.gpsimd.tensor_copy(den[0:n, b, :], p_f[0:n, s, :]).then_inc(sem("added"), 1)
                else:
                    pool.wait_ge(sem("added"), c)
                    nc.gpsimd.tensor_tensor(den[0:n, b, :], den[0:n, b, :], p_f[0:n, s, :], ALU.add).then_inc(sem("added"), 1)

            def main(ph):
                pr = ph == 0

                def trip(g, slot, static):
                    for s in range(GRP):
                        i = g * GRP + s
                        add(ph, i, s, first=static and i == 0)
                        if pr and s == 0 and not (static and g + AHEAD > NG):
                            prep(g + AHEAD, (g + AHEAD) * GRP, (NT - TAIL0 if static and g + AHEAD == NG else GRP), None, s)
                        if pr and s == 2:
                            prep(g, g * GRP, GRP, slot, 2, first=static and g < 2)
                        if static and ph in (1, 2) and i in (5, 13):
                            inv_root(2 + 2 * (ph - 1) + (5, 13).index(i))
                        elif static and ph == 3 and i in (6, 10):
                            inv_root(6 + (6, 10).index(i))
                        if static and ph == 1 and i == 6:
                            prep(NG, TAIL0, NT - TAIL0, 0, 2)
                        if static and ph == 1 and i == 9:
                            pool.wait_ge(sem("prep_split"), NG + 1)
                            pool.wait_ge(sem("prep_m"), NG + 1)
                            nc.gpsimd.memset(ctx_nat[:, 20, ME:D], 0.0)
                            nc.gpsimd.memset(ctx_nat[:, 41, ME:D], 0.0).then_inc(sem("stage_clr"), 1)
                        if static and ph == 2 and i == 4:
                            pool.wait_ge(sem("pv_done"), 2 * NT)
                            pool.wait_ge(sem("added"), 2 * NT + i + 1)
                            nc.gpsimd.memset(stage[2][ME:D, 20, :], 0.0).then_inc(sem("down_clr"), 1)
                            pool.wait_ge(sem("down_clr"), 1)
                if pr:
                    for g in range(AHEAD):
                        prep(g, g * GRP, GRP, None, 0)
                    for g in range(2):
                        trip(g, g % 2, True)
                    with pool.Fori(2, NG - AHEAD - 1, 2) as g:
                        trip(g, 0, False)
                        trip(g + 1, 1, False)
                    for g in range(NG - AHEAD, NG):
                        trip(g, g % 2, True)
                else:
                    for g in written(ph, 0):
                        trip(g, None, True)
                    with pool.Fori(*LOOP[ph]) as g:
                        trip(g, None, False)
                    for g in written(ph, 1):
                        trip(g, None, True)
                for k in range(3):
                    add(ph, TAIL0 + k, k, REST if k == 2 else D)

            for ph in range(4):
                main(ph)

            def low(h, t, s):
                pool.wait_ge(sem("hid_hi"), MOE_T * h + t + 1)
                nc.gpsimd.tensor_tensor(p_lo[:, s, :], p_f[:, 2 + s, :], p_hi[:, s, :], ALU.subtract).then_inc(sem("hid_lo"), 1)
            for t in range(MOE_T):
                if t == 5:
                    inv_root(8)
                if t == 9:
                    inv_root(9)
                low(0, t, t % 2)
            with pool.Fori(0, MOE_T - 2, 2) as t:
                low(1, t, 0)
                low(1, t + 1, 1)
            low(1, MOE_T - 1, 0)

        @block.scalar
        def _(act):
            xv = a["x"].rearrange("a (h p t) d -> (a h) p t d", p=128, t=QT)
            act.dma_start(xres[:, 0], xv[0]).then_inc(sem("in_x"), 16)
            act.dma_start(wraw[:, 0, :], a[WNAMES[0]]).then_inc(sem("in_q"), 16)
            act.dma_start(C[COLS[0]], a[COLS[0]].rearrange("(d o) -> d o", o=1)).then_inc(sem("in_bq"), 16)
            act.dma_start(wk0[:, :], a["L0_xattn_Wk"]).then_inc(sem("in_k0"), 16)
            act.dma_start(C[COLS[1]], a[COLS[1]].rearrange("(d o) -> d o", o=1)).then_inc(sem("in_bk"), 16)
            act.wait_ge(sem("in_id"), 16)
            nc.scalar.copy(ident16[:, :], ident[:, :]).then_inc(sem("id16"), 1)

            def high(c):
                lo, hi = CHUNKS[c]
                act.wait_ge(sem(f"in_c{c}"), 16)
                if c == 3:
                    act.wait_ge(sem("in_rest"), 16)
                    nc.scalar.mul(c_val[:, FULL, C_F:C_F + D], ctx_nat[:, FULL, :], SPLIT)
                nc.scalar.mul(c_val[:, lo:hi, C_F:C_F + D], ctx_nat[:, lo:hi, :], SPLIT).then_inc(sem("c_hi"), 1)

            def turned(g0, g1):
                for g in range(g0, g1):
                    n = min(GRP, NT - g * GRP)
                    act.wait_ge(sem("ct_ps"), g + 1)
                    nc.scalar.copy(c_key[:, :, g * GRP:g * GRP + n, :].rearrange("p s t d -> p s (t d)"),
                                   acc[:, g % 2, :].bitcast(F16).rearrange("p (s w) -> p s w", s=2)[:, :, 0:n * D]).then_inc(sem("ct_out"), 1)

            def spread(c):
                lo, hi = CHUNKS[c]
                act.wait_ge(sem("centred"), c + 1)
                for t in range(lo, NT if c == 3 else hi):
                    last = nc.scalar.activation(junk[:, t, :], ctx_nat[:, t, :], ACT.Square,
                                                accum_out=ck[:, 1, t:t + 1])
                last.then_inc(sem("spread"), 1)

            def query0(h, part):
                if part == 0:
                    if h:
                        act.wait_ge(sem("t0"), 2)
                        nc.scalar.copy(opT[:, :], b6[:, :]).then_inc(sem("t0_sb"), 1)
                    act.wait_ge(sem("q0"), h + 1)
                    nc.scalar.activation(qT[:, :], b7[:, :], ACT.Identity, bias=C["L0_xattn_bq"]).then_inc(sem("q0_sb"), 1)
                else:
                    act.wait_ge(sem("k0"), h + 1)
                    nc.scalar.mul(q_hi[:, h, :], b6[:, :], SPLIT).then_inc(sem("q_hi"), 1)

            act.wait_ge(sem("wq_ps"), 1)
            nc.scalar.copy(W[WNAMES[0]], b7[:, 0:D]).then_inc(sem("wq_sb"), 1)
            high(0)
            act.wait_ge(sem("t0"), 1)
            nc.scalar.copy(opT[:, :], b6[:, :]).then_inc(sem("t0_sb"), 1)
            high(1)
            act.wait_ge(sem("in_bq"), 16)
            query0(0, 0)
            turned(0, 1)
            query0(0, 1)
            turned(1, 2)
            high(2)
            turned(2, 3)
            high(3)
            turned(3, NG + 1)
            spread(0)
            act.wait_ge(sem("wT_ps"), 1)
            nc.scalar.copy(wT[:, 1:8, :].rearrange("p a b -> p (a b)")[:, 0:512], acc[:, 0, :])
            nc.scalar.copy(wT[:, 1:8, :].rearrange("p a b -> p (a b)")[:, 512:896], acc[:, 1, 0:384])
            nc.scalar.copy(gwT[:, :], acc[:, 1, 384:384 + NE]).then_inc(sem("wT"), 1)
            spread(1)
            query0(1, 0)
            spread(2)
            query0(1, 1)
            act.wait_ge(sem("in_v"), 16 * len(COLS))
            nc.scalar.activation(tg[:, :], gates[:, :], ACT.Tanh).then_inc(sem("tg"), 1)
            spread(3)

            def shift(ph):
                if ph < 2:
                    act.wait_ge(sem("m_ps"), ph + 1)
                    nc.scalar.copy(aug[:, ph, :], b6[:, :]).then_inc(sem("aug_hi"), 1)
                else:
                    act.wait_ge(sem("g1"), ph - 1)
                    nc.scalar.mul(q_hi[:, ph % 2, :], opT[:, :], SPLIT).then_inc(sem("q_hi"), 1)

            def mid(h, i):
                if i == 1:
                    act.wait_ge(sem("pv_done"), NT * (h + 1))
                    if h:
                        act.wait_ge(sem("q_lo"), 3)
                    nc.scalar.copy(opT[:, :], acc[:, h, :]).then_inc(sem("av_done"), 1)
                elif i == 6:
                    act.wait_ge(sem("nT"), h + 1)
                    nc.scalar.copy(opT[:, :], b6[:, :]).then_inc(sem("nT_sb"), 1)
                elif i == 7:
                    gate(h, 0)
                    gate(h, 1)
                elif i == 8:
                    gate(h, 2)
                elif i == 11:
                    act.wait_ge(sem("f_sum"), h + 1)
                    nc.scalar.activation(avg[:, :, :], scr[:, :, :], ACT.Tanh).then_inc(sem("f_tanh"), 1)
                elif i == 15:
                    act.wait_ge(sem("tT"), h + 1)
                    nc.scalar.activation(opT[:, :], b6[:, :], ACT.Identity, scale=C["L1_xattn_ln_t_g"],
                                         bias=C["L1_xattn_ln_t_b"]).then_inc(sem("tT_sb"), 1)
                elif i == 16:
                    act.wait_ge(sem("q1"), h + 1)
                    nc.scalar.activation(qT[:, :], b7[:, :], ACT.Identity, bias=C["L1_xattn_bq"]).then_inc(sem("q1_sb"), 1)
                elif i == 17:
                    act.wait_ge(sem("g0"), h + 1)
                    nc.scalar.copy(opT[:, :], b6[:, :])
                    nc.scalar.mul(opT2[:, :], b6[:, :], C["L1_xattn_ln_a_g"]).then_inc(sem("g0_sb"), 1)
                elif i == 20:
                    act.wait_ge(sem("qc_sb"), h + 1)
                    nc.scalar.activation(qm[:, h, :], qg[:, h, :], ACT.Copy, scale=SPLIT, bias=SPLIT).then_inc(sem("qm"), 1)

            def gate(h, i):
                act.wait_ge(sem("gate_ps"), 3 * h + i + 1)
                act.wait_ge(sem("gate_bias"), 1)
                nc.scalar.activation(gt[:, i, :], bk[(i + 1) % 2][:, :], ACT.Tanh, bias=bcols[:, i:i + 1],
                                     scale=0.5 if i < 2 else 1.0).then_inc(sem("gate"), 1)

            def post(h, i):
                if i == 1:
                    act.wait_ge(sem("pv_done"), NT * (h + 3))
                    if h:
                        act.wait_ge(sem("x3_lo"), 1)
                    else:
                        act.wait_ge(sem("q_lo"), 4)
                    nc.scalar.mul(opT[:, :], acc[:, h, :], C["L1_xattn_ln_a_g"]).then_inc(sem("av_done"), 1)
                elif i == 12:
                    act.wait_ge(sem("n3T"), h + 1)
                    nc.scalar.copy(opT[:, :], b6[:, :])
                    nc.scalar.mul(q_hi[:, h, :], b6[:, :], SPLIT).then_inc(sem("x3_hi"), 1)
                elif i == 14:
                    act.wait_ge(sem("lg"), h + 1)
                    nc.scalar.activation(rt[:, 0, :, :].rearrange("p a b -> p (a b)"), b6[:, 0:QT * NE], ACT.Tanh, scale=0.5).then_inc(sem("lg_t"), 1)
                elif i == 21:
                    act.wait_ge(sem("cwT"), h + 1)
                    nc.scalar.mul(cw16[0:64, h, :], b6[0:64, :], CW_SCALE).then_inc(sem("cw_hi"), 1)

            def exps(ph, t, s, n=D, first=False):
                c = NT * ph + t
                act.wait_ge(sem("scores"), c + 1)
                if not first:
                    act.wait_ge(sem("pv_done"), c - 3)
                elif ph and t < 3:
                    act.wait_ge(sem("pv_done"), c - 2)
                away = away4[0:n, s:s + 1] if ph >= 2 else 0.0
                nc.scalar.activation(p_hi[0:n, s, :], sco[0:n, s, :], ACT.Exp, scale=ATT_SCALE / PROD, bias=away)
                if not first:
                    act.wait_ge(sem("added"), c - 3)
                elif ph and t < 3:
                    act.wait_ge(sem("added"), c - 2)
                nc.scalar.activation(p_f[0:n, s, :], sco[0:n, s, :], ACT.Exp, scale=ATT_SCALE / PROD, bias=away).then_inc(sem("exps"), 1)

            def prep_split(g, t0, n, s, first=False):
                act.wait_ge(sem("prep_pool"), g + 1)
                if not first:
                    act.wait_ge(sem("ht_m"), g - 1)
                nc.scalar.copy(h_val[:, bass.ds(t0, n), C_F:C_F + D], ctx_nat[:, bass.ds(t0, n), :])
                nc.scalar.activation(pre_t[:, 0, s, 0:n, :], ctx_nat[:, bass.ds(t0, n), :], ACT.Copy, bias=SPLIT).then_inc(sem("h_hi"), 1)

            def prep_out(g, t0, n):
                act.wait_ge(sem("ht_ps"), g + 1)
                nc.scalar.copy(h_key[:, :, bass.ds(t0, n), :].rearrange("p s t d -> p s (t d)"),
                               b7[:, :].bitcast(F16).rearrange("p (s w) -> p s w", s=2)[:, :, 0:n * D]).then_inc(sem("ht_out"), 1)

            def take_away(ph, g, n=GRP):
                act.wait_ge(sem("exps"), NT * ph + g * GRP)
                nc.scalar.copy(away4[:, 0:n], ck[:, 7, bass.ds(g * GRP, n)]).then_inc(sem("away"), 1)
                act.wait_ge(sem("away"), (NG + 1) * (ph - 2) + g + 1)

            def main(ph):
                pr = ph == 0

                def trip(g, slot, static):
                    if ph >= 2:
                        take_away(ph, g)
                    for s in range(GRP):
                        i = g * GRP + s
                        exps(ph, i, s, first=static and g == 0 and (s < 3 or ph == 0))
                        if static and ph and i >= LAG:
                            if ph < 3:
                                mid(ph - 1, i - LAG)
                            else:
                                post(0, i - LAG)
                        if static and ph == 1 and i == 2:
                            prep_out(NG - 1, TAIL0 - GRP, GRP)
                        if static and ph == 1 and i == 3:
                            prep_split(NG, TAIL0, NT - TAIL0, 0)
                        if static and ph == 1 and i == 12:
                            prep_out(NG, TAIL0, NT - TAIL0)
                        if static and pr and i == 45:
                            shift(1)
                        if pr and s == 0 and not (static and g == 0):
                            prep_split(g - 1, (g - 1) * GRP, GRP, slot, first=static and g <= 2)
                        if pr and s == 2 and not (static and g <= 1):
                            prep_out(g - 2, (g - 2) * GRP, GRP)
                for g in written(ph, 0):
                    trip(g, (g + 1) % 2, True)
                if pr:
                    with act.Fori(LOOP[ph][0], LOOP[ph][1] - 1, 2) as g:
                        trip(g, 1, False)
                        trip(g + 1, 0, False)
                else:
                    with act.Fori(*LOOP[ph]) as g:
                        trip(g, None, False)
                for g in written(ph, 1):
                    trip(g, (g + 1) % 2, True)
                if ph >= 2:
                    take_away(ph, NG, NT - TAIL0)
                exps(ph, TAIL0, 0)
                if pr:
                    prep_split(NG - 1, TAIL0 - GRP, GRP, 1)
                    prep_out(NG - 2, TAIL0 - 2 * GRP, GRP)
                exps(ph, TAIL0 + 1, 1)
                exps(ph, TAIL0 + 2, 2, REST)
                if ph in (1, 2):
                    shift(ph + 1)
            def moe(h):
                def silu(t, s, first=False):
                    c = MOE_T * h + t
                    act.wait_ge(sem("cwb"), c + 1)
                    if not first:
                        act.wait_ge(sem("t2"), c - 1)
                    elif h:
                        act.wait_ge(sem("t2"), MOE_T * h)
                    nc.scalar.copy(p_f[:, s, :], acc[:, s, :])
                    act.wait_ge(sem("gate_m"), c + 1)
                    nc.scalar.activation(den[:, s, :], sco[:, s, :], ACT.Silu, scale=1.0 / PROD).then_inc(sem("silu"), 1)

                def high(t, s, first=False):
                    c = MOE_T * h + t
                    act.wait_ge(sem("t2"), c + 1)
                    if not first:
                        act.wait_ge(sem("down"), c - 1)
                    elif h:
                        act.wait_ge(sem("down"), MOE_T * h)
                    nc.scalar.copy(p_hi[:, s, :], p_f[:, 2 + s, :]).then_inc(sem("hid_hi"), 1)
                if h == 0:
                    act.wait_ge(sem("p_low"), 4 * NT - 2)
                    act.wait_ge(sem("added"), 4 * NT - 2)
                silu(0, 0, True)
                if h == 0:
                    post(1, 1)
                    for t in range(1, MOE_T):
                        silu(t, t % 2, t < 2)
                        high(t - 1, (t - 1) % 2, t <= 2)
                        if t in MOE_ACT:
                            post(1, MOE_ACT[t])
                else:
                    silu(1, 1, True)
                    high(0, 0, True)
                    silu(2, 0)
                    high(1, 1, True)
                    with act.Fori(2, MOE_T - 2, 2) as t:
                        silu(t + 1, 1)
                        high(t, 0)
                        silu(t + 2, 0)
                        high(t + 1, 1)
                high(MOE_T - 1, 0)
                act.wait_ge(sem("down"), MOE_T * h + MOE_T)
                nc.scalar.mul(opT[:, :], b7[:, :], 1.0 / (HID_SCALE * SPLIT)).then_inc(sem("yT"), 1)

            shift(0)
            for ph in range(4):
                main(ph)
            moe(0)
            moe(1)

        @block.vector
        def _(dve):
            chain = [0]
            V = nc.vector

            def link(ins):
                chain[0] += 1
                ins.then_inc(sem("v_chain"), 1)
                dve.wait_ge(sem("v_chain"), chain[0])

            def norm_a(n, src, twice=False):
                for q in range(QT):
                    last = V.bn_stats(lnst[:, q, :], src[:, q, :])
                link(last)
                for q in range(QT):
                    last = V.bn_aggr(lnmv[:, n, q, :], lnst[:, q, :])
                link(last)
                if twice:
                    V.tensor_scalar(lnve[:, n, :], lnmv[:, n, :, 1], 1.0 + LN_EPS, LN_EPS * LN_EPS, ALU.mult, ALU.add).then_inc(sem("ln_var"), 1)
                else:
                    V.tensor_scalar(lnve[:, n, :], lnmv[:, n, :, 1], LN_EPS, None, ALU.add).then_inc(sem("ln_var"), 1)

            def norm_b(n, src, dst, done=None):
                dve.wait_ge(sem("ln_inv"), n + 1)
                for q in range(QT):
                    last = V.tensor_scalar(dst[:, q, :], src[:, q, :], lnmv[:, n, q, 0:1], lnrs[:, n, q:q + 1],
                                           ALU.subtract, ALU.mult)
                if done:
                    last.then_inc(sem(done), 1)
                else:
                    link(last)

            def over(v, n=QT):
                return v.unsqueeze(1).broadcast_to([128, n, v.shape[1]])

            def low(c):
                lo, hi = CHUNKS[c]
                dve.wait_ge(sem("c_hi"), c + 1)
                V.scalar_tensor_tensor(c_val[:, lo:hi, C_L:C_L + D], ctx_nat[:, lo:hi, :], SPLIT,
                                       c_val[:, lo:hi, C_F:C_F + D], ALU.mult, ALU.subtract).then_inc(sem("c_lo"), 1)
                if c == 3:
                    V.scalar_tensor_tensor(c_val[:, FULL, C_L:C_L + D], ctx_nat[:, FULL, :], SPLIT,
                                           c_val[:, FULL, C_F:C_F + D], ALU.mult, ALU.subtract).then_inc(sem("c_lo"), 1)

            def mean(c):
                lo, hi = CHUNKS[c]
                hi = NT if c == 3 else hi
                dve.wait_ge(sem("sum_ps"), c + 1)
                V.tensor_scalar(ck[:, 0, lo:hi], b6[:, lo:hi], -1.0 / (D * SPLIT), None, ALU.mult).then_inc(sem("mean"), 1)

            def query0(h):
                dve.wait_ge(sem("q_hi"), h + 1)
                V.scalar_tensor_tensor(q_lo[:, h, :], b6[:, :], SPLIT, q_hi[:, h, :], ALU.mult, ALU.subtract).then_inc(sem("q_lo"), 1)
                dve.wait_ge(sem("c0"), h + 1)
                V.tensor_copy(cq[:, h, :], b7[:, 0:QT]).then_inc(sem("cq"), 1)

            def first_max(g):
                n = 512 if g < NG else TAILW
                for j in range(2):
                    dve.wait_ge(sem("mf_ps"), 2 * g + j + 1)
                    V.reduce_max(mx[:, 2 * j:2 * j + 2, g], sco[:, 2 * j:2 * j + 2, 0:n], axis=AX.X).then_inc(sem("mf"), 1)

            dve.wait_ge(sem("in_x"), 16)
            norm_a(0, xres[:, 0])
            norm_b(0, xres[:, 0], nrm, "n0")
            low(0)
            low(1)
            dve.wait_ge(sem("in_m"), 32)
            link(V.tensor_scalar(ck[:, 5, :], mask_i[:, :], 0.0, None, ALU.not_equal))
            V.reduce_max(small[:, 8:9], ck[:, 5, :], axis=AX.X).then_inc(sem("any"), 1)
            query0(0)
            first_max(0)
            low(2)
            first_max(1)
            low(3)
            mean(0)
            dve.wait_ge(sem("any_ps"), 1)
            V.tensor_scalar(small[:, 9:10], b7[:, 4:5], 1.0, None, ALU.min).then_inc(sem("any_sb"), 1)
            dve.wait_ge(sem("any_sb"), 1)
            link(V.tensor_scalar(small[:, 10:11], small[:, 9:10], -1.0, 1.0, ALU.mult, ALU.add))
            link(V.tensor_scalar(ck[:, 5, :], ck[:, 5, :], small[:, 10:11], None, ALU.max))
            link(V.tensor_scalar(ck[:, 6, :], ck[:, 5, :], 1.0, PEN, ALU.subtract, ALU.mult))
            link(V.tensor_scalar(ck[:, 5, :], ck[:, 5, :], SPLIT, None, ALU.mult))
            V.tensor_tensor(ck[:, 6, :], ck[:, 6, :], ck[:, 5, :], ALU.add)
            V.tensor_scalar(ck[:, 7, :], ck[:, 5, :], SPLIT, 1e30, ALU.subtract, ALU.mult).then_inc(sem("w"), 1)
            for g in range(2, NG + 1):
                first_max(g)
                if g in (2, 4, 5):
                    mean((2, 4, 5).index(g) + 1)
                if g == 2:
                    dve.wait_ge(sem("in_x1"), 16)
                    norm_a(1, xres[:, 1])
                if g == 4:
                    norm_b(1, xres[:, 1], nrm, "n0")
                if g == NG - 1:
                    query0(1)

            def consts(part):
                if part == 0:
                    dve.wait_ge(sem("in_u"), 16 * 13)
                    dve.wait_ge(sem("tg"), 1)
                    link(V.tensor_tensor(scr[:, 0:3, :], us[:, :, :], over(avg[:, 3, :], 3), ALU.mult))
                elif part == 1:
                    link(V.reduce_sum(bcols[:, 0:3], scr[:, 0:3, :], axis=AX.X))
                elif part == 2:
                    link(V.tensor_tensor(bcols[:, 0:3], bcols[:, 0:3], cols[:, 2:5], ALU.add))
                    V.tensor_scalar(bcols[:, 3:4], C["L0_ffn_in_c"], 0.5, None, ALU.mult)
                    V.tensor_scalar(bcols[:, 0:2], bcols[:, 0:2], 0.5, None, ALU.mult).then_inc(sem("gate_bias"), 1)
                else:
                    h = part - 3
                    V.scalar_tensor_tensor(xres[:, h], over(R["L0_xattn_bv"]), tg[:, 0:1], xres[:, h], ALU.mult, ALU.add).then_inc(sem("consts"), 1)

            def low_p(ph, t, s, n=D):
                c = NT * ph + t
                dve.wait_ge(sem("exps"), c + 1)
                V.tensor_tensor(p_lo[0:n, s, :], p_f[0:n, s, :], p_hi[0:n, s, :], ALU.subtract).then_inc(sem("p_low"), 1)

            def max_g(c, g, j, bank, n=512):
                dve.wait_ge(sem("mx_ps"), c + 1)
                V.reduce_max(mx[:, j, bass.ds(g, 1)], bank[:, 0:n], axis=AX.X).then_inc(sem("mx"), 1)

            def prep_low(g, t0, n, s):
                dve.wait_ge(sem("h_hi"), g + 1)
                V.tensor_tensor(h_val[:, bass.ds(t0, n), C_L:C_L + D], ctx_nat[:, bass.ds(t0, n), :],
                                h_val[:, bass.ds(t0, n), C_F:C_F + D], ALU.subtract)
                V.scalar_tensor_tensor(pre_t[:, 1, s, 0:n, :], ctx_nat[:, bass.ds(t0, n), :], SPLIT, pre_t[:, 0, s, 0:n, :],
                                       ALU.add, ALU.subtract).then_inc(sem("prep_split"), 1)

            def hm_out(g, t0, n):
                dve.wait_ge(sem("ht_m"), g + 1)
                V.tensor_copy(h_max[:, bass.ds(t0, n), :].rearrange("p t d -> p (t d)"),
                              b7[:, :].bitcast(F16)[:, 0:n * D]).then_inc(sem("hm_done"), 1)

            def main(ph):
                pr = ph == 0

                def trip(g, slot, static):
                    for s in range(GRP):
                        i = g * GRP + s
                        low_p(ph, i + 1, (s + 1) % GRP)
                        if static and ph in (1, 2) and i + 1 >= LAG:
                            mid(ph - 1, i + 1 - LAG)
                        c, todo = mx_plan(ph, i) if static else mx_loop(ph, g, s)
                        for m, (gk, j) in enumerate(todo):
                            tail = static and gk == NG
                            max_g(c + m, gk, j, b6 if pr else bk[m % 2 if not static else (c + m) % 2], TAILW if tail else 512)
                        if pr and s == 2 and not (static and g <= 1):
                            hm_out(g - 2, (g - 2) * GRP, GRP)
                        if pr and s == 1 and not (static and g == 0):
                            prep_low(g - 1, (g - 1) * GRP, GRP, slot)
                        if static and pr and i == 41:
                            shift(1, 0)
                        if static and pr and i == 46:
                            shift(1, 1)
                        if static and ph in (1, 2):
                            if ph == 1 and i == 4:
                                hm_out(NG - 1, TAIL0 - GRP, GRP)
                            if ph == 1 and i == 5:
                                prep_low(NG, TAIL0, NT - TAIL0, 0)
                            if ph == 1 and i == 14:
                                hm_out(NG, TAIL0, NT - TAIL0)
                            if i == 45:
                                shift(ph + 1, 0)
                        if static and ph == 3 and i + 1 >= LAG:
                            post(0, i + 1 - LAG)
                        if ph == 3 and (static and 21 <= i < 24 or not static and s < CW):
                            w = i - 21 if static else s
                            t0 = 0 if static else (g - LOOP[3][0] + 1) * CW
                            if static:
                                dve.wait_ge(sem(f"in_w{w}"), 48)
                            V.tensor_scalar(MOE_W[w][:, 0, bass.ds(t0, CW), :], stage[w][:, bass.ds(t0, CW), :], SPLIT, None,
                                            ALU.mult).then_inc(sem("w_hi"), 1)
                            dve.wait_ge(sem("w_hi"), (0 if static else (g - LOOP[3][0] + 1) * CW) + w + 1)
                            V.scalar_tensor_tensor(MOE_W[w][:, 1, bass.ds(t0, CW), :], stage[w][:, bass.ds(t0, CW), :], SPLIT,
                                                   MOE_W[w][:, 0, bass.ds(t0, CW), :], ALU.mult, ALU.subtract).then_inc(sem("split_w"), 1)
                low_p(ph, 0, 0)
                for g in written(ph, 0):
                    trip(g, (g + 1) % 2, True)
                if pr:
                    with dve.Fori(LOOP[ph][0], LOOP[ph][1] - 1, 2) as g:
                        trip(g, 1, False)
                        trip(g + 1, 0, False)
                else:
                    with dve.Fori(*LOOP[ph]) as g:
                        trip(g, None, False)
                for g in written(ph, 1):
                    trip(g, (g + 1) % 2, True)
                low_p(ph, TAIL0 + 1, 1)
                if pr:
                    prep_low(NG - 1, TAIL0 - GRP, GRP, 1)
                low_p(ph, TAIL0 + 2, 2, REST)
                if pr:
                    hm_out(NG - 2, (NG - 2) * GRP, GRP)
                if ph in (1, 2):
                    shift(ph + 1, 1)

            def shift(ph, part):
                h, L = ph % 2, ph // 2
                if part == 0:
                    if ph:
                        dve.wait_ge(sem("mx"), 4 * (NG + 1) * ph)
                    else:
                        dve.wait_ge(sem("mf"), 2 * (NG + 1))
                    link(V.reduce_max(small[:, 0:4], mx[:, :, :], axis=AX.X))
                    if L:
                        link(V.tensor_scalar(small[:, 0:4], small[:, 0:4], 1.0 / PROD, -float(D), ALU.mult, ALU.add))
                        link(V.scalar_tensor_tensor(small[:, 0:4], small[:, 0:4], small[:, 9:10], cq[:, h, :], ALU.mult, ALU.add))
                    else:
                        link(V.scalar_tensor_tensor(small[:, 0:4], small[:, 0:4], 1.0 / PROD, cq[:, h, :], ALU.mult, ALU.add))
                    link(V.tensor_tensor(small[:, 4:8], cq[:, h, :], small[:, 0:4], ALU.subtract))
                    link(V.tensor_scalar(small[:, 4:8], small[:, 4:8], P_LOG, 1.0 / D if L else 1.0, ALU.add, ALU.mult))
                    for q in range(QT):
                        last = V.tensor_scalar(scr[:, q, :], ident[:, :], small[:, 4 + q:5 + q], None, ALU.mult)
                    last.then_inc(sem("dg"), 1)
                elif L:
                    dve.wait_ge(sem("m_ps"), ph + 1)
                    V.tensor_tensor(opT[:, :], b6[:, :], qg[:, h, :], ALU.add).then_inc(sem("g1"), 1)
                    dve.wait_ge(sem("q_hi"), ph + 1)
                    V.scalar_tensor_tensor(q_lo[:, h, :], opT[:, :], SPLIT, q_hi[:, h, :], ALU.mult, ALU.subtract).then_inc(sem("q_lo"), 1)
                else:
                    dve.wait_ge(sem("aug_hi"), ph + 1)
                    V.tensor_tensor(aug[64:128, ph, :], b6[64:128, :], aug[64:128, ph, :], ALU.subtract).then_inc(sem("aug"), 1)

            def rows_of(bank):
                return bank[:, :].rearrange("p (t d) -> p t d", t=QT)

            def inverse(ph):
                dve.wait_ge(sem("den_ps"), ph + 1)
                V.reciprocal(small[:, 16:20], b6[:, 0:QT]).then_inc(sem("den_sb"), 1)
                dve.wait_ge(sem("den_sb"), ph + 1)

            def over_den(bank):
                link(V.tensor_tensor(scr[:, :, :], rows_of(bank), small[:, 16:20].unsqueeze(2).broadcast_to([128, QT, D]), ALU.mult))

            def mid(h, i):
                if h == 0 and i in (0, 2, 4, 7):
                    consts({0: 0, 2: 3, 4: 2, 7: 4}[i])
                elif i == 1:
                    inverse(h)
                    if h == 0:
                        consts(1)
                elif i == 3:
                    dve.wait_ge(sem("o_ps"), h + 1)
                    dve.wait_ge(sem("consts"), h + 1)
                    over_den(b6)
                    link(V.scalar_tensor_tensor(xres[:, h], scr[:, :, :], tg[:, 0:1], xres[:, h], ALU.mult, ALU.add))
                    norm_a(2 + 2 * h, xres[:, h])
                elif i == 5:
                    norm_b(2 + 2 * h, xres[:, h], nrm, "n1")
                elif i == 8:
                    dve.wait_ge(sem("gate"), 3 * h + 3)
                    dve.wait_ge(sem("gate_bias"), 1)
                    link(V.tensor_scalar(gt[:, 0, :], gt[:, 0, :], 1.0, bcols[:, 3:4], ALU.add, ALU.mult))
                    link(V.scalar_tensor_tensor(gt[:, 1, :], gt[:, 1, :], 1.0, gt[:, 2, :], ALU.add, ALU.mult))
                    V.scalar_tensor_tensor(opT2[:, :], gt[:, 1, :], 0.5, gt[:, 0, :], ALU.mult, ALU.add).then_inc(sem("cell"), 1)
                elif i == 10:
                    dve.wait_ge(sem("ffn_ps"), h + 1)
                    V.tensor_tensor(scr[:, :, :], rows_of(b6), over(R["L0_ffn_bo"]), ALU.add).then_inc(sem("f_sum"), 1)
                elif i == 11:
                    dve.wait_ge(sem("f_tanh"), h + 1)
                    link(V.scalar_tensor_tensor(xres[:, h], avg[:, :, :], tg[:, 2:3], xres[:, h], ALU.mult, ALU.add))
                    norm_a(3 + 2 * h, xres[:, h], twice=True)
                elif i == 13:
                    norm_b(3 + 2 * h, xres[:, h], avg, "n2")
                elif i == 19:
                    dve.wait_ge(sem("qc"), h + 1)
                    V.tensor_copy(cq[:, h, :], b7[:, 0:QT])
                    V.tensor_scalar(qg[:, h, :], b6[:, :], small[:, 9:10], None, ALU.mult).then_inc(sem("qc_sb"), 1)

            def post(h, i):
                if i == 0 and h == 0:
                    V.tensor_scalar(avg[:, 0, :], ones[:, :], C["L1_xattn_ln_a_b"], None, ALU.mult).then_inc(sem("shift_rows"), 1)
                    link(V.tensor_scalar(R["L1_xattn_ln_p_b"], R["L1_xattn_ln_p_b"], tg[:, 1:2], None, ALU.mult))
                elif i == 1:
                    inverse(2 + h)
                    if h == 0:
                        dve.wait_ge(sem("bias_ps"), 1)
                        link(V.tensor_tensor(R["L1_xattn_bv"], R["L1_xattn_bv"], b7[:, 0:D], ALU.add))
                elif i == 2:
                    link(V.tensor_tensor(xres[:, h], xres[:, h], over(R["L1_xattn_ln_p_b"]), ALU.add))
                elif i == 3:
                    dve.wait_ge(sem("o1_ps"), h + 1)
                    over_den(b6)
                    link(V.tensor_tensor(scr[:, :, :], scr[:, :, :], over(R["L1_xattn_bv"]), ALU.add))
                elif i == 4:
                    norm_a(6 + 2 * h, scr)
                elif i == 5:
                    norm_b(6 + 2 * h, scr, nrm)
                elif i == 6:
                    link(V.scalar_tensor_tensor(nrm[:, :, :], nrm[:, :, :], tg[:, 1:2], over(R["L1_xattn_ln_p_g"]), ALU.mult, ALU.mult))
                elif i == 7:
                    link(V.tensor_tensor(xres[:, h], nrm[:, :, :], xres[:, h], ALU.add))
                elif i == 8:
                    norm_a(7 + 2 * h, xres[:, h])
                elif i == 10:
                    norm_b(7 + 2 * h, xres[:, h], nrm, "n3")
                elif i == 13:
                    dve.wait_ge(sem("x3_hi"), h + 1)
                    V.scalar_tensor_tensor(q_lo[:, h, :], opT[:, :], SPLIT, q_hi[:, h, :], ALU.mult, ALU.subtract).then_inc(sem("x3_lo"), 1)
                elif 15 <= i <= 20:
                    route(h, i - 15)
                elif i == 22:
                    dve.wait_ge(sem("cw_hi"), h + 1)
                    V.scalar_tensor_tensor(cw16[64:128, h, :], b6[0:64, :], CW_SCALE, cw16[0:64, h, :], ALU.mult, ALU.subtract).then_inc(sem("cw_lo"), 1)

            def wide(v, n):
                return v.unsqueeze(3).broadcast_to([128, QT, v.shape[2], n])

            def route(h, part):
                sc, sb_, m, gtv, eq, pre, pick, top = (rt[:, i, :, :] for i in range(8))

                def nth(i):
                    return r8[:, :, i:i + 1].broadcast_to([128, QT, NE])

                def place(eqv, out):
                    link(V.tensor_tensor_scan(out.rearrange("p t e -> p (t e)"), seg[:, :],
                                              eqv.rearrange("p t e -> p (t e)"), 0.0, ALU.mult, ALU.add))
                def group_max(tiles):
                    for q in tiles:
                        for g in range(4):
                            last = V.max(g8[:, q, g, :], rt[:, 1, q, 8 * g:8 * g + 8])
                    return last

                def v4(i):
                    return gp[:, i].rearrange("p t (i j) -> p t i j", i=4)
                if part == 0:
                    dve.wait_ge(sem("lg_t"), h + 1)
                    link(V.tensor_scalar(sc, sc, 0.5, 0.5, ALU.mult, ALU.add))
                    link(V.tensor_tensor(sb_, sc, over(gbias[:, :]), ALU.add))
                    group_max(range(0, QT // 2))
                elif part == 1:
                    link(group_max(range(QT // 2, QT)))
                    link(V.tensor_tensor(gs[:, 0], g8[:, :, :, 0], g8[:, :, :, 1], ALU.add))
                    mine = gs[:, 0].unsqueeze(3).broadcast_to([128, QT, 4, 4])
                    other = gs[:, 0].unsqueeze(2).broadcast_to([128, QT, 4, 4])
                    V.tensor_tensor(v4(0), other, mine, ALU.is_gt)
                    link(V.tensor_tensor(v4(1), other, mine, ALU.is_equal))
                    link(V.tensor_tensor(gp[:, 1], gp[:, 1], over(lt4[:, :]), ALU.mult))
                    link(V.tensor_tensor(gp[:, 0], gp[:, 0], gp[:, 1], ALU.add))
                elif part == 2:
                    link(V.reduce_sum(gs[:, 1], v4(0), axis=AX.X))
                    link(V.tensor_scalar(gs[:, 2], gs[:, 1], 1.5, None, ALU.is_lt))
                    link(V.tensor_scalar(gs[:, 3], gs[:, 2], 1.0, 1e30, ALU.subtract, ALU.mult))
                    link(V.tensor_tensor(m.rearrange("p t (g e) -> p t g e", g=4), sb_.rearrange("p t (g e) -> p t g e", g=4),
                                         wide(gs[:, 3], 8), ALU.add))
                    for q in range(QT):
                        last = V.max(r8[:, q, :], rt[:, 2, q, :])
                    link(last)
                elif part == 3:
                    V.tensor_tensor(gtv, m, nth(TOPK - 1), ALU.is_gt)
                    V.tensor_tensor(top, m, nth(0), ALU.is_equal)
                    link(V.tensor_tensor(eq, m, nth(TOPK - 1), ALU.is_equal))
                    link(V.reduce_sum(gs[:, 4, :, 0], gtv, axis=AX.X))
                    place(eq, pre)
                elif part == 4:
                    link(V.tensor_tensor(pre, pre, gs[:, 4, :, 0:1].broadcast_to([128, QT, NE]), ALU.add))
                    link(V.scalar_tensor_tensor(pre, pre, TOPK + 0.5, eq, ALU.is_lt, ALU.mult))
                    link(V.tensor_tensor(pick, gtv, pre, ALU.add))
                    link(V.tensor_tensor(pick, pick, sc, ALU.mult))
                    link(V.reduce_sum(gs[:, 5, :, 0], pick, axis=AX.X))
                else:
                    link(V.tensor_scalar(gs[:, 5, :, 0], gs[:, 5, :, 0], 1e-20, None, ALU.add))
                    link(V.reciprocal(gs[:, 5, :, 1], gs[:, 5, :, 0]))
                    link(V.tensor_scalar(gs[:, 5, :, 1], gs[:, 5, :, 1], ROUTED_SCALE, None, ALU.mult))
                    if h == 0:
                        dve.wait_ge(sem("coef1"), 1)
                    V.tensor_tensor(coef[:, :, 0:NE], pick, gs[:, 5, :, 1:2].broadcast_to([128, QT, NE]), ALU.mult)
                    place(top, pre)
                    link(V.scalar_tensor_tensor(pre, pre, 1.5, top, ALU.is_lt, ALU.mult))
                    pairs = pre.rearrange("p t (a b) -> p t a b", b=2)
                    link(V.tensor_tensor(coef[:, :, NE:NE + NA], pairs[:, :, :, 0], pairs[:, :, :, 1], ALU.add))
                    V.tensor_scalar(coef[:, :, NE:NE + NA], coef[:, :, NE:NE + NA], ANCHOR_ALPHA, None, ALU.mult).then_inc(sem("coef"), 1)

            def moe(h):
                def slot(name, t, first):
                    if not first:
                        dve.wait_ge(sem(name), MOE_T * h + t - 1)
                    elif h:
                        dve.wait_ge(sem(name), MOE_T * h)

                def t1(t, s):
                    dve.wait_ge(sem("silu"), MOE_T * h + t + 1)
                    V.tensor_tensor(den[:, s, :], den[:, s, :], p_f[:, s, :], ALU.mult).then_inc(sem("t1"), 1)

                def t2(t, s, first=False):
                    dve.wait_ge(sem("t1"), MOE_T * h + t + 1)
                    dve.wait_ge(sem("up"), MOE_T * h + t + 1)
                    slot("hid_lo", t, first)
                    V.scalar_tensor_tensor(p_f[:, 2 + s, :], sco[:, 2 + s, :], HID_SCALE / (PROD * CW_SCALE), den[:, s, :],
                                           ALU.mult, ALU.mult).then_inc(sem("t2"), 1)
                if h == 0:
                    dve.wait_ge(sem("added"), 4 * NT)
                    for t in range(MOE_T):
                        t1(t, t % 2)
                        t2(t, t % 2, t < 2)
                        if t == 0:
                            post(1, 1)
                        if t in MOE_DVE:
                            for i in MOE_DVE[t]:
                                post(1, i)
                    post(1, 22)
                else:
                    for t in range(2):
                        t1(t, t)
                        t2(t, t, True)
                    with dve.Fori(2, MOE_T - 2, 2) as t:
                        t1(t, 0)
                        t2(t, 0)
                        t1(t + 1, 1)
                        t2(t + 1, 1)
                    t1(MOE_T - 1, 0)
                    t2(MOE_T - 1, 0)
                dve.wait_ge(sem("y_ps"), h + 1)
                V.scalar_tensor_tensor(xres[:, h], rows_of(b6), tg[:, 3:4], xres[:, h], ALU.mult, ALU.add).then_inc(sem("y_out"), 1)

            shift(0, 0)
            shift(0, 1)
            for ph in range(4):
                main(ph)
            moe(0)
            moe(1)

        @block.tensor
        def _(pe):
            T = nc.tensor

            def transp4(dst, src, done, n=128):
                for q in range(QT):
                    last = T.transpose(dst[0:n, q * D:(q + 1) * D], src[:, q, :], ident[:, :])
                last.then_inc(sem(done), 1)

            def turn(g):
                n = min(GRP, NT - g * GRP)
                c = sum(g >= hi for _, hi in GROUPS)
                pe.wait_ge(sem("c_lo"), c + 1 if c < 3 else 5)
                if g >= 2:
                    pe.wait_ge(sem("ct_out"), g - 1)
                for half, c0 in ((0, C_F), (1, C_L)):
                    for j in range(n):
                        last = T.transpose(acc[:, g % 2, :].bitcast(F16)[:, half * 512 + j * D:half * 512 + (j + 1) * D],
                                           c_val[:, g * GRP + j, c0:c0 + D], ident16[:, :])
                last.then_inc(sem("ct_ps"), 1)

            def sums(c):
                lo, hi = CHUNKS[c]
                pe.wait_ge(sem("ct_out"), GROUPS[c][1])
                if c:
                    pe.wait_ge(sem("mean"), c)
                for t in range(lo, NT if c == 3 else hi):
                    T.matmul(b6[:, t:t + 1], c_key[:, 0, t, :], ones16[:, :], start=True, stop=False)
                    last = T.matmul(b6[:, t:t + 1], c_key[:, 1, t, :], ones16[:, :], start=False, stop=True)
                last.then_inc(sem("sum_ps"), 1)

            def query0(h, part):
                if part == 0:
                    pe.wait_ge(sem("n0"), h + 1)
                    if h:
                        pe.wait_ge(sem("mean"), 4)
                        pe.wait_ge(sem("cq"), 1)
                    transp4(b6, nrm, "t0")
                elif part == 1:
                    pe.wait_ge(sem("t0_sb"), h + 1)
                    T.matmul(b7[:, :], W["L0_xattn_Wq"], opT[:, :], start=True, stop=True).then_inc(sem("q0"), 1)
                else:
                    pe.wait_ge(sem("q0_sb"), h + 1)
                    T.matmul(b6[:, :], wk0[:, :], qT[:, :], start=True, stop=True).then_inc(sem("k0"), 1)
                    if h == 0:
                        pe.wait_ge(sem("in_bk"), 16)
                    for q in range(QT):
                        last = T.matmul(b7[:, q:q + 1], qT[:, q * D:(q + 1) * D], C["L0_xattn_bk"], start=True, stop=True)
                    last.then_inc(sem("c0"), 1)

            def first_max(g):
                n = 512 if g < NG else TAILW
                if g == 0:
                    pe.wait_ge(sem("q_hi"), 1)
                pe.wait_ge(sem("ct_out"), g + 1)
                for j in range(2):
                    if g:
                        pe.wait_ge(sem("mf"), 2 * g + j - 1)
                    for q in (2 * j, 2 * j + 1):
                        last = T.matmul(sco[:, q, 0:n], q_hi[:, 0, q * D:(q + 1) * D],
                                        c_key[:, 0, g * GRP:min(NT, g * GRP + GRP), :].rearrange("p t d -> p (t d)")[:, 0:n],
                                        start=True, stop=True)
                    last.then_inc(sem("mf_ps"), 1)

            pe.wait_ge(sem("in_id"), 16)
            pe.wait_ge(sem("in_q"), 16)
            T.transpose(b7[:, 0:D], wraw[:, 0, :], ident[:, :]).then_inc(sem("wq_ps"), 1)
            pe.wait_ge(sem("wq_sb"), 1)
            query0(0, 0)
            query0(0, 1)
            pe.wait_ge(sem("id16"), 1)
            turn(0)
            pe.wait_ge(sem("in_k0"), 16)
            query0(0, 2)
            turn(1)
            first_max(0)
            turn(2)
            turn(3)
            first_max(1)
            turn(4)
            turn(5)
            pe.wait_ge(sem("set"), 1)
            pe.wait_ge(sem("any"), 1)
            pe.wait_ge(sem("cq"), 1)
            T.matmul(b7[:, 4:5], ones[:, :], small[:, 8:9], start=True, stop=True).then_inc(sem("any_ps"), 1)
            pe.wait_ge(sem("q_lo"), 1)
            sums(0)
            first_max(2)
            turn(6)
            turn(7)
            turn(8)
            sums(1)
            first_max(3)
            turn(9)
            turn(10)
            first_max(4)
            turn(11)
            turn(12)
            sums(2)
            first_max(5)
            sums(3)
            for g in range(6, NG + 1):
                first_max(g)
                if g == 6:
                    pe.wait_ge(sem("in_w"), 16 * len(WNAMES))
                    for i in range(1, len(WNAMES)):
                        T.transpose(acc[:, (i - 1) // 4, ((i - 1) % 4) * D:((i - 1) % 4 + 1) * D], wraw[:, i, :], ident[:, :])
                    T.transpose(acc[:, 1, 3 * D:3 * D + NE], gw[:, :], ident[0:NE, 0:NE]).then_inc(sem("wT_ps"), 1)
                if g == 7:
                    pe.wait_ge(sem("any_sb"), 1)
                    query0(1, 0)
                if g == 9:
                    query0(1, 1)
                if g == 10:
                    query0(1, 2)

            def max_mm(ph, c, g, j, bank, two, static, n=512):
                if ph or not static or c:
                    pe.wait_ge(sem("mx"), c - 1 if two else c)
                keys, qs = (c_key[:, 0], q_hi) if ph == 0 else (h_max, qm)
                T.matmul(bank[:, 0:n], qs[:, (ph + 1) % 2, j * D:(j + 1) * D],
                         keys[:, bass.ds(g * GRP, GRP), :].rearrange("p t d -> p (t d)") if n == 512 else
                         keys[:, TAIL0:NT, :].rearrange("p t d -> p (t d)")[:, 0:n],
                         start=True, stop=True).then_inc(sem("mx_ps"), 1)

            def first_scores(t):
                if t == 0:
                    pe.wait_ge(sem("q_lo"), 1)
                pe.wait_ge(sem("mf"), 2 * NG + t // 2 + 1)
                T.matmul(sco[:, t, :], c_key[:, 0, t, :], q_hi[:, 0, :], start=True, stop=False)
                T.matmul(sco[:, t, :], c_key[:, 0, t, :], q_lo[:, 0, :], start=False, stop=False)
                T.matmul(sco[:, t, :], c_key[:, 1, t, :], q_hi[:, 0, :], start=False, stop=False)

            def scores(ph, t, s, first=False):
                c = NT * ph + t
                L, h = ph // 2, ph % 2
                if not first:
                    pe.wait_ge(sem("exps"), c - 3)
                elif ph and t < 3:
                    pe.wait_ge(sem("exps"), c - 2)
                kk = h_key if L else c_key
                if L == 0:
                    T.matmul(sco[:, s, :], augw[:, :], aug[:, ph, :], start=True, stop=False)
                T.matmul(sco[:, s, :], kk[:, 0, t, :], q_hi[:, h, :], start=bool(L), stop=False)
                T.matmul(sco[:, s, :], kk[:, 0, t, :], q_lo[:, h, :], start=False, stop=False)
                T.matmul(sco[:, s, :], kk[:, 1, t, :], q_hi[:, h, :], start=False, stop=True).then_inc(sem("scores"), 1)

            def pv(ph, t, s, n=D, start=False, stop=False):
                pe.wait_ge(sem("p_low"), NT * ph + t + 1)
                if start and ph >= 2:
                    pe.wait_ge(sem("av_done"), ph - 1)
                val = h_val if ph // 2 else c_val
                out = acc[:, ph % 2, :]
                T.matmul(out, val[0:n, t, C_F:C_F + D], p_hi[0:n, s, :], start=start, stop=False)
                T.matmul(out, val[0:n, t, C_F:C_F + D], p_lo[0:n, s, :], start=False, stop=False)
                T.matmul(out, val[0:n, t, C_L:C_L + D], p_hi[0:n, s, :], start=False, stop=stop).then_inc(sem("pv_done"), 1)

            def denominators(ph):
                pe.wait_ge(sem("added"), NT * (ph + 1))
                for q in range(QT):
                    last = T.matmul(b6[:, q:q + 1], den[:, ph % 2, q * D:(q + 1) * D], split_col[:, :], start=True, stop=True)
                last.then_inc(sem("den_ps"), 1)

            def turn_h(g, s, n, m):
                if m == 0:
                    pe.wait_ge(sem("prep_split"), g + 1)
                else:
                    pe.wait_ge(sem("ht_out"), g + 1)
                    pe.wait_ge(sem("prep_m"), g + 1)
                for half in ((0, 1) if m == 0 else (2,)):
                    for j in range(n):
                        o = (half % 2) * 512 + j * D
                        last = T.transpose(b7[:, :].bitcast(F16)[:, o:o + D], pre_t[:, half, s, j, :], ident16[:, :])
                last.then_inc(sem("ht_ps" if m == 0 else "ht_m"), 1)

            def shift(ph):
                pe.wait_ge(sem("dg"), ph + 1)
                if ph == 0:
                    pe.wait_ge(sem("q_lo"), 2)
                T.matmul(b6[:, :], ones[:, :], scr[:, :, :].rearrange("p t d -> p (t d)"), start=True,
                         stop=True).then_inc(sem("m_ps"), 1)

            def main(ph):
                pr = ph == 0

                def trip(g, slot, static):
                    for s in range(GRP):
                        i = g * GRP + s
                        scores(ph, i + 3, (s + 3) % GRP, first=static and i == 0 and ph == 0)
                        c, todo = mx_plan(ph, i) if static else mx_loop(ph, g, s)
                        if static and ph in (1, 2) and i == 22:
                            pe.wait_ge(sem("qm"), ph)
                            pe.wait_ge(sem("hm_done"), NG + 1)

                        def one(m):
                            gk, j = todo[m]
                            tail = static and gk == NG
                            max_mm(ph, c + m, gk, j, b6 if pr else bk[m % 2 if not static else (c + m) % 2], not pr, static,
                                   TAILW if tail else 512)
                        for m in range(1 if pr else 2):
                            if m < len(todo):
                                one(m)
                        pv(ph, i, s, start=static and i == 0)
                        if len(todo) > (1 if pr else 2):
                            one(len(todo) - 1)
                        if pr:
                            if s == 1 and not (static and g <= 1):
                                turn_h(g - 2, 1 - slot, GRP, 1)
                            if s == 3 and not (static and g == 0):
                                if not (static and g == 1):
                                    pe.wait_ge(sem("hm_done"), g - 1)
                                turn_h(g - 1, slot, GRP, 0)
                            if static and i == 42:
                                shift(1)
                        elif static and ph < 3:
                            mid(ph - 1, i)
                            if ph == 1 and i == 3:
                                turn_h(NG - 1, 1, GRP, 1)
                            if ph == 1 and i == 10:
                                turn_h(NG, 0, NT - TAIL0, 0)
                            if ph == 1 and i == 12:
                                turn_h(NG, 0, NT - TAIL0, 1)
                            if i == 46:
                                shift(ph + 1)
                        elif static:
                            post(0, i)

                def ahead(t):
                    if t == 0:
                        if ph + 1 < 2:
                            pe.wait_ge(sem("aug"), ph + 2)
                        else:
                            pe.wait_ge(sem("q_lo"), ph + 2)
                    scores(ph + 1, t, t, first=True)

                if pr:
                    pe.wait_ge(sem("wT"), 1)
                    pe.wait_ge(sem("aug"), 1)
                    for t in range(3):
                        T.matmul(sco[:, t, :], augw[:, :], aug[:, 0, :], start=False, stop=True).then_inc(sem("scores"), 1)
                for g in written(ph, 0):
                    trip(g, (g + 1) % 2, True)
                if pr:
                    with pe.Fori(LOOP[ph][0], LOOP[ph][1] - 1, 2) as g:
                        trip(g, 1, False)
                        trip(g + 1, 0, False)
                else:
                    with pe.Fori(*LOOP[ph]) as g:
                        trip(g, None, False)
                for g in written(ph, 1):
                    trip(g, (g + 1) % 2, True)
                pv(ph, TAIL0, 0)
                if pr:
                    ahead(0)
                pv(ph, TAIL0 + 1, 1)
                if pr:
                    turn_h(NG - 2, 0, GRP, 1)
                    ahead(1)
                if ph == 3:
                    pe.wait_ge(sem("exps"), 4 * NT)
                    pe.wait_ge(sem("split_w"), MOE_T)
                    pe.wait_ge(sem("in_k"), 48)
                    pe.wait_ge(sem("cw_lo"), 1)
                    gu(0, 0, 0, True)
                pv(ph, TAIL0 + 2, 2, REST, stop=True)
                if ph in (1, 2):
                    ahead(0)
                    ahead(1)
                if ph < 3:
                    ahead(2)
                if pr:
                    pe.wait_ge(sem("hm_done"), NG - 1)
                    turn_h(NG - 1, 1, GRP, 0)

            def mid(h, i):
                if i == 1:
                    denominators(h)
                elif i == 3:
                    pe.wait_ge(sem("av_done"), h + 1)
                    pe.wait_ge(sem("den_sb"), h + 1)
                    for q in range(QT):
                        last = T.matmul(b6[:, q * D:(q + 1) * D], opT[:, q * D:(q + 1) * D], W["L0_xattn_Wv"], start=True, stop=True)
                    last.then_inc(sem("o_ps"), 1)
                elif i == 6:
                    pe.wait_ge(sem("n1"), h + 1)
                    transp4(b6, nrm, "nT")
                elif i == 7:
                    pe.wait_ge(sem("nT_sb"), h + 1)
                    if h == 0:
                        pe.wait_ge(sem("hm_done"), NG)
                    for i, n in enumerate(("wf", "wi")):
                        T.matmul(bk[(i + 1) % 2][:, :], W["L0_ffn_" + n], opT[:, :], start=True, stop=True).then_inc(sem("gate_ps"), 1)
                elif i == 8:
                    pe.wait_ge(sem("gate"), 3 * h + 1)
                    T.matmul(b7[:, :], W["L0_ffn_wc"], opT[:, :], start=True, stop=True).then_inc(sem("gate_ps"), 1)
                elif i == 10:
                    pe.wait_ge(sem("cell"), h + 1)
                    for q in range(QT):
                        o = b6[:, q * D:(q + 1) * D]
                        T.matmul(o, opT[:, q * D:(q + 1) * D], W["L0_ffn_wo"], start=True, stop=False)
                        last = T.matmul(o, opT2[:, q * D:(q + 1) * D], W["L0_ffn_uo"], start=False, stop=True)
                    last.then_inc(sem("ffn_ps"), 1)
                elif i == 15:
                    pe.wait_ge(sem("n2"), h + 1)
                    transp4(b6, avg, "tT")
                elif i == 16:
                    pe.wait_ge(sem("tT_sb"), h + 1)
                    T.matmul(b7[:, :], wq1[:, :], opT[:, :], start=True, stop=True).then_inc(sem("q1"), 1)
                elif i == 17:
                    pe.wait_ge(sem("q1_sb"), h + 1)
                    T.matmul(b6[:, :], W["L1_xattn_Wk"], qT[:, :], start=True, stop=True).then_inc(sem("g0"), 1)
                elif i == 19:
                    pe.wait_ge(sem("g0_sb"), h + 1)
                    for q in range(QT):
                        T.matmul(b7[:, q:q + 1], opT[:, q * D:(q + 1) * D], C["L1_xattn_ln_a_b"], start=True, stop=False)
                        T.matmul(b7[:, q:q + 1], qT[:, q * D:(q + 1) * D], C["L1_xattn_bk"], start=False, stop=True)
                    T.matmul(b6[:, :], cent[:, :], opT2[:, :], start=True, stop=True).then_inc(sem("qc"), 1)

            def post(h, i):
                if i == 0:
                    if h:
                        pe.wait_ge(sem("cw_lo"), 1)
                    denominators(2 + h)
                elif i == 1 and h == 0:
                    pe.wait_ge(sem("shift_rows"), 1)
                    T.matmul(b7[:, 0:D], avg[:, 0, :], wv1[:, :], start=True, stop=True).then_inc(sem("bias_ps"), 1)
                elif i == 3:
                    pe.wait_ge(sem("av_done"), 3 + h)
                    pe.wait_ge(sem("den_sb"), 3 + h)
                    for q in range(QT):
                        last = T.matmul(b6[:, q * D:(q + 1) * D], opT[:, q * D:(q + 1) * D], wv1[:, :], start=True, stop=True)
                    last.then_inc(sem("o1_ps"), 1)
                elif i == 12:
                    pe.wait_ge(sem("n3"), h + 1)
                    transp4(b6, nrm, "n3T")
                elif i == 13:
                    pe.wait_ge(sem("x3_hi"), h + 1)
                    for q in range(QT):
                        last = T.matmul(b6[:, q * NE:(q + 1) * NE], opT[:, q * D:(q + 1) * D], gwT[:, :], start=True, stop=True)
                    last.then_inc(sem("lg"), 1)
                elif i == 22:
                    pe.wait_ge(sem("coef"), h + 1)
                    transp4(b6, coef, "cwT", 64)

            def gu(h, t, s, first=False):
                c = MOE_T * h + t
                before = MOE_T * h if first else c - 1
                if h or not first:
                    pe.wait_ge(sem("silu"), before)
                T.matmul(acc[:, s, :], sel[:, t, :], cw16[:, h, :], start=True, stop=True).then_inc(sem("cwb"), 1)
                for w, out, done in ((moe_g, sco[:, s, :], "gate_m"), (moe_u, sco[:, 2 + s, :], "up")):
                    if done == "up" and (h or not first):
                        pe.wait_ge(sem("t2"), before)
                    T.matmul(out, w[:, 0, t, :], q_hi[:, h, :], start=True, stop=False)
                    T.matmul(out, w[:, 0, t, :], q_lo[:, h, :], start=False, stop=False)
                    T.matmul(out, w[:, 1, t, :], q_hi[:, h, :], start=False, stop=True).then_inc(sem(done), 1)

            def moe(h):
                def down(t, s, start=False, stop=False):
                    pe.wait_ge(sem("hid_lo"), MOE_T * h + t + 1)
                    T.matmul(b7[:, :], moe_d[:, 0, t, :], p_hi[:, s, :], start=start, stop=False)
                    T.matmul(b7[:, :], moe_d[:, 0, t, :], p_lo[:, s, :], start=False, stop=False)
                    T.matmul(b7[:, :], moe_d[:, 1, t, :], p_hi[:, s, :], start=False, stop=stop).then_inc(sem("down"), 1)
                if h == 0:
                    post(1, 0)
                    pe.wait_ge(sem("av_done"), 4)
                gu(h, 1, 1, True)
                gu(h, 2, 0)
                if h:
                    pe.wait_ge(sem("yT"), h)
                down(0, 0, start=True)
                if h == 0:
                    for t in range(1, MOE_T - 3):
                        gu(h, t + 2, t % 2)
                        down(t, t % 2)
                        if t in MOE_PE:
                            post(1, MOE_PE[t])
                else:
                    gu(h, 3, 1)
                    down(1, 1)
                    with pe.Fori(2, MOE_T - 4, 2) as t:
                        gu(h, t + 2, 0)
                        down(t, 0)
                        gu(h, t + 3, 1)
                        down(t + 1, 1)
                gu(h, MOE_T - 1, 0)
                down(MOE_T - 3, 0)
                if h == 0:
                    post(1, MOE_PE[MOE_T - 3])
                down(MOE_T - 2, 1)
                down(MOE_T - 1, 0, stop=True)
                if h:
                    pe.wait_ge(sem("y_out"), h)
                else:
                    pe.wait_ge(sem("cw_lo"), 2)
                    gu(1, 0, 0, True)
                pe.wait_ge(sem("yT"), h + 1)
                transp4(b6, opT[:, :].rearrange("p (t d) -> p t d", t=QT), "y_ps")

            first_scores(0)
            first_scores(1)
            shift(0)
            first_scores(2)
            for ph in range(4):
                main(ph)
            moe(0)
            moe(1)


_INS = ['x', 'ctx_1024', 'mask_BxS2_ik0', 'g_xattn', 'g_ffn', 'L0_xattn_Wq', 'L0_xattn_bq', 'L0_xattn_Wk', 'L0_xattn_bk', 'L0_xattn_Wv', 'L0_xattn_bv', 'L0_ffn_wf', 'L0_ffn_uf', 'L0_ffn_bf', 'L0_ffn_wi', 'L0_ffn_ui', 'L0_ffn_bi', 'L0_ffn_wc', 'L0_ffn_uc', 'L0_ffn_bc', 'L0_ffn_wo', 'L0_ffn_uo', 'L0_ffn_bo', 'L0_ffn_in_c', 'L1_xattn_ln_t_g', 'L1_xattn_ln_t_b', 'L1_xattn_ln_a_g', 'L1_xattn_ln_a_b', 'L1_xattn_Wq', 'L1_xattn_bq', 'L1_xattn_Wk', 'L1_xattn_bk', 'L1_xattn_Wv', 'L1_xattn_bv', 'L1_xattn_ln_p_g', 'L1_xattn_ln_p_b', 'L1_ffn_gate_weight', 'L1_ffn_gate_bias', 'L1_ffn_w_gate', 'L1_ffn_w_up', 'L1_ffn_w_down', 'L1_ffn_shared_w_gate', 'L1_ffn_shared_w_up', 'L1_ffn_shared_w_down', 'L1_ffn_anchor_w_gate', 'L1_ffn_anchor_w_up', 'L1_ffn_anchor_w_down']


def _constants():
    import numpy as np
    seg = np.ones((128, QT, NE), np.float32)
    seg[:, :, 0] = 0.0
    i, j = np.divmod(np.arange(16), 4)
    lt4 = np.broadcast_to((j < i).astype(np.float32), (128, 16))
    sel = np.zeros((128, MOE_T, D), np.float16)
    lane = np.arange(D)
    for t in range(MOE_T):
        if t < ROUTED_T:
            r = 2 * t + lane // ME
        elif t < ROUTED_T + ANCHOR_T:
            r = NE + 4 * (t - ROUTED_T) + lane // MA
        else:
            r = np.full(D, NE + NA)
        sel[r, t, lane] = 1.0
        sel[64 + r, t, lane] = 1.0
    return {
        "c_ident": np.eye(D, dtype=np.float32),
        "c_cent": (np.eye(D) - 1.0 / D).astype(np.float32),
        "c_seg": seg.reshape(128, QT * NE),
        "c_lt4": np.ascontiguousarray(lt4),
        "c_sel": sel.reshape(128, MOE_T * D),
    }


def kernel(**inputs):
    import numpy as _np
    import concourse.bacc as _bacc
    from concourse import mybir as _mybir
    from concourse.bass_utils import run_bass_kernel_spmd as _run

    nc = _bacc.Bacc("TRN2", target_bir_lowering=False, num_devices=1)
    arrays, args = {}, {}
    data = {name: inputs[name] for name in _INS}
    data.update(_constants())
    for name, value in data.items():
        v = _np.ascontiguousarray(value)
        arrays[f"in_{name}_dram"] = v
        args[name] = nc.dram_tensor(f"in_{name}_dram", v.shape, _mybir.dt.from_np(v.dtype), kind="ExternalInput").ap()
    args["out"] = nc.dram_tensor("out_0_dram", (1, NQ, D), _mybir.dt.float32, kind="ExternalOutput").ap()
    build(nc, args)
    r = _run(nc, [arrays], core_ids=[0])
    return r.results[0]["out_0_dram"]
```
